# Optimizing a Trainium2 kernel written in Bass

```python
import numpy as np
import jax
import jax.numpy as jnp

def _softmax(x, axis=-1):
    return jax.nn.softmax(x, axis=axis)

def _gelu(x):
    return jax.nn.gelu(x, approximate=True)

def _silu(x):
    return jax.nn.silu(x)

def _sigmoid(x):
    return jax.nn.sigmoid(x)

def _layernorm(x, axis=-1, eps=1e-05):
    m = jnp.mean(x, axis=axis, keepdims=True)
    v = jnp.var(x, axis=axis, keepdims=True)
    return (x - m) / jnp.sqrt(v + eps)

def _scatter_add(tgt, idx, src, axis=0):
    return tgt.at[idx].add(src)

def _segment_sum(src, seg, n):
    return jax.ops.segment_sum(src, seg, n)
kernel_name = 'mk_gnn_resnorm_d4_gnn_r16_982e66'

def setup_inputs(seed: int=0):
    np.random.seed(seed)
    _w = jnp.asarray

    def _rec_inputs():
        import jax
        import jax.numpy as jnp
        _gk = jax.random.key(seed)
        x = -0.000202 + 1 * jax.random.normal(jax.random.fold_in(_gk, 1), (3125, 128), jnp.float32)
        _s = jax.random.randint(jax.random.fold_in(_gk, 2), (50000,), 0, 3125, jnp.int32)
        _d = jax.random.randint(jax.random.fold_in(_gk, 3), (50000,), 0, 3125, jnp.int32)
        _loop = jnp.arange(3125, dtype=jnp.int32)
        src = jnp.concatenate([_s, _d, _loop])
        dst = jnp.concatenate([_d, _s, _loop])
        _o = jnp.argsort(dst, stable=True)
        src = src[_o]
        dst = dst[_o]
        edge_type_3 = jax.random.randint(jax.random.fold_in(_gk, 13), (103125,), 0, 3, jnp.int32)
        return (x, src, dst, edge_type_3)
    x, src, dst, edge_type_3 = _rec_inputs()

    def _L0_gnn_setup():
        import jax, jax.numpy as jnp
        import numpy as np
        N = 3125
        E = 100000
        D = 128
        L = 3
        EPS = 1e-05
        SLOPE = 0.2

        def _gat_forward(x, src, dst, W, a_src, a_dst, b):
            z = x
            for l in range(L):
                h = z @ W[l]
                e = jax.nn.leaky_relu((h @ a_src[l])[src] + (h @ a_dst[l])[dst], SLOPE)
                m = jax.lax.stop_gradient(jax.ops.segment_max(e, dst, num_segments=N))
                p = jnp.exp(e - m[dst])
                s = jax.ops.segment_sum(p, dst, num_segments=N)
                alpha = p / s[dst]
                z = jax.ops.segment_sum(alpha[:, None] * h[src], dst, num_segments=N) + b[l]
                mu = jnp.mean(z, axis=0)
                var = jnp.var(z, axis=0)
                z = jax.nn.relu((z - mu) * jax.lax.rsqrt(var + EPS))
            return z
        key = jax.random.key(seed)
        ks = jax.random.split(key, 5)
        x = jax.random.normal(ks[0], (N, D), jnp.float32)
        edge_index = jax.random.randint(ks[1], (2, E), 0, N)
        W = jax.random.normal(ks[2], (L, D, D), jnp.float32) * 0.1
        a_src = jax.random.normal(ks[3], (L, D), jnp.float32) * 0.1
        a_dst = jax.random.normal(ks[4], (L, D), jnp.float32) * 0.1
        b = jnp.zeros((L, D), jnp.float32)
        return {'x': x, 'edge_index': edge_index, 'W': W, 'a_src': a_src, 'a_dst': a_dst, 'b': b}
    _L0_gnn_all = _L0_gnn_setup()
    _L0_gnn_in = {k: v for k, v in _L0_gnn_all.items() if k in ('W', 'a_src', 'a_dst', 'b')}
    del _L0_gnn_all

    def _L1_gnn_setup():
        import jax, jax.numpy as jnp
        import numpy as np
        N = 3125
        E = 50000
        F_IN = 128
        H = 128
        EPS = 1e-05

        def batchnorm(x, g, b):
            m = jnp.mean(x, axis=0)
            v = jnp.var(x, axis=0)
            return (x - m) * jax.lax.rsqrt(v + EPS) * g + b

        def gcn_conv(x, w, b, src, dst, deg_inv_sqrt):
            h = x @ w
            norm = deg_inv_sqrt[src] * deg_inv_sqrt[dst]
            msg = h[src] * norm[:, None]
            out = jax.ops.segment_sum(msg, dst, num_segments=N)
            return out + b
        key = jax.random.key(seed)
        ks = jax.random.split(key, 6)
        x = jax.random.normal(ks[0], (N, F_IN), dtype=jnp.float32)
        edge_index = jax.random.randint(ks[1], (2, E), 0, N, dtype=jnp.int64)
        s = 0.05
        return {'x': x, 'edge_index': edge_index, 'g_in': jnp.ones((F_IN,), jnp.float32), 'be_in': jnp.zeros((F_IN,), jnp.float32), 'w1': jax.random.normal(ks[2], (F_IN, 2 * H), jnp.float32) * s, 'b1': jnp.zeros((2 * H,), jnp.float32), 'g1': jnp.ones((2 * H,), jnp.float32), 'be1': jnp.zeros((2 * H,), jnp.float32), 'w2': jax.random.normal(ks[3], (2 * H, H), jnp.float32) * s, 'b2': jnp.zeros((H,), jnp.float32), 'g2': jnp.ones((H,), jnp.float32), 'be2': jnp.zeros((H,), jnp.float32)}
    _L1_gnn_all = _L1_gnn_setup()
    _L1_gnn_in = {k: v for k, v in _L1_gnn_all.items() if k in ('g_in', 'be_in', 'w1', 'b1', 'g1', 'be1', 'w2', 'b2', 'g2', 'be2')}
    del _L1_gnn_all

    def _L2_gnn_setup():
        import jax, jax.numpy as jnp
        import numpy as np
        N_NODES = 3125
        N_EDGES = 100000
        IN_DIM = 128
        HEADS = 4
        HEAD_DIM = 32
        N_REL = 3
        NEG_SLOPE = 0.2
        key = jax.random.key(seed)
        ks = jax.random.split(key, 8)
        x = jax.random.normal(ks[0], (N_NODES, IN_DIM), dtype=jnp.float32)
        edge_index = jax.random.randint(ks[1], (2, N_EDGES), 0, N_NODES, dtype=jnp.int64)
        edge_type = jax.random.randint(ks[2], (N_EDGES,), 0, N_REL, dtype=jnp.int64)
        s = 1.0 / np.sqrt(IN_DIM)
        W = jax.random.normal(ks[3], (N_REL, IN_DIM, HEADS * HEAD_DIM), dtype=jnp.float32) * s
        att_src = jax.random.normal(ks[4], (N_REL, HEADS, HEAD_DIM), dtype=jnp.float32) * s
        att_dst = jax.random.normal(ks[5], (N_REL, HEADS, HEAD_DIM), dtype=jnp.float32) * s
        bias = jnp.zeros((N_REL, HEADS * HEAD_DIM), dtype=jnp.float32)
        rel_w = jnp.ones((N_REL,), dtype=jnp.float32)
        return {'x': x, 'W': W, 'att_src': att_src, 'att_dst': att_dst, 'bias': bias, 'rel_w': rel_w, 'edge_index': edge_index, 'edge_type': edge_type}
    _L2_gnn_all = _L2_gnn_setup()
    _L2_gnn_in = {k: v for k, v in _L2_gnn_all.items() if k in ('W', 'att_src', 'att_dst', 'bias', 'rel_w')}
    del _L2_gnn_all

    def _L3_gnn_setup():
        import jax, jax.numpy as jnp
        import numpy as np
        N, E, EMB, HID, H = (3125, 50000, 128, 512, 8)
        D = EMB // H
        EPS = 1e-05

        def _linear_params(key, fan_in, fan_out):
            s = 1.0 / np.sqrt(fan_in)
            k1, k2 = jax.random.split(key)
            w = jax.random.uniform(k1, (fan_in, fan_out), minval=-s, maxval=s, dtype=jnp.float32)
            b = jax.random.uniform(k2, (fan_out,), minval=-s, maxval=s, dtype=jnp.float32)
            return (w, b)

        def _batchnorm(x, g, b):
            mu = x.mean(axis=0)
            var = ((x - mu) ** 2).mean(axis=0)
            return g * (x - mu) * jax.lax.rsqrt(var + EPS) + b

        def _forward(x, wq, bq, wk, bk, wv, bv, wo, bo, w1, b1, w2, b2, g1, be1, g2, be2, A, B):
            n = x.shape[0]
            q = (x @ wq + bq).reshape(n, H, D)
            k = (x @ wk + bk).reshape(n, H, D)
            v = (x @ wv + bv).reshape(n, H, D)
            score = jnp.einsum('ehd,egd->ehg', q[A], k[B])
            ssum = jax.ops.segment_sum(score, A, num_segments=n)
            cnt = jax.ops.segment_sum(jnp.ones((A.shape[0],), score.dtype), A, num_segments=n)
            score = ssum / jnp.maximum(cnt, 1.0)[:, None, None]
            score = jax.nn.softmax(score, axis=-1)
            out = jnp.einsum('ehg,egd->ehd', score, v).reshape(n, EMB)
            out = out @ wo + bo
            x = _batchnorm(out + x, g1, be1)
            h = jax.nn.gelu(x @ w1 + b1, approximate=False)
            h = h @ w2 + b2
            x = _batchnorm(h + x, g2, be2)
            return x
        key = jax.random.key(seed)
        ks = jax.random.split(key, 9)
        x = jax.random.normal(ks[0], (N, EMB), dtype=jnp.float32)
        edge_index = jax.random.randint(ks[1], (2, E), 0, N, dtype=jnp.int32)
        batch = jnp.zeros((N,), dtype=jnp.int32)
        wq, bq = _linear_params(ks[2], EMB, EMB)
        wk, bk = _linear_params(ks[3], EMB, EMB)
        wv, bv = _linear_params(ks[4], EMB, EMB)
        wo, bo = _linear_params(ks[5], EMB, EMB)
        w1, b1 = _linear_params(ks[6], EMB, HID)
        w2, b2 = _linear_params(ks[7], HID, EMB)
        g1 = jnp.ones((EMB,), jnp.float32)
        be1 = jnp.zeros((EMB,), jnp.float32)
        g2 = jnp.ones((EMB,), jnp.float32)
        be2 = jnp.zeros((EMB,), jnp.float32)
        return {'x': x, 'wq': wq, 'bq': bq, 'wk': wk, 'bk': bk, 'wv': wv, 'bv': bv, 'wo': wo, 'bo': bo, 'w1': w1, 'b1': b1, 'w2': w2, 'b2': b2, 'g1': g1, 'be1': be1, 'g2': g2, 'be2': be2, 'edge_index': edge_index, 'batch': batch, 'latent': 0}
    _L3_gnn_all = _L3_gnn_setup()
    _L3_gnn_in = {k: v for k, v in _L3_gnn_all.items() if k in ('wq', 'bq', 'wk', 'bk', 'wv', 'bv', 'wo', 'bo', 'w1', 'b1', 'w2', 'b2', 'g1', 'be1', 'g2', 'be2')}
    del _L3_gnn_all
    return {'x': x, 'src': src, 'dst': dst, 'edge_type_3': edge_type_3, 'L0_gnn_W': _L0_gnn_in['W'], 'L0_gnn_a_src': _L0_gnn_in['a_src'], 'L0_gnn_a_dst': _L0_gnn_in['a_dst'], 'L0_gnn_b': _L0_gnn_in['b'], 'L1_gnn_g_in': _L1_gnn_in['g_in'], 'L1_gnn_be_in': _L1_gnn_in['be_in'], 'L1_gnn_w1': _L1_gnn_in['w1'], 'L1_gnn_b1': _L1_gnn_in['b1'], 'L1_gnn_g1': _L1_gnn_in['g1'], 'L1_gnn_be1': _L1_gnn_in['be1'], 'L1_gnn_w2': _L1_gnn_in['w2'], 'L1_gnn_b2': _L1_gnn_in['b2'], 'L1_gnn_g2': _L1_gnn_in['g2'], 'L1_gnn_be2': _L1_gnn_in['be2'], 'L2_gnn_W': _L2_gnn_in['W'], 'L2_gnn_att_src': _L2_gnn_in['att_src'], 'L2_gnn_att_dst': _L2_gnn_in['att_dst'], 'L2_gnn_bias': _L2_gnn_in['bias'], 'L2_gnn_rel_w': _L2_gnn_in['rel_w'], 'L3_gnn_wq': _L3_gnn_in['wq'], 'L3_gnn_bq': _L3_gnn_in['bq'], 'L3_gnn_wk': _L3_gnn_in['wk'], 'L3_gnn_bk': _L3_gnn_in['bk'], 'L3_gnn_wv': _L3_gnn_in['wv'], 'L3_gnn_bv': _L3_gnn_in['bv'], 'L3_gnn_wo': _L3_gnn_in['wo'], 'L3_gnn_bo': _L3_gnn_in['bo'], 'L3_gnn_w1': _L3_gnn_in['w1'], 'L3_gnn_b1': _L3_gnn_in['b1'], 'L3_gnn_w2': _L3_gnn_in['w2'], 'L3_gnn_b2': _L3_gnn_in['b2'], 'L3_gnn_g1': _L3_gnn_in['g1'], 'L3_gnn_be1': _L3_gnn_in['be1'], 'L3_gnn_g2': _L3_gnn_in['g2'], 'L3_gnn_be2': _L3_gnn_in['be2']}

def reference(x, src, dst, edge_type_3, L0_gnn_W, L0_gnn_a_src, L0_gnn_a_dst, L0_gnn_b, L1_gnn_g_in, L1_gnn_be_in, L1_gnn_w1, L1_gnn_b1, L1_gnn_g1, L1_gnn_be1, L1_gnn_w2, L1_gnn_b2, L1_gnn_g2, L1_gnn_be2, L2_gnn_W, L2_gnn_att_src, L2_gnn_att_dst, L2_gnn_bias, L2_gnn_rel_w, L3_gnn_wq, L3_gnn_bq, L3_gnn_wk, L3_gnn_bk, L3_gnn_wv, L3_gnn_bv, L3_gnn_wo, L3_gnn_bo, L3_gnn_w1, L3_gnn_b1, L3_gnn_w2, L3_gnn_b2, L3_gnn_g1, L3_gnn_be1, L3_gnn_g2, L3_gnn_be2):
    import jax
    import jax.numpy as jnp

    def _L0_gnn_ref(x, edge_index, W, a_src, a_dst, b):
        import jax, jax.numpy as jnp
        import numpy as np
        N = 3125
        E = 100000
        D = 128
        L = 3
        EPS = 1e-05
        SLOPE = 0.2

        def _gat_forward(x, src, dst, W, a_src, a_dst, b):
            z = x
            for l in range(L):
                h = z @ W[l]
                e = jax.nn.leaky_relu((h @ a_src[l])[src] + (h @ a_dst[l])[dst], SLOPE)
                m = jax.lax.stop_gradient(jax.ops.segment_max(e, dst, num_segments=N))
                p = jnp.exp(e - m[dst])
                s = jax.ops.segment_sum(p, dst, num_segments=N)
                alpha = p / s[dst]
                z = jax.ops.segment_sum(alpha[:, None] * h[src], dst, num_segments=N) + b[l]
                mu = jnp.mean(z, axis=0)
                var = jnp.var(z, axis=0)
                z = jax.nn.relu((z - mu) * jax.lax.rsqrt(var + EPS))
            return z
        loops = jnp.arange(N, dtype=edge_index.dtype)
        src = jnp.concatenate([edge_index[0], loops])
        dst = jnp.concatenate([edge_index[1], loops])
        return _gat_forward(x, src, dst, W, a_src, a_dst, b)

    def _L1_gnn_ref(x, edge_index, g_in, be_in, w1, b1, g1, be1, w2, b2, g2, be2):
        import jax, jax.numpy as jnp
        import numpy as np
        N = 3125
        E = 50000
        F_IN = 128
        H = 128
        EPS = 1e-05

        def batchnorm(x, g, b):
            m = jnp.mean(x, axis=0)
            v = jnp.var(x, axis=0)
            return (x - m) * jax.lax.rsqrt(v + EPS) * g + b

        def gcn_conv(x, w, b, src, dst, deg_inv_sqrt):
            h = x @ w
            norm = deg_inv_sqrt[src] * deg_inv_sqrt[dst]
            msg = h[src] * norm[:, None]
            out = jax.ops.segment_sum(msg, dst, num_segments=N)
            return out + b
        loop = jnp.arange(N, dtype=edge_index.dtype)
        src = jnp.concatenate([edge_index[0], loop])
        dst = jnp.concatenate([edge_index[1], loop])
        deg = jax.ops.segment_sum(jnp.ones_like(src, dtype=x.dtype), dst, num_segments=N)
        deg_inv_sqrt = jnp.where(deg > 0, jax.lax.rsqrt(jnp.maximum(deg, 1.0)), 0.0)
        h = batchnorm(x, g_in, be_in)
        h = jax.nn.relu(batchnorm(gcn_conv(h, w1, b1, src, dst, deg_inv_sqrt), g1, be1))
        h = jax.nn.relu(batchnorm(gcn_conv(h, w2, b2, src, dst, deg_inv_sqrt), g2, be2))
        return h

    def _L2_gnn_ref(x, W, att_src, att_dst, bias, rel_w, edge_index, edge_type):
        import jax, jax.numpy as jnp
        import numpy as np
        N_NODES = 3125
        N_EDGES = 100000
        IN_DIM = 128
        HEADS = 4
        HEAD_DIM = 32
        N_REL = 3
        NEG_SLOPE = 0.2
        N = x.shape[0]
        NEG = jnp.float32(-1000000000.0)
        self_idx = jnp.arange(N, dtype=edge_index.dtype)
        src = jnp.concatenate([edge_index[0], self_idx])
        dst = jnp.concatenate([edge_index[1], self_idx])
        weights = jax.nn.softmax(rel_w)
        out = jnp.zeros((N, HEADS * HEAD_DIM), dtype=x.dtype)
        for r in range(N_REL):
            h = (x @ W[r]).reshape(N, HEADS, HEAD_DIM)
            a_s = jnp.einsum('nhc,hc->nh', h, att_src[r])
            a_d = jnp.einsum('nhc,hc->nh', h, att_dst[r])
            score = jax.nn.leaky_relu(a_s[src] + a_d[dst], NEG_SLOPE)
            mask = jnp.concatenate([edge_type == r, jnp.ones((N,), dtype=bool)])
            score = jnp.where(mask[:, None], score, NEG)
            smax = jax.ops.segment_max(score, dst, num_segments=N)
            ex = jnp.exp(score - smax[dst])
            denom = jax.ops.segment_sum(ex, dst, num_segments=N)
            alpha = ex / denom[dst]
            msg = alpha[:, :, None] * h[src]
            rel_out = jax.ops.segment_sum(msg, dst, num_segments=N).reshape(N, HEADS * HEAD_DIM)
            out = out + weights[r] * (rel_out + bias[r])
        return out

    def _L3_gnn_ref(x, wq, bq, wk, bk, wv, bv, wo, bo, w1, b1, w2, b2, g1, be1, g2, be2, edge_index, batch, latent):
        import jax, jax.numpy as jnp
        import numpy as np
        N, E, EMB, HID, H = (3125, 50000, 128, 512, 8)
        D = EMB // H
        EPS = 1e-05

        def _linear_params(key, fan_in, fan_out):
            s = 1.0 / np.sqrt(fan_in)
            k1, k2 = jax.random.split(key)
            w = jax.random.uniform(k1, (fan_in, fan_out), minval=-s, maxval=s, dtype=jnp.float32)
            b = jax.random.uniform(k2, (fan_out,), minval=-s, maxval=s, dtype=jnp.float32)
            return (w, b)

        def _batchnorm(x, g, b):
            mu = x.mean(axis=0)
            var = ((x - mu) ** 2).mean(axis=0)
            return g * (x - mu) * jax.lax.rsqrt(var + EPS) + b

        def _forward(x, wq, bq, wk, bk, wv, bv, wo, bo, w1, b1, w2, b2, g1, be1, g2, be2, A, B):
            n = x.shape[0]
            q = (x @ wq + bq).reshape(n, H, D)
            k = (x @ wk + bk).reshape(n, H, D)
            v = (x @ wv + bv).reshape(n, H, D)
            score = jnp.einsum('ehd,egd->ehg', q[A], k[B])
            ssum = jax.ops.segment_sum(score, A, num_segments=n)
            cnt = jax.ops.segment_sum(jnp.ones((A.shape[0],), score.dtype), A, num_segments=n)
            score = ssum / jnp.maximum(cnt, 1.0)[:, None, None]
            score = jax.nn.softmax(score, axis=-1)
            out = jnp.einsum('ehg,egd->ehd', score, v).reshape(n, EMB)
            out = out @ wo + bo
            x = _batchnorm(out + x, g1, be1)
            h = jax.nn.gelu(x @ w1 + b1, approximate=False)
            h = h @ w2 + b2
            x = _batchnorm(h + x, g2, be2)
            return x
        A, B = (edge_index[0], edge_index[1])
        return _forward(x, wq, bq, wk, bk, wv, bv, wo, bo, w1, b1, w2, b2, g1, be1, g2, be2, A, B)
    edge_index = jnp.stack([src, dst])
    batch0 = jnp.zeros((3125,), jnp.int32)
    x = _layernorm(x + _L0_gnn_ref(x, edge_index, L0_gnn_W, L0_gnn_a_src, L0_gnn_a_dst, L0_gnn_b), axis=-1)
    x = _layernorm(x + _L1_gnn_ref(x, edge_index, L1_gnn_g_in, L1_gnn_be_in, L1_gnn_w1, L1_gnn_b1, L1_gnn_g1, L1_gnn_be1, L1_gnn_w2, L1_gnn_b2, L1_gnn_g2, L1_gnn_be2), axis=-1)
    x = _layernorm(x + _L2_gnn_ref(x, L2_gnn_W, L2_gnn_att_src, L2_gnn_att_dst, L2_gnn_bias, L2_gnn_rel_w, edge_index, edge_type_3), axis=-1)
    x = _layernorm(x + _L3_gnn_ref(x, L3_gnn_wq, L3_gnn_bq, L3_gnn_wk, L3_gnn_bk, L3_gnn_wv, L3_gnn_bv, L3_gnn_wo, L3_gnn_bo, L3_gnn_w1, L3_gnn_b1, L3_gnn_w2, L3_gnn_b2, L3_gnn_g1, L3_gnn_be1, L3_gnn_g2, L3_gnn_be2, edge_index, batch0, 0), axis=-1)
    return x

_drawn_inputs = setup_inputs


def setup_inputs(seed=0):
    import zlib

    import numpy as np

    out = dict(_drawn_inputs(seed))
    spreads = {'L0_gnn_b': (0.0, 0.8),
     'L1_gnn_g_in': (1.0, 0.2),
     'L1_gnn_be_in': (0.0, 0.349),
     'L1_gnn_b1': (0.0, 0.8),
     'L1_gnn_g1': (1.0, 0.2),
     'L1_gnn_be1': (0.0, 0.1),
     'L1_gnn_b2': (0.0, 0.8),
     'L1_gnn_g2': (1.0, 0.2),
     'L1_gnn_be2': (0.0, 0.1),
     'L2_gnn_bias': (0.0, 0.272),
     'L2_gnn_rel_w': (1.0, 0.545),
     'L3_gnn_g1': (1.0, 0.2),
     'L3_gnn_be1': (0.0, 0.8),
     'L3_gnn_g2': (1.0, 0.2),
     'L3_gnn_be2': (0.0, 0.1)}
    factors = {'L3_gnn_wq': 2.836,
     'L3_gnn_bq': 8.0,
     'L3_gnn_wk': 2.946,
     'L3_gnn_bk': 7.862,
     'L3_gnn_bv': 8.0,
     'L3_gnn_bo': 8.0,
     'L3_gnn_b1': 8.0,
     'L3_gnn_b2': 8.0}
    for name, (base, spread) in spreads.items():
        noise = np.random.default_rng([zlib.crc32(name.encode()), seed]).standard_normal(out[name].shape)
        drawn = base * np.exp(spread * noise) if base else spread * noise
        out[name] = jnp.asarray(drawn.astype(out[name].dtype))
    for name, factor in factors.items():
        out[name] = (out[name] * factor).astype(out[name].dtype)
    return out
```

```python
from contextlib import ExitStack

import concourse.bass as bass
from concourse import mybir

F32 = mybir.dt.float32
F16 = mybir.dt.float16
BF16 = mybir.dt.bfloat16
I32 = mybir.dt.int32
ALU = mybir.AluOpType
ACT = mybir.ActivationFunctionType
AX = mybir.AxisListType

N = 3125
P = 125
NB = N // P
D = 128
PAD = 128
E = 103125
CH = P
NCH = E // CH
R = 3
DG = 5
NG = N // DG
GW = R * NB * DG
GE = GW + 1
WIN = 3
EPS = 1e-5
ROUND = 12582912.0


class Chain:

    def __init__(self, eng, sem, base=0):
        self.eng, self.sem, self.n, self.base = eng, sem, 0, base

    def __call__(self, ins):
        self.n += 1
        ins.then_inc(self.sem, 1)
        self.eng.wait_ge(self.sem, self.base + self.n)


def phase(body):
    def run(nc, K, *rest, **more):
        body(nc, K, nc.alloc_semaphore, *rest, **more)
    return run


def ready_first(eng, *values):
    for value in values:
        eng.compute_val(value)


@phase
def prepare_edges(nc, K, S):
    with ExitStack() as ctx:
        sb = lambda name, shape, dt: ctx.enter_context(nc.sbuf_tensor(name, shape, dt))
        es = sb("es", [P, NCH], I32)
        ed = sb("ed", [P, NCH], I32)
        et = sb("et", [P, NCH], I32)
        fs = sb("fs", [P, NCH], F32)
        fd = sb("fd", [P, NCH], F32)
        ft = sb("ft", [P, NCH], F32)
        q = sb("q", [P, NCH], F32)
        q5 = sb("q5", [P, NCH], F32)
        dn = sb("dn", [75, 11, CH], I32)
        mm = sb("mm", [75, 2, 11], F32)
        lohi = sb("lohi", [P, 2, NCH], F32)
        ci = sb("ci", [P, NCH], I32)
        cf = sb("cf", [P, NCH], F32)
        gi = sb("gi", [P, DG], I32)
        gf = sb("gf", [P, DG], F32)
        t1 = sb("t1", [P, NCH], F32)
        t2 = sb("t2", [P, NCH], F32)
        wlo = sb("wlo", [P, DG], F32)
        whi = sb("whi", [P, DG], F32)
        need = sb("need", [P, DG], F32)
        wi = sb("wi", [P, DG], I32)
        big = sb("big", [P, 1], F32)
        alln = sb("alln", [P, 1], F32)
        flag = sb("flag", [1, 1], I32)
        ti = sb("ti", [P, NG], I32)
        ki = sb("ki", [P, GE], I32)
        loaded, iotas, own, mmout, mmin, wout, win_in, shared = (S("prep_" + n) for n in
            ("loaded", "iotas", "own", "mmout", "mmin", "wout", "win", "shared"))
        need_ready = S("prep_need")
        with nc.Block() as block:
            @block.sync
            def _(sp):
                sp.dma_start(es[:], K.src_t[:]).then_inc(loaded, 16)
                sp.dma_start(ed[:], K.dst_t[:]).then_inc(loaded, 16)
                sp.dma_start(et[:], K.typ_t[:]).then_inc(loaded, 16)
                sp.dma_start(dn[:], K.dst_n[:]).then_inc(loaded, 16)
                sp.wait_ge(mmout, 1)
                sp.dma_start(K.chunk_range[:].rearrange("a (p c) -> p a c", c=11), mm[:]).then_inc(mmin, 16)
                sp.wait_ge(mmin, 16)
                sp.dma_start(lohi[:].rearrange("p a c -> p (a c)"),
                             K.chunk_range[:].rearrange("a c -> (a c)").partition_broadcast(P)).then_inc(mmin, 16)
                sp.wait_ge(wout, 1)
                sp.dma_start(K.first_chunk[:].rearrange("(g p) -> p g", p=P), wi[:],
                             allow_slow_non_contiguous=True).then_inc(win_in, 16)
                sp.wait_ge(win_in, 16)
                sp.dma_start(K.window[0:1, 0:NG], K.first_chunk[:].unsqueeze(0)).then_inc(win_in, 16)
                sp.dma_start(K.wide[0:1, :], flag[:]).then_inc(win_in, 16)
                sp.wait_ge(win_in, 48)

            @block.gpsimd
            def _(pool):
                pool.iota(ci[:], [[1, NCH]], channel_multiplier=0).then_inc(iotas, 1)
                pool.iota(gi[:], [[P, DG]], channel_multiplier=1).then_inc(iotas, 1)
                pool.iota(ti[:], [[GW, NG]], channel_multiplier=0).then_inc(iotas, 1)
                pool.iota(ki[:], [[1, GE]], channel_multiplier=0).then_inc(iotas, 1)
                pool.wait_ge(need_ready, 1)
                pool.partition_all_reduce(alln[:], big[:], P, bass.bass_isa.ReduceOp.max).then_inc(shared, 1)

            @block.vector
            def _(v):
                link = Chain(v, own)
                v.wait_ge(loaded, 64)
                link(v.tensor_copy(fs[:], es[:]))
                link(v.tensor_copy(fd[:], ed[:]))
                link(v.tensor_copy(ft[:], et[:]))
                link(v.tensor_scalar(q[:], fs[:], -62.0, 1.0 / P, ALU.add, ALU.mult))
                link(v.tensor_scalar(q[:], q[:], ROUND, None, ALU.add))
                link(v.tensor_scalar(q[:], q[:], -ROUND, None, ALU.add))
                link(v.scalar_tensor_tensor(K.key_lo[:], q[:], -float(P), fs[:], ALU.mult, ALU.add))
                link(v.tensor_scalar(q5[:], fd[:], -2.0, 1.0 / DG, ALU.add, ALU.mult))
                link(v.tensor_scalar(q5[:], q5[:], ROUND, None, ALU.add))
                link(v.tensor_scalar(q5[:], q5[:], -ROUND, None, ALU.add))
                link(v.scalar_tensor_tensor(fd[:], q5[:], -float(DG), fd[:], ALU.mult, ALU.add))
                link(v.scalar_tensor_tensor(fd[:], q5[:], float(GW), fd[:], ALU.mult, ALU.add))
                link(v.scalar_tensor_tensor(fd[:], ft[:], float(NB * DG), fd[:], ALU.mult, ALU.add))
                link(v.scalar_tensor_tensor(K.key_col[:], q[:], float(DG), fd[:], ALU.mult, ALU.add))
                link(v.tensor_reduce(mm[:, 0], dn[:], AX.X, ALU.min))
                link(v.tensor_reduce(mm[:, 1], dn[:], AX.X, ALU.max))
                link(v.tensor_scalar(mm[:], mm[:], -2.0, 1.0 / DG, ALU.add, ALU.mult))
                link(v.tensor_scalar(mm[:], mm[:], ROUND, None, ALU.add))
                v.tensor_scalar(mm[:], mm[:], -ROUND, None, ALU.add).then_inc(mmout, 1)
                v.wait_ge(iotas, 4)
                link(v.tensor_copy(cf[:], ci[:]))
                link(v.tensor_copy(gf[:], gi[:]))
                link(v.tensor_copy(K.group_base[:], ti[:]))
                link(v.tensor_copy(K.iota_col[:], ki[:]))
                v.wait_ge(mmin, 32)
                for j in range(DG):
                    g = gf[:, j:j + 1]
                    link(v.tensor_scalar(t1[:], lohi[:, 0], g, None, ALU.is_le))
                    link(v.scalar_tensor_tensor(t1[:], lohi[:, 1], g, t1[:], ALU.is_ge, ALU.mult))
                    link(v.scalar_tensor_tensor(t2[:], t1[:], -1024.0, cf[:], ALU.mult, ALU.add))
                    link(v.tensor_reduce(wlo[:, j:j + 1], t2[:], AX.X, ALU.min))
                    link(v.scalar_tensor_tensor(t2[:], t1[:], 1024.0, cf[:], ALU.mult, ALU.add))
                    link(v.tensor_reduce(whi[:, j:j + 1], t2[:], AX.X, ALU.max))
                link(v.tensor_scalar(wlo[:], wlo[:], 1024.0, None, ALU.add))
                link(v.tensor_scalar(whi[:], whi[:], -1023.0, None, ALU.add))
                link(v.tensor_tensor(need[:], whi[:], wlo[:], ALU.subtract))
                link(v.tensor_reduce(big[:], need[:], AX.X, ALU.max))
                v.tensor_scalar(wlo[:], wlo[:], float(NCH - WIN), 0.0, ALU.min, ALU.max).then_inc(need_ready, 1)
                v.wait_ge(need_ready, 1)
                link(v.tensor_copy(wi[:], wlo[:]))
                v.wait_ge(shared, 1)
                v.tensor_scalar(flag[:], alln[0:1, :], float(WIN), None, ALU.is_gt).then_inc(wout, 1)


@phase
def count_edges(nc, K, S):
    OHS = 5
    SLOTS = 25
    STEPS = NCH // SLOTS
    with ExitStack() as ctx:
        sb = lambda name, shape, dt: ctx.enter_context(nc.sbuf_tensor(name, shape, dt))
        lo1 = sb("lo1", [P, SLOTS, PAD], BF16)
        col1 = sb("col1", [P, SLOTS, GE], BF16)
        stage = sb("stage", [P, 2, R, NB, PAD], F16)
        total = sb("total", [P, 2, NB, PAD], F16)
        iota_lo = K.iota_col[:, 0:PAD]
        (hot, counted, taken, summed, stored, cleared, diag, wide_hot, wide_used) = (
            S("count_" + n) for n in ("hot", "counted", "taken", "summed", "stored", "cleared", "diag",
                                      "wide_hot", "wide_used"))
        with nc.Block() as block:
            @block.gpsimd
            def _(pool):
                pool.memset(stage[:], 0.0).then_inc(cleared, 1)
                with pool.Fori(0, NB) as i:
                    pool.wait_ge(taken, (i + 1) * (P // DG) + OHS)
                    pool.wait_ge(stored, 64 * i + 64)
                    st = stage[:, bass.ds(i % 2, 1)].rearrange("p a r h d -> p (a r) h d")
                    tot = total[:, bass.ds(i % 2, 1)].rearrange("p a h d -> p (a h) d")
                    link = Chain(pool, summed, 3 * i)
                    link(pool.tensor_tensor(tot, st[:, 0], st[:, 1], ALU.add))
                    link(pool.tensor_tensor(tot, tot, st[:, 2], ALU.add))
                    for r in range(R):
                        own_r = stage[:, bass.ds(i % 2, 1), r, bass.ds(i, 1), 0:P].rearrange("p a h d -> p (a h) d")
                        pool.tensor_tensor(own_r, own_r, K.ident16[0:P, 0:P].unsqueeze(1), ALU.add).then_inc(diag, 1)
                    pool.wait_ge(diag, 3 * i + 3)
                    own_t = total[:, bass.ds(i % 2, 1), bass.ds(i, 1), 0:P].rearrange("p a h d -> p (a h) d")
                    link(pool.tensor_tensor(own_t, own_t, K.ident16[0:P, 0:P].unsqueeze(1), ALU.add))
                    assert link.n == 3

            @block.vector
            def _(v):
                def one_hots(slot, chunk, base):
                    v.tensor_scalar(lo1[:, slot], iota_lo, K.key_lo[:, bass.ds(chunk, 1)], None, ALU.is_equal)
                    return v.tensor_scalar(col1[:, slot], K.iota_col[:], base, K.key_col[:, bass.ds(chunk, 1)],
                                           ALU.add, ALU.is_equal)

                wide = v.value_load(K.wide[0:1, 0:1], min_val=0, max_val=1)
                with v.If(wide < 1):
                    with v.Fori(0, NB) as i:
                        for b in range(P // DG):
                            v.wait_ge(counted, i * (P // DG) + b + 1)
                            first = v.value_load(K.window[0:1, bass.ds(i * (P // DG) + b, 1)], min_val=0,
                                                 max_val=NCH - WIN)
                            base = K.group_base[:, bass.ds(i * (P // DG) + b, 1)]
                            for w in range(WIN):
                                ins = one_hots(b % OHS * WIN + w, first + w, base)
                            ins.then_inc(hot, 1)
                with v.Else():
                    with v.Fori(0, NG // OHS) as i:
                        for s in range(OHS):
                            with v.Fori(0, STEPS) as c:
                                v.wait_ge(wide_used, i * (OHS * STEPS) + s * STEPS + c + 1)
                                base = K.group_base[:, bass.ds(i * OHS + s, 1)]
                                for w in range(SLOTS):
                                    ins = one_hots(w, c * SLOTS + w, base)
                                ins.then_inc(wide_hot, 1)

            @block.tensor
            def _(pe):
                pe.sem_inc(counted, OHS)
                wide = pe.value_load(K.wide[0:1, 0:1], min_val=0, max_val=1)
                with pe.If(wide < 1):
                    with pe.Fori(0, NB) as i:
                        for b in range(P // DG):
                            s = b % OHS
                            pe.wait_ge(hot, i * (P // DG) + b + 1)
                            pe.wait_ge(taken, i * (P // DG) + b + 1)
                            for w in range(WIN):
                                ins = pe.matmul(K.ps[0:P, s, 0:GW], lo1[:, s * WIN + w, 0:P], col1[:, s * WIN + w, 0:GW],
                                                start=(w == 0), stop=(w == WIN - 1))
                            ins.then_inc(counted, 1)
                with pe.Else():
                    pe.sem_inc(wide_used, 1)
                    with pe.Fori(0, NG // OHS) as i:
                        for s in range(OHS):
                            pe.wait_ge(taken, i * OHS + s + 1)
                            pe.matmul(K.ps[:, s, :], K.zeros[:, 0:128], K.zeros[:], start=True, stop=True)
                            with pe.Fori(0, STEPS) as c:
                                pe.wait_ge(wide_hot, i * (OHS * STEPS) + s * STEPS + c + 1)
                                for w in range(SLOTS):
                                    ins = pe.matmul(K.ps[0:P, s, 0:GW], lo1[:, w, 0:P], col1[:, w, 0:GW], start=False, stop=False,
                                                    skip_group_check=True)
                                ins.then_inc(wide_used, 1)
                            pe.matmul(K.ps[:, s, 0:128], K.zeros[:, 0:128], K.zeros[:, 0:128], start=False, stop=False,
                                      skip_group_check=True).then_inc(counted, 1)

            @block.scalar
            def _(act):
                act.sem_inc(taken, OHS)
                act.wait_ge(cleared, 1)
                with act.Fori(0, NB) as i:
                    act.wait_ge(stored, 64 * i + 64)
                    for b in range(P // DG):
                        act.wait_ge(counted, i * (P // DG) + b + 1 + OHS)
                        dst = stage[:, bass.ds(i % 2, 1), :, :, DG * b:DG * (b + 1)]
                        act.activation(dst.rearrange("p a r h d -> p (a r h) d"),
                                       K.ps[0:P, b % OHS, 0:GW].rearrange("p (x d) -> p x d", d=DG),
                                       ACT.Copy).then_inc(taken, 1)

            @block.sync
            def _(sp):
                sp.sem_inc(stored, 128)
                with sp.Fori(0, NB) as i:
                    sp.wait_ge(summed, 3 * i + 3)
                    sp.wait_ge(stored, 64 * i + 128)
                    for r in range(R):
                        sp.dma_start(K.counts[r, :, bass.ds(i, 1)].rearrange("p a h d -> p (a h d)"),
                                     stage[:, bass.ds(i % 2, 1), r].rearrange("p a h d -> p (a h d)")).then_inc(stored, 16)
                    sp.dma_start(K.counts_all[:, bass.ds(i, 1)].rearrange("p a h d -> p (a h d)"),
                                 total[:, bass.ds(i % 2, 1)].rearrange("p a h d -> p (a h d)")).then_inc(stored, 16)
                sp.wait_ge(stored, 64 * NB + 128)


@phase
def load_constants(nc, K, S):
    loaded, cleared, made = S("const_loaded"), S("const_cleared"), S("const_made")
    with nc.Block() as block:
        @block.sync
        def _(sp):
            sp.dma_start(K.x[:], K.x_in.rearrange("(b p) f -> p b f", p=P)).then_inc(loaded, 16)
            sp.dma_start(K.cols[:], K.cols_in).then_inc(loaded, 16)
            sp.dma_start(K.wext[:, :, 0:D], K.w_in.rearrange("k f j -> f k j")).then_inc(loaded, 16)
            sp.wait_ge(loaded, 48)

        @block.gpsimd
        def _(pool):
            pool.memset(K.ident[:], 0.0).then_inc(cleared, 1)
            pool.memset(K.ident16[:], 0.0).then_inc(cleared, 1)
            pool.memset(K.zeros[:], 0.0).then_inc(made, 1)
            pool.wait_ge(cleared, 2)
            for m in (K.ident, K.ident16):
                pool.affine_select(out=m[:], in_=m[:], compare_op=ALU.not_equal, fill=1.0, base=0,
                                   pattern=[[-1, 128]], channel_multiplier=1).then_inc(made, 1)


@phase
def score_weights(nc, K, S):
    with ExitStack() as ctx:
        sb = lambda name, shape, dt: ctx.enter_context(nc.sbuf_tensor(name, shape, dt))
        wt = sb("wt", [D, 6, D], F32)
        a = sb("a", [D, 6, 8], F32)
        cleared, filled, turned, moved, scored = (S("sw_" + n) for n in
                                                  ("cleared", "filled", "turned", "moved", "scored"))
        with nc.Block() as block:
            @block.vector
            def _(v):
                v.memset(a[:], 0.0).then_inc(cleared, 1)
                v.wait_ge(cleared, 1)
                for l in range(3):
                    v.tensor_copy(a[:, l, 0:2], K.cols[:, COL["a"] + 2 * l:COL["a"] + 2 * l + 2]).then_inc(filled, 1)
                for r in range(R):
                    for h in range(4):
                        rows = slice(32 * h, 32 * h + 32)
                        for side in range(2):
                            c = COL["att"] + 2 * r + side
                            v.tensor_copy(a[rows, 3 + r, 4 * side + h:4 * side + h + 1],
                                          K.cols[rows, c:c + 1]).then_inc(filled, 1)
                for k in range(6):
                    v.wait_ge(turned, k + 1)
                    v.tensor_copy(wt[:, k], K.ps[:, k, 0:D]).then_inc(moved, 1)
                v.wait_ge(scored, 6)
                for k in range(6):
                    v.tensor_copy(K.wext[:, k, D:D + 8], K.ps[:, k, D:D + 8])

            @block.tensor
            def _(pe):
                for k in range(6):
                    pe.transpose(K.ps[:, k, 0:D], K.wext[:, k, 0:D], K.ident[:]).then_inc(turned, 1)
                pe.wait_ge(filled, 27)
                for k in range(6):
                    pe.wait_ge(moved, k + 1)
                    pe.matmul(K.ps[:, k, D:D + 8], wt[:, k], a[:, k], start=True, stop=True).then_inc(scored, 1)


@phase
def turn_to_columns(nc, K, S, tag, src, dst, bias=None, add=None):
    turned = S(tag + "_turned")
    with nc.Block() as block:
        @block.tensor
        def _(pe):
            for k in range(NB):
                pe.transpose(K.ps[:, k // 4, (k % 4) * P:(k % 4 + 1) * P], src[0:P, k, 0:D],
                             K.ident[0:P, 0:P]).then_inc(turned, 1)

        def move(eng, bank):
            eng.wait_ge(turned, min(4 * bank + 4, NB))
            w = min(4 * P, N - 4 * P * bank)
            out, got = dst[:, 4 * P * bank:4 * P * bank + w], K.ps[:, bank, 0:w]
            return out, got

        @block.vector
        def _(v):
            for bank in range(0, 7, 2):
                out, got = move(v, bank)
                v.tensor_scalar(out, got, 1.0 if bias is None else bias, None, ALU.mult if bias is None else ALU.add)

        @block.scalar
        def _(act):
            for bank in range(1, 7, 2):
                out, got = move(act, bank)
                act.activation(out, got, ACT.Identity, bias=0.0 if bias is None else bias)


@phase
def turn_to_rows(nc, K, S, tag, src, dst, residual=None):
    turned = S(tag + "_turned")
    with nc.Block() as block:
        @block.tensor
        def _(pe):
            for k in range(NB):
                pe.transpose(K.ps[0:P, k // 4, (k % 4) * D:(k % 4 + 1) * D], src[:, k * P:(k + 1) * P],
                             K.ident[:]).then_inc(turned, 1)

        @block.vector
        def _(v):
            for bank in range(7):
                v.wait_ge(turned, min(4 * bank + 4, NB))
                n = min(4, NB - 4 * bank)
                out = dst[0:P, 4 * bank:4 * bank + n, 0:D]
                got = K.ps[0:P, bank, 0:n * D].rearrange("p (b f) -> p b f", f=D)
                if residual is None:
                    v.tensor_copy(out, got)
                else:
                    v.tensor_tensor(out, got, residual[0:P, 4 * bank:4 * bank + n, 0:D], ALU.add)


@phase
def batch_norm(nc, K, S, tag, z, out, g=None, b=None, relu=False):
    with ExitStack() as ctx:
        sb = lambda name, shape, dt: ctx.enter_context(nc.sbuf_tensor(tag + name, shape, dt))
        st = sb("st", [D, 7, 6], F32)
        mv = sb("mv", [D, 2], F32)
        sc = sb("sc", [D, 2], F32)
        own, rstd = S(tag + "_own"), S(tag + "_rstd")
        with nc.Block() as block:
            @block.vector
            def _(v):
                link = Chain(v, own)
                for m in range(7):
                    ins = v.bn_stats(st[:, m], z[:, 500 * m:min(500 * m + 500, N)])
                link(ins)
                link(v.bn_aggr(mv[:], st[:].rearrange("p a b -> p (a b)")))
                link(v.tensor_scalar(mv[:, 1:2], mv[:, 1:2], EPS, None, ALU.add))
                v.wait_ge(rstd, 1)
                link(v.reciprocal(sc[:, 0:1], mv[:, 1:2]))
                if g is not None:
                    link(v.tensor_tensor(sc[:, 0:1], sc[:, 0:1], g, ALU.mult))
                link(v.scalar_tensor_tensor(sc[:, 1:2], mv[:, 0:1], -1.0, sc[:, 0:1], ALU.mult, ALU.mult))
                if b is not None:
                    link(v.tensor_tensor(sc[:, 1:2], sc[:, 1:2], b, ALU.add))
                half = 1700
                link(v.tensor_scalar(out[:, 0:half], z[:, 0:half], sc[:, 0:1], sc[:, 1:2], ALU.mult, ALU.add))
                if relu:
                    v.tensor_scalar(out[:, 0:half], out[:, 0:half], 0.0, None, ALU.max)

            @block.scalar
            def _(act):
                act.wait_ge(own, 3)
                act.activation(mv[:, 1:2], mv[:, 1:2], ACT.Sqrt).then_inc(rstd, 1)
                act.wait_ge(own, 5 + (g is not None) + (b is not None))
                act.activation(out[:, 1700:N], z[:, 1700:N], ACT.Relu if relu else ACT.Identity,
                               bias=sc[:, 1:2], scale=sc[:, 0:1])


@phase
def layer_norm(nc, K, S, tag, x):
    with ExitStack() as ctx:
        sb = lambda name, shape, dt: ctx.enter_context(nc.sbuf_tensor(tag + name, shape, dt))
        st = sb("st", [P, NB, 6], F32)
        mv = sb("mv", [P, NB, 2], F32)
        own, rstd = S(tag + "_own"), S(tag + "_rstd")
        with nc.Block() as block:
            @block.vector
            def _(v):
                link = Chain(v, own)
                for k in range(NB):
                    ins = v.bn_stats(st[:, k], x[:, k])
                link(ins)
                for k in range(NB):
                    ins = v.bn_aggr(mv[:, k], st[:, k])
                link(ins)
                link(v.tensor_scalar(mv[:, :, 1], mv[:, :, 1], EPS, None, ALU.add))
                v.wait_ge(rstd, 1)
                link(v.reciprocal(mv[:, :, 1], mv[:, :, 1]))
                for k in range(NB):
                    v.tensor_scalar(x[:, k], x[:, k], mv[:, k, 0:1], mv[:, k, 1:2], ALU.subtract, ALU.mult)

            @block.scalar
            def _(act):
                act.wait_ge(own, 3)
                act.activation(mv[:, :, 1], mv[:, :, 1], ACT.Sqrt).then_inc(rstd, 1)


@phase
def scores(nc, K, S, tag, k, H, F, T):
    FH = D // H
    with ExitStack() as ctx:
        sb = lambda name, shape, dt: ctx.enter_context(nc.sbuf_tensor(tag + name, shape, dt))
        hx = sb("hx", [P, NB, D + 8], F32)
        val = sb("val", [P, NB, H, 2, F], F32)
        adr = sb("adr", [H, NB, PAD], F32)
        gmax = sb("gmax", [P, 2, H], F32)
        asg = sb("asg", [P, NB, H], F32)
        u = sb("u", [P, 2, NB, H], F32)
        t = sb("t", [P, NB, H], F32)
        tm = sb("tm", [P, 2, NB, H], F32)
        (proj, projv, adp, adt, adz, adst, own, mx, mxr, asr, ur, tr, part, rest, vals_ready) = (
            S(tag + "_" + n) for n in ("proj", "projv", "adp", "adt", "adz", "adst", "own", "mx", "mxr", "asr",
                                       "ur", "tr", "part", "rest", "vals"))
        W = D + 2 * H
        with nc.Block() as block:
            @block.tensor
            def _(pe):
                for m in range(7):
                    w = min(500, N - 500 * m)
                    pe.matmul(K.ps[0:H, m, 0:w], K.wext[:, k, D + H:D + 2 * H], K.zT[:, 500 * m:500 * m + w],
                              start=True, stop=True).then_inc(adp, 1)
                for b in range(NB):
                    if b < 7:
                        pe.wait_ge(adt, b + 1)
                    else:
                        pe.wait_ge(projv, b - 6)
                    pe.matmul(K.ps[0:P, b % 7, 0:W], K.zT[:, P * b:P * b + P], K.wext[:, k, 0:W],
                              start=True, stop=True).then_inc(proj, 1)

            @block.scalar
            def _(act):
                act.wait_ge(adz, 1)
                for m in range(7):
                    n = min(4, NB - 4 * m)
                    act.wait_ge(adp, m + 1)
                    act.activation(adr[:, 4 * m:4 * m + n, 0:P],
                                   K.ps[0:H, m, 0:n * P].rearrange("p (b c) -> p b c", c=P), ACT.Copy).then_inc(adt, 1)
                act.wait_ge(asr, 1)
                act.activation(u[:, 0], asg[:], ACT.Exp).then_inc(ur, 1)
                act.activation(u[:, 1], asg[:], ACT.Exp, scale=0.2).then_inc(ur, 1)
                act.wait_ge(tr, 2)
                act.activation(T.c[:], tm[:], ACT.Exp).then_inc(ur, 1)
                for p in range(3):
                    for q in range(5):
                        if p == 0:
                            act.wait_ge(vals_ready, q + 1)
                        else:
                            act.wait_ge(rest, 5 * (p - 1) + q + 1)
                        act.activation(T.mv[:, 5 * q:5 * q + 5, 0:6 * H * F]
                                       .rearrange("p b (h c f) -> p b h c f", h=H, c=3)[:, :, :, p],
                                       val[:, 5 * q:5 * q + 5].rearrange("p b h a f -> p b h (a f)"),
                                       ACT.Copy).then_inc(part, 1)

            @block.gpsimd
            def _(pool):
                pool.memset(adr[:], 0.0).then_inc(adz, 1)
                pool.wait_ge(mx, 1)
                pool.partition_all_reduce(gmax[:, 1], gmax[:, 0], P, bass.bass_isa.ReduceOp.max).then_inc(mxr, 1)

            @block.sync
            def _(sp):
                sp.wait_ge(adt, 7)
                sp.dma_start(K.ad_rows[0:H], adr[:]).then_inc(adst, 16)
                sp.wait_ge(adst, 16)

            @block.vector
            def _(v):
                link = Chain(v, own)
                for b in range(NB):
                    v.wait_ge(proj, b + 1)
                    v.tensor_copy(hx[:, b, 0:W], K.ps[0:P, b % 7, 0:W]).then_inc(projv, 1)
                v.wait_ge(projv, NB)
                a_s, a_d = hx[:, :, D:D + H], hx[:, :, D + H:D + 2 * H]
                v.tensor_reduce(gmax[:, 0], a_s.rearrange("p b h -> p h b"), AX.X, ALU.max).then_inc(mx, 1)
                link(v.tensor_scalar(T.thr[:, 0], a_s, -1.0, None, ALU.mult))
                link(v.tensor_scalar(T.thr[:, 1], a_s, -STEEP, None, ALU.mult))
                v.wait_ge(mxr, 1)
                G = gmax[:, 1].unsqueeze(1).to_broadcast([P, NB, H])
                v.tensor_tensor(asg[:], a_s, G, ALU.subtract).then_inc(asr, 1)
                link(v.tensor_tensor(t[:], a_d, G, ALU.add))
                v.tensor_scalar(tm[:, 0], t[:], 0.8, 0.0, ALU.mult, ALU.min).then_inc(tr, 1)
                v.tensor_scalar(tm[:, 1], t[:], -0.8, 0.0, ALU.mult, ALU.min).then_inc(tr, 1)
                v.wait_ge(ur, 2)
                if F > FH + 1:
                    link(v.memset(val[:, :, :, 0, F - 1:F], 1.0))
                    link(v.memset(val[:, :, :, 1, F - 1:F], -1.0))
                link(v.tensor_copy(val[:, :, :, 0, FH:FH + 1], u[:, 1].unsqueeze(3)))
                link(v.tensor_scalar(val[:, :, :, 1, FH:FH + 1], u[:, 0].unsqueeze(3), -1.0, None, ALU.mult))
                for q in range(5):
                    s = slice(5 * q, 5 * q + 5)
                    h4 = hx[:, s, 0:D].rearrange("p b (h f) -> p b h f", h=H)
                    ub = lambda i: u[:, i, s].unsqueeze(3).to_broadcast([P, 5, H, FH])
                    link(v.tensor_tensor(val[:, s, :, 0, 0:FH], h4, ub(1), ALU.mult))
                    link(v.scalar_tensor_tensor(val[:, s, :, 1, 0:FH], h4, -1.0, ub(0), ALU.mult, ALU.mult))
                    v.sem_inc(vals_ready, 1)
                for p in range(2):
                    for q in range(5):
                        s = slice(5 * q, 5 * q + 5)
                        v.wait_ge(part, 5 * p + q + 1)
                        if p == 1:
                            v.wait_ge(rest, q + 1)
                        vv = val[:, s].rearrange("p b h a f -> p b h (a f)")
                        v.tensor_tensor(vv, vv, T.mv[:, s, 0:6 * H * F]
                                        .rearrange("p b (h c f) -> p b h c f", h=H, c=3)[:, :, :, p],
                                        ALU.subtract).then_inc(rest, 1)
                for c in range(3):
                    v.wait_ge(part, 5 * c + 5)
                    v.tensor_scalar(T.mv[:, :, (6 + c) * H * F:(7 + c) * H * F].rearrange("p b (h f) -> p b h f", h=H),
                                    T.mv[:, :, 0:6 * H * F]
                                    .rearrange("p b (h c a f) -> p b h c a f", h=H, c=3, a=2)[:, :, :, c, 1],
                                    -1.0, None, ALU.mult)


@phase
def attention(nc, K, S, tag, counts, H, F, T):
    L = 9 * H * F
    G5 = NB // 5
    HF = H * F
    on_act = [h for h in range(H) if h % 2 == 1]
    with ExitStack() as ctx:
        sb = lambda name, shape, dt: ctx.enter_context(nc.sbuf_tensor(tag + name, shape, dt))
        ct = sb("ct", [P, 2, 5, 5, PAD], F16)
        ad = sb("ad", [P, 2, H, 5 * PAD], F32)
        sel = sb("sel", [P, 5, H, 5, PAD], F16)
        msk = sb("msk", [P, 5, 2, 5, PAD], F16)
        cs = sb("cs", [P, 5, 5, PAD], F16)
        vs = sb("vs", [P, 5, L], BF16)
        tmp = sb("tmp", [P, 2, HF], F32)
        landed, ad_landed, masked, copied, valued, used, drained, own, mready = (
            S(tag + "_" + n) for n in ("landed", "adl", "masked", "copied", "valued", "used", "drained", "own", "mready"))
        with nc.Block() as block:
            @block.sync
            def _(sp):
                sp.sem_inc(landed, 16)
                sp.sem_inc(ad_landed, 16)
                with sp.Fori(0, 5) as g:
                    slot, first = sp.snap(g % 2), sp.snap(5 * g)
                    made, had = sp.snap(25 * g + 5), sp.snap(16 * g + 16)
                    ready_first(sp, slot, first, made, had)
                    sp.wait_ge(masked, made)
                    sp.wait_ge(ad_landed, had)
                    sp.dma_start(ad[:, bass.ds(slot, 1)].rearrange("p a h d -> p (a h) d"),
                                 K.ad_rows[0:H, bass.ds(first, 5)].rearrange("h b d -> h (b d)").partition_broadcast(P)
                                 ).then_inc(ad_landed, 16)
                    with sp.Fori(0, 5) as c:
                        made, had = sp.snap(25 * g + 5 * c + 5), sp.snap(80 * g + 16 * c + 16)
                        cslot, hi = sp.snap((g + c) % 2), sp.snap(5 * c)
                        ready_first(sp, made, had, cslot, hi)
                        sp.wait_ge(masked, made)
                        sp.wait_ge(copied, made)
                        sp.wait_ge(landed, had)
                        sp.dma_start(ct[:, bass.ds(cslot, 1)].rearrange("p a b h d -> p (a b) h d"),
                                     counts[:, bass.ds(first, 5), bass.ds(hi, 5)]).then_inc(landed, 16)

            @block.vector
            def _(v):
                v.sem_inc(masked, 10)
                v.sem_inc(drained, 1)
                with v.Fori(0, 5) as g:
                    with v.Fori(0, 5) as c:
                        v.wait_ge(ad_landed, 16 * g + 32)
                        v.wait_ge(landed, 80 * g + 16 * c + 32)
                        tile = ct[:, bass.ds((g + c) % 2, 1)].rearrange("p a b h d -> p (a b) h d")
                        for j in range(5):
                            v.wait_ge(used, 25 * g + 5 * c + j + 1)
                            for h in range(H):
                                if h in on_act:
                                    continue
                                thr = T.thr[:, 0, bass.ds(5 * c + j, 1), h:h + 1].rearrange("p a b -> p (a b)")
                                ins = v.scalar_tensor_tensor(
                                    sel[:, j, h], ad[:, bass.ds(g % 2, 1), h].rearrange("p a (b d) -> p (a b) d", d=PAD),
                                    thr, tile[:, :, j], ALU.is_lt, ALU.mult)
                            for n, h in enumerate(on_act):
                                v.wait_ge(mready, len(on_act) * (25 * g + 5 * c + j) + n + 1)
                                ins = v.tensor_tensor(sel[:, j, h], msk[:, j, n], tile[:, :, j], ALU.mult)
                            ins.then_inc(masked, 1)
                    v.wait_ge(used, 25 * g + 30)
                    for b in range(5):
                        acc = K.ps[0:P, b, 0:2 * HF].rearrange("p (h a f) -> p h a f", h=H, a=2)
                        cb = lambda i, n: T.c[:, i, bass.ds(5 * g + b, 1)].rearrange("p b h -> p (b h)").unsqueeze(2) \
                            .to_broadcast([P, H, n])
                        t0, t1 = (tmp[:, i].rearrange("p (h f) -> p h f", h=H) for i in (0, 1))
                        n = F - (F > D + 1)
                        v.tensor_tensor(t0[:, :, 0:n], acc[:, :, 0, 0:n], cb(1, n), ALU.mult).then_inc(own, 1)
                        v.tensor_tensor(t1[:, :, 0:n], acc[:, :, 1, 0:n], cb(0, n), ALU.mult).then_inc(own, 1)
                        if F > D + 1:
                            v.tensor_copy(t0[:, :, F - 1:F], acc[:, :, 0, F - 1:F]).then_inc(own, 1)
                            v.tensor_copy(t1[:, :, F - 1:F], acc[:, :, 1, F - 1:F]).then_inc(own, 1)
                        q = 5 if F > D + 1 else 3
                        v.wait_ge(own, 5 * q * g + q * b + q - 1)
                        v.tensor_tensor(T.num[:, bass.ds(5 * g + b, 1)].rearrange("p b h f -> p (b h) f"), t0, t1,
                                        ALU.add).then_inc(own, 1)
                        v.wait_ge(own, 5 * q * g + q * b + q)
                    v.sem_inc(drained, 1)

            @block.scalar
            def _(act):
                act.sem_inc(copied, 10)
                with act.Fori(0, 5) as g:
                    with act.Fori(0, 5) as c:
                        act.wait_ge(ad_landed, 16 * g + 32)
                        act.wait_ge(landed, 80 * g + 16 * c + 32)
                        tile = ct[:, bass.ds((g + c) % 2, 1)].rearrange("p a b h d -> p (a b) h d")
                        for j in range(5):
                            act.wait_ge(masked, 25 * g + 5 * c + j + 1 + 5)
                            for n, h in enumerate(on_act):
                                thr = T.thr[:, 1, bass.ds(5 * c + j, 1), h:h + 1].rearrange("p a b -> p (a b)")
                                act.activation(msk[:, j, n], ad[:, bass.ds(g % 2, 1), h]
                                               .rearrange("p a (b d) -> p (a b) d", d=PAD),
                                               ACT.Sigmoid, bias=thr, scale=-STEEP).then_inc(mready, 1)
                            act.wait_ge(used, 25 * g + 5 * c + j + 1)
                            act.activation(cs[:, j], tile[:, :, j], ACT.Copy).then_inc(copied, 1)

            @block.gpsimd
            def _(pool):
                with pool.Fori(0, 5) as g:
                    with pool.Fori(0, 5) as c:
                        for j in range(5):
                            pool.wait_ge(used, 25 * g + 5 * c + j + 1)
                            pool.tensor_copy(vs[:, j].bitcast(F32).unsqueeze(1),
                                             T.mv[:, bass.ds(5 * c + j, 1)].bitcast(F32)).then_inc(valued, 1)

            @block.tensor
            def _(pe):
                pe.sem_inc(used, 5)
                with pe.Fori(0, 5) as g:
                    pe.wait_ge(drained, g + 1)
                    for b in range(5):
                        pe.matmul(K.ps[:, b, :], K.zeros[:, 0:128], K.zeros[:], start=True, stop=True)
                    with pe.Fori(0, 5) as c:
                        for j in range(5):
                            pe.wait_ge(masked, 25 * g + 5 * c + j + 1 + 10)
                            pe.wait_ge(copied, 25 * g + 5 * c + j + 1 + 10)
                            pe.wait_ge(valued, 25 * g + 5 * c + j + 1)
                            for b in range(5):
                                for h in range(H):
                                    for p in range(3):
                                        pe.matmul(K.ps[:, b, 2 * h * F:2 * (h + 1) * F], sel[:, j, h, b],
                                                  vs[:, j, (h * 3 + p) * 2 * F:(h * 3 + p + 1) * 2 * F],
                                                  start=False, stop=False, skip_group_check=True)
                                for p in range(3):
                                    ins = pe.matmul(K.ps[:, b, 0:2 * HF].rearrange("p (h a f) -> p h a f", h=H, a=2)[:, :, 1],
                                                    cs[:, j, b],
                                                    vs[:, j, (6 + p) * HF:(7 + p) * HF].rearrange("p (h f) -> p h f", h=H),
                                                    start=False, stop=False, skip_group_check=True)
                            ins.then_inc(used, 1)


@phase
def gat_normalise(nc, K, S, tag, num, z, degree):
    with ExitStack() as ctx:
        rden = ctx.enter_context(nc.sbuf_tensor(tag + "rden", [P, NB], F32))
        own, root = S(tag + "_own"), S(tag + "_root")
        with nc.Block() as block:
            @block.vector
            def _(v):
                link = Chain(v, own)
                if degree:
                    link(v.tensor_scalar(K.dinv[:], num[:, :, 0, D + 1], 1.0, None, ALU.max))
                link(v.reciprocal(rden[:], num[:, :, 0, D]))
                v.tensor_tensor(z[0:P], num[:, :, 0, 0:D], rden[:].unsqueeze(2).to_broadcast([P, NB, D]), ALU.mult)
                if degree:
                    v.wait_ge(root, 1)
                    v.reciprocal(K.dinv[:], K.dinv[:])

            @block.scalar
            def _(act):
                if degree:
                    act.wait_ge(own, 1)
                    act.activation(K.dinv[:], K.dinv[:], ACT.Sqrt).then_inc(root, 1)


@phase
def relation_sum(nc, K, S, tag, num, r):
    with ExitStack() as ctx:
        sb = lambda name, shape, dt: ctx.enter_context(nc.sbuf_tensor(tag + name, shape, dt))
        rden = sb("rden", [P, NB, 4], F32)
        own = S(tag + "_own")
        with nc.Block() as block:
            @block.vector
            def _(v):
                link = Chain(v, own)
                wr = K.relw[0:P, 3 + r:4 + r]
                link(v.reciprocal(rden[:], num[:, :, :, 32]))
                link(v.tensor_scalar(rden[:], rden[:], wr, None, ALU.mult))
                link(v.tensor_tensor(num[:, :, :, 0:32], num[:, :, :, 0:32],
                                     rden[:].unsqueeze(3).to_broadcast([P, NB, 4, 32]), ALU.mult))
                x4 = K.x[:].rearrange("p b (h f) -> p b h f", h=4)
                link(v.tensor_tensor(x4, x4, num[:, :, :, 0:32], ALU.add))
                v.scalar_tensor_tensor(K.x[:], K.rows[0:P, r * D:(r + 1) * D].unsqueeze(1).to_broadcast([P, NB, D]),
                                       wr, K.x[:], ALU.mult, ALU.add)


@phase
def relation_weights(nc, K, S):
    own, done = S("relw_own"), S("relw_exp")
    with ExitStack() as ctx:
        m = ctx.enter_context(nc.sbuf_tensor("relm", [128, 2], F32))
        with nc.Block() as block:
            @block.vector
            def _(v):
                link = Chain(v, own)
                link(v.tensor_copy(K.relw[:, 0:3], K.rows[:, ROW_RELW:ROW_RELW + 3]))
                link(v.tensor_reduce(m[:, 0:1], K.relw[:, 0:3], AX.X, ALU.max))
                link(v.tensor_scalar(K.relw[:, 0:3], K.relw[:, 0:3], m[:, 0:1], None, ALU.subtract))
                v.wait_ge(done, 1)
                link(v.tensor_reduce(m[:, 0:1], K.relw[:, 3:6], AX.X, ALU.add))
                link(v.reciprocal(m[:, 1:2], m[:, 0:1]))
                v.tensor_scalar(K.relw[:, 3:6], K.relw[:, 3:6], m[:, 1:2], None, ALU.mult)

            @block.scalar
            def _(act):
                act.wait_ge(own, 3)
                act.activation(K.relw[:, 3:6], K.relw[:, 0:3], ACT.Exp).then_inc(done, 1)


@phase
def split_parts(nc, K, S, tag, val, W, parts, scale=None):
    ready, part, rest = (S(tag + "_" + n) for n in ("ready", "part", "rest"))
    with nc.Block() as block:
        @block.vector
        def _(v):
            for q in range(5):
                s = slice(5 * q, 5 * q + 5)
                if scale is not None:
                    v.tensor_tensor(val[:, s], val[:, s], scale[:, s].unsqueeze(2).to_broadcast([P, 5, W]),
                                    ALU.mult).then_inc(ready, 1)
                else:
                    v.sem_inc(ready, 1)
            for p in range(2):
                for q in range(5):
                    s = slice(5 * q, 5 * q + 5)
                    v.wait_ge(part, 5 * p + q + 1)
                    if p == 0:
                        v.wait_ge(ready, q + 1)
                    else:
                        v.wait_ge(rest, q + 1)
                    v.tensor_tensor(val[:, s], val[:, s], parts[:, s, p], ALU.subtract).then_inc(rest, 1)

        @block.scalar
        def _(act):
            for p in range(3):
                for q in range(5):
                    act.wait_ge(ready if p == 0 else rest, q + 1 if p == 0 else 5 * (p - 1) + q + 1)
                    act.activation(parts[:, 5 * q:5 * q + 5, p], val[:, 5 * q:5 * q + 5], ACT.Copy).then_inc(part, 1)


@phase
def gather_in(nc, K, S, tag, parts, dst):
    with ExitStack() as ctx:
        ct = ctx.enter_context(nc.sbuf_tensor(tag + "ct", [P, 5, 5, 5, PAD], F16))
        landed = [S(f"{tag}_landed{c}") for c in range(5)]
        used, drained = S(tag + "_used"), S(tag + "_drained")
        with nc.Block() as block:
            @block.sync
            def _(sp):
                with sp.Fori(0, 5) as g:
                    for c in range(5):
                        sp.wait_ge(used, 5 * g + c + 1)
                        sp.dma_start(ct[:, c], K.counts_all[:, bass.ds(5 * g, 5), 5 * c:5 * c + 5]).then_inc(landed[c], 16)

            @block.tensor
            def _(pe):
                pe.sem_inc(used, 5)
                with pe.Fori(0, 5) as g:
                    pe.wait_ge(drained, 5 * g + 5)
                    for c in range(5):
                        pe.wait_ge(landed[c], 16 * g + 16)
                        for j in range(5):
                            hi = 5 * c + j
                            for b in range(5):
                                for p in range(3):
                                    ins = pe.matmul(K.ps[:, b, 0:D], ct[:, c, b, j], parts[:, hi, p],
                                                    start=(hi == 0 and p == 0), stop=(hi == NB - 1 and p == 2))
                        ins.then_inc(used, 1)

            @block.vector
            def _(v):
                v.sem_inc(drained, 5)
                with v.Fori(0, 5) as g:
                    v.wait_ge(used, 5 * g + 10)
                    for b in range(5):
                        v.tensor_scalar(dst[:, bass.ds(5 * g + b, 1)].rearrange("p a f -> p (a f)"), K.ps[0:P, b, 0:D],
                                        K.dinv[:, bass.ds(5 * g + b, 1)], None, ALU.mult).then_inc(drained, 1)


@phase
def gather_out(nc, K, S, tag, parts, W, dst):
    with ExitStack() as ctx:
        sb = lambda name, shape, dt: ctx.enter_context(nc.sbuf_tensor(tag + name, shape, dt))
        ct = sb("ct", [P, 5, 5, 5, PAD], F16)
        cT = sb("cT", [128, 5, 5, PAD], F16)
        landed = [S(f"{tag}_landed{c}") for c in range(5)]
        turned, moved_v, moved_a, used, drained, cleared = (S(tag + "_" + n) for n in
                                                ("turned", "movedv", "moveda", "used", "drained", "cleared"))
        T16 = K.ps[:].bitcast(F16)
        with nc.Block() as block:
            @block.sync
            def _(sp):
                with sp.Fori(0, 5) as c:
                    for g in range(5):
                        sp.wait_ge(turned, 25 * c + 5 * g + 5)
                        sp.dma_start(ct[:, g], K.counts_all[:, 5 * g:5 * g + 5, bass.ds(5 * c, 5)]).then_inc(landed[g], 16)

            def moved(eng, c, n):
                eng.wait_ge(moved_a if n % 2 else moved_v, (12 * c if n % 2 else 13 * c) + n // 2 + (13 if n % 2 else 14))

            @block.tensor
            def _(pe):
                pe.wait_ge(cleared, 1)
                pe.sem_inc(used, 5)
                pe.sem_inc(turned, 25)
                with pe.Fori(0, 5) as c:
                    for n in range(26):
                        if n < 25:
                            g, j = n // 5, n % 5
                            if j == 0:
                                pe.wait_ge(landed[g], 16 * c + 16)
                            if n >= 3:
                                moved(pe, c, n - 3)
                            else:
                                pe.wait_ge(moved_v, 13 * c + 13)
                                pe.wait_ge(moved_a, 12 * c + 12)
                            for b in range(5):
                                ins = pe.transpose(T16[:, 5 + n % 3, b * PAD:b * PAD + P], ct[:, g, b, j],
                                                   K.ident16[0:P, 0:P])
                            ins.then_inc(turned, 1)
                        if n >= 1:
                            m = n - 1
                            g, j = m // 5, m % 5
                            moved(pe, c, m)
                            if m == 0:
                                pe.wait_ge(drained, 5 * c + 5)
                            for b in range(5):
                                for p in range(3):
                                    ins = pe.matmul(K.ps[:, j, 0:W], cT[0:P, m % 5, b], parts[:, 5 * g + b, p],
                                                    start=(g == 0 and b == 0 and p == 0),
                                                    stop=(g == 4 and b == 4 and p == 2))
                            ins.then_inc(used, 1)

            def move(eng, c, n, copy, sem):
                eng.wait_ge(turned, 25 * c + n + 26)
                eng.wait_ge(used, 25 * c + n + 1)
                out = cT[:, n % 5, :, 0:P]
                got = T16[:, 5 + n % 3, 0:5 * PAD].rearrange("p (b s) -> p b s", s=PAD)[:, :, 0:P]
                copy(out, got).then_inc(sem, 1)

            @block.vector
            def _(v):
                v.memset(cT[:], 0.0).then_inc(cleared, 1)
                v.wait_ge(cleared, 1)
                v.sem_inc(moved_v, 13)
                v.sem_inc(drained, 5)
                with v.Fori(0, 5) as c:
                    for n in range(0, 25, 2):
                        move(v, c, n, v.tensor_copy, moved_v)
                    v.wait_ge(used, 25 * c + 30)
                    for j in range(5):
                        v.tensor_copy(dst[:, bass.ds(5 * c + j, 1)].rearrange("p a f -> p (a f)"),
                                      K.ps[0:P, j, 0:W]).then_inc(drained, 1)

            @block.scalar
            def _(act):
                act.wait_ge(cleared, 1)
                act.sem_inc(moved_a, 12)
                with act.Fori(0, 5) as c:
                    for n in range(1, 25, 2):
                        move(act, c, n, lambda o, i: act.activation(o, i, ACT.Copy), moved_a)


@phase
def linear_columns(nc, K, S, tag, outs):
    done, taken_a, taken_v = S(tag + "_done"), S(tag + "_takena"), S(tag + "_takenv")
    steps = [(o, m) for o in outs for m in range(7)]
    on_act = [o[3] is not None or (o[4] is None and m % 2 == 1) for o, m in steps]
    with nc.Block() as block:
        @block.tensor
        def _(pe):
            for n, ((dst, terms, bias, func, add), m) in enumerate(steps):
                if n >= 8:
                    a = on_act[n - 8]
                    pe.wait_ge(taken_a if a else taken_v, sum(x == a for x in on_act[:n - 7]))
                w = min(500, N - 500 * m)
                for i, (wt, src) in enumerate(terms):
                    ins = pe.matmul(K.ps[:, n % 8, 0:w], wt, src[:, 500 * m:500 * m + w], start=(i == 0),
                                    stop=(i == len(terms) - 1))
                ins.then_inc(done, 1)

        @block.scalar
        def _(act):
            for n, ((dst, terms, bias, func, add), m) in enumerate(steps):
                if on_act[n]:
                    w = min(500, N - 500 * m)
                    act.wait_ge(done, n + 1)
                    act.activation(dst[:, 500 * m:500 * m + w], K.ps[:, n % 8, 0:w], func or ACT.Identity,
                                   bias=bias).then_inc(taken_a, 1)

        @block.vector
        def _(v):
            for n, ((dst, terms, bias, func, add), m) in enumerate(steps):
                if not on_act[n]:
                    w = min(500, N - 500 * m)
                    s = slice(500 * m, 500 * m + w)
                    v.wait_ge(done, n + 1)
                    if add is None:
                        v.tensor_scalar(dst[:, s], K.ps[:, n % 8, 0:w], bias, None, ALU.add).then_inc(taken_v, 1)
                    else:
                        v.scalar_tensor_tensor(dst[:, s], K.ps[:, n % 8, 0:w], bias, add[:, s], ALU.add,
                                               ALU.add).then_inc(taken_v, 1)


@phase
def linear_rows(nc, K, S, tag, terms, W, dst, bias=None):
    done, taken = S(tag + "_done"), S(tag + "_taken")
    with nc.Block() as block:
        @block.tensor
        def _(pe):
            for b in range(NB):
                if b >= 8:
                    pe.wait_ge(taken, b - 7)
                for i, (src, wt) in enumerate(terms):
                    ins = pe.matmul(K.ps[0:P, b % 8, 0:W], src[:, P * b:P * b + P], wt, start=(i == 0),
                                    stop=(i == len(terms) - 1))
                ins.then_inc(done, 1)

        @block.vector
        def _(v):
            for b in range(NB):
                v.wait_ge(done, b + 1)
                if bias is None:
                    v.tensor_copy(dst[:, b, 0:W], K.ps[0:P, b % 8, 0:W]).then_inc(taken, 1)
                else:
                    v.tensor_tensor(dst[:, b, 0:W], K.ps[0:P, b % 8, 0:W], bias, ALU.add).then_inc(taken, 1)


@phase
def load(nc, K, S, tag, pairs):
    landed = S(tag + "_landed")
    with nc.Block() as block:
        @block.sync
        def _(sp):
            for dst, src in pairs:
                sp.dma_start(dst, src).then_inc(landed, 16)
            sp.wait_ge(landed, 16 * len(pairs))


@phase
def head_attention(nc, K, S, tag, qkv, ks, att):
    H, DH = 8, 16
    with ExitStack() as ctx:
        sb = lambda name, shape, dt: ctx.enter_context(nc.sbuf_tensor(tag + name, shape, dt))
        rc = sb("rc", [P, NB], F32)
        pr = sb("pr", [P, 4, H, H, DH], F32)
        s = sb("s", [P, NB, H, H], F32)
        m = sb("m", [P, NB, H], F32)
        own, mult, red, pown, edone = (S(tag + "_" + n) for n in ("own", "mult", "red", "pown", "exp"))
        q = qkv[:, :, 0:D].rearrange("p b (h d) -> p b h d", h=H)
        k = ks[:, :, 0:D].rearrange("p b (g d) -> p b g d", g=H)
        vT = qkv[:, :, 2 * D:3 * D].rearrange("p b (g d) -> p b d g", g=H)
        with nc.Block() as block:
            @block.vector
            def _(v):
                link = Chain(v, own)
                link(v.tensor_scalar(rc[:], ks[:, :, D], -1.0, 1.0, ALU.add, ALU.max))
                link(v.reciprocal(rc[:], rc[:]))
                link(v.tensor_tensor(ks[:, :, 0:D], ks[:, :, 0:D], qkv[:, :, D:2 * D], ALU.subtract))
                link(v.tensor_tensor(ks[:, :, 0:D], ks[:, :, 0:D], rc[:].unsqueeze(2).to_broadcast([P, NB, D]), ALU.mult))
                for b in range(NB):
                    if b >= 2:
                        v.wait_ge(red, b - 1)
                    v.tensor_tensor(pr[:, b % 2], q[:, b].unsqueeze(2).to_broadcast([P, H, H, DH]),
                                    k[:, b].unsqueeze(1).to_broadcast([P, H, H, DH]), ALU.mult).then_inc(mult, 1)
                    v.wait_ge(mult, b + 1)
                    v.tensor_reduce(s[:, b], pr[:, b % 2], AX.X, ALU.add).then_inc(red, 1)
                v.wait_ge(red, NB)
                link(v.tensor_reduce(m[:], s[:], AX.X, ALU.max))
                link(v.tensor_tensor(s[:], s[:], m[:].unsqueeze(3).to_broadcast([P, NB, H, H]), ALU.subtract))
                v.wait_ge(edone, 1)
                link(v.tensor_reduce(m[:], s[:], AX.X, ALU.add))
                link(v.reciprocal(m[:], m[:]))
                link(v.tensor_tensor(s[:], s[:], m[:].unsqueeze(3).to_broadcast([P, NB, H, H]), ALU.mult))
                for b in range(NB):
                    v.wait_ge(red, NB + max(b - 1, 0))
                    prb = pr[:, b % 2].rearrange("p h g d -> p (h g d)").rearrange("p (h d g) -> p h d g", h=H, d=DH)
                    v.tensor_tensor(prb, s[:, b].unsqueeze(2).to_broadcast([P, H, DH, H]),
                                    vT[:, b].unsqueeze(1).to_broadcast([P, H, DH, H]), ALU.mult).then_inc(mult, 1)
                    v.wait_ge(mult, NB + b + 1)
                    v.tensor_reduce(att[:, b].rearrange("p (h d) -> p h d", h=H), prb, AX.X, ALU.add).then_inc(red, 1)

            @block.scalar
            def _(act):
                act.wait_ge(own, 6)
                act.activation(s[:], s[:], ACT.Exp).then_inc(edone, 1)


STEEP = 1.0e8
COLS = [("a", 6), ("att", 6), ("b0", 3), ("g_in", 1), ("be_in", 1), ("b1", 2), ("g1", 2), ("be1", 2), ("b2", 1),
        ("g2", 1), ("be2", 1), ("bo", 1), ("fb1", 4), ("fb2", 1), ("fg1", 1), ("fbe1", 1), ("fg2", 1), ("fbe2", 1)]
COL, NCOL = {}, 0
for _name, _n in COLS:
    COL[_name] = NCOL
    NCOL += _n
ROW_RELW = 3 * D
ROW_QKV = 3 * D + 3
NROW = ROW_QKV + 3 * D


class Names:
    pass


def build(nc, args, out):
    K, T = Names(), Names()
    K.src_t, K.dst_t, K.typ_t, K.dst_n = (args[n] for n in ("src_t", "dst_t", "typ_t", "dst_n"))
    K.x_in, K.w_in, K.cols_in, K.rows_in = (args[n] for n in ("x_in", "w_in", "cols_in", "rows_in"))
    K.w1_in, K.w2_in, K.wq_in, K.wk_in = (args[n] for n in ("w1_in", "w2_in", "wq_in", "wk_in"))
    K.wv_in, K.wo_in, K.fw1_in, K.fw2_in = (args[n] for n in ("wv_in", "wo_in", "fw1_in", "fw2_in"))
    with ExitStack() as ctx:
        sb = lambda name, shape, dt: ctx.enter_context(nc.sbuf_tensor(name, shape, dt))
        S = lambda name: ctx.enter_context(nc.semaphore(name))
        col = lambda name, i=0: K.cols[:, COL[name] + i:COL[name] + i + 1]
        K.ps = ctx.enter_context(nc.psum_tensor("ps", [128, 8, 512], F32))
        K.counts = nc.dram_tensor("counts", [R, P, NB, NB, PAD], F16)
        K.counts_all = nc.dram_tensor("counts_all", [P, NB, NB, PAD], F16)
        K.chunk_range = nc.dram_tensor("chunk_range", [2, NCH], F32)
        K.first_chunk = nc.dram_tensor("first_chunk", [NG], I32)
        K.ad_rows = nc.dram_tensor("ad_rows", [4, NB, PAD], F32)
        K.x = sb("x", [P, NB, D], F32)
        K.zT = sb("zT", [D, N], F32)
        K.wext = sb("wext", [D, 6, D + 8], F32)
        K.cols = sb("cols", [D, NCOL], F32)
        K.rows = sb("rows", [128, NROW], F32)
        K.relw = sb("relw", [128, 6], F32)
        K.ident = sb("ident", [128, 128], F32)
        K.ident16 = sb("ident16", [128, 128], F16)
        K.zeros = sb("zeros", [P, 512], BF16)
        K.dinv = sb("dinv", [P, NB], F32)
        with nc.cleanup_on_exit():
            load_constants(nc, K)
            load(nc, K, "rows", [(K.rows[:], K.rows_in.partition_broadcast(128))])
            score_weights(nc, K)
            relation_weights(nc, K)
            with ExitStack() as c2:
                sb2 = lambda name, shape, dt: c2.enter_context(nc.sbuf_tensor(name, shape, dt))
                K.key_lo = sb2("key_lo", [P, NCH], F32)
                K.key_col = sb2("key_col", [P, NCH], F32)
                K.group_base = sb2("group_base", [P, NG], F32)
                K.iota_col = sb2("iota_col", [P, GE], F16)
                K.window = sb2("window", [1, NG], I32)
                K.wide = sb2("wide", [1, 1], I32)
                prepare_edges(nc, K)
                count_edges(nc, K)

        def gat(tag, k, H, F, counts, finish):
            with ExitStack() as c3:
                sb3 = lambda name, shape, dt: c3.enter_context(nc.sbuf_tensor(tag + name, shape, dt))
                T.mv = sb3("mv", [P, NB, 9 * H * F], BF16)
                T.thr = sb3("thr", [P, 2, NB, H], F32)
                T.c = sb3("c", [P, 2, NB, H], F32)
                scores(nc, K, tag + "s", k, H, F, T)
                T.num = sb3("num", [P, NB, H, F], F32)
                attention(nc, K, tag + "a", counts, H, F, T)
                finish()

        turn_to_columns(nc, K, "t0", K.x, K.zT)
        for l in range(3):
            tag = f"g{l}"

            def finish():
                gat_normalise(nc, K, tag + "n", T.num, K.z, l == 0)
                turn_to_columns(nc, K, tag + "t", K.z, K.zT, bias=col("b0", l))
            with nc.cleanup_on_exit(), nc.sbuf_tensor(tag + "z", [P, NB, D], F32) as K.z:
                gat(tag, l, 1, D + 2, K.counts_all, finish)
                batch_norm(nc, K, tag + "b", K.zT, K.zT, relu=True)
        with nc.cleanup_on_exit():
            turn_to_rows(nc, K, "r0", K.zT, K.x, residual=K.x)
            layer_norm(nc, K, "ln0", K.x)

        with nc.cleanup_on_exit(), ExitStack() as c2:
            sb2 = lambda name, shape, dt: c2.enter_context(nc.sbuf_tensor(name, shape, dt))
            z = sb2("z1", [P, NB, D], F32)
            parts = sb2("parts1", [P, NB, 3, D], BF16)
            wide = sb2("wide1", [D, 2, N], F32)
            w1 = sb2("w1", [D, 2, D], F32)
            w2 = sb2("w2", [D, 2, D], F32)
            load(nc, K, "w1", [(w1[:], K.w1_in.rearrange("f (j o) -> f j o", j=2)),
                                  (w2[:], K.w2_in.rearrange("(j f) o -> f j o", j=2))])
            turn_to_columns(nc, K, "t1", K.x, K.zT)
            batch_norm(nc, K, "b1", K.zT, K.zT, col("g_in"), col("be_in"))
            turn_to_rows(nc, K, "r1", K.zT, z)
            split_parts(nc, K, "p1", z, D, parts, scale=K.dinv)
            gather_in(nc, K, "c1", parts, z)
            turn_to_columns(nc, K, "t2", z, K.zT)
            linear_columns(nc, K, "l1", [(wide[:, j], [(w1[:, j], K.zT)], col("b1", j), None, None) for j in range(2)])
            for j in range(2):
                batch_norm(nc, K, f"b2{j}", wide[:, j], wide[:, j], col("g1", j), col("be1", j), relu=True)
            linear_rows(nc, K, "l2", [(wide[:, j], w2[:, j]) for j in range(2)], D, z)
            split_parts(nc, K, "p2", z, D, parts, scale=K.dinv)
            gather_in(nc, K, "c2", parts, z)
            turn_to_columns(nc, K, "t3", z, K.zT, bias=col("b2"))
            batch_norm(nc, K, "b3", K.zT, K.zT, col("g2"), col("be2"), relu=True)
            turn_to_rows(nc, K, "r2", K.zT, K.x, residual=K.x)
            layer_norm(nc, K, "ln1", K.x)

        turn_to_columns(nc, K, "t4", K.x, K.zT)
        for r in range(R):
            tag = f"r{r}"
            with nc.cleanup_on_exit():
                gat(tag, 3 + r, 4, 33, K.counts[r], lambda: relation_sum(nc, K, tag + "n", T.num, r))
        layer_norm(nc, K, "ln2", K.x)

        turn_to_columns(nc, K, "t5", K.x, K.zT)
        with ExitStack() as c2:
            sb2 = lambda name, shape, dt: c2.enter_context(nc.sbuf_tensor(name, shape, dt))
            att = sb2("att3", [P, NB, D], F32)
            with ExitStack() as c3:
                sb3 = lambda name, shape, dt: c3.enter_context(nc.sbuf_tensor(name, shape, dt))
                wqkv = sb3("wqkv", [D, 3 * D], F32)
                qkv = sb3("qkv", [P, NB, 3 * D], F32)
                ks = sb3("ks", [P, NB, D + 1], F32)
                load(nc, K, "wqkv", [(wqkv[:, i * D:(i + 1) * D], w) for i, w in enumerate((K.wq_in, K.wk_in, K.wv_in))])
                linear_rows(nc, K, "l3", [(K.zT, wqkv[:])], 3 * D, qkv, K.rows[0:P, ROW_QKV:NROW])
                with nc.sbuf_tensor("parts3", [P, NB, 3, D + 1], BF16) as parts:
                    key_values(nc, K, qkv, ks)
                    split_parts(nc, K, "p3", ks, D + 1, parts)
                    gather_out(nc, K, "c3", parts, D + 1, ks)
                head_attention(nc, K, "h3", qkv, ks, att)
            with ExitStack() as c3:
                sb3 = lambda name, shape, dt: c3.enter_context(nc.sbuf_tensor(name, shape, dt))
                wo = sb3("wo", [D, D], F32)
                fw1 = sb3("fw1", [D, 4, D], F32)
                fw2 = sb3("fw2", [D, 4, D], F32)
                aT = sb3("aT", [D, N], F32)
                hid = sb3("hid", [D, 4, N], F32)
                load(nc, K, "ffw", [(wo[:], K.wo_in), (fw1[:], K.fw1_in.rearrange("f (j o) -> f j o", j=4)),
                                       (fw2[:], K.fw2_in.rearrange("(j f) o -> f j o", j=4))])
                turn_to_columns(nc, K, "t6", att, aT)
                linear_columns(nc, K, "l4", [(K.zT, [(wo[:], aT)], col("bo"), None, K.zT)])
                batch_norm(nc, K, "b4", K.zT, K.zT, col("fg1"), col("fbe1"))
                linear_columns(nc, K, "l5", [(hid[:, j], [(fw1[:, j], K.zT)], col("fb1", j), ACT.Gelu, None)
                                                for j in range(4)])
                linear_columns(nc, K, "l6", [(K.zT, [(fw2[:, j], hid[:, j]) for j in range(4)], col("fb2"), None, K.zT)])
                batch_norm(nc, K, "b5", K.zT, K.zT, col("fg2"), col("fbe2"))
                turn_to_rows(nc, K, "r3", K.zT, K.x, residual=K.x)
                layer_norm(nc, K, "ln3", K.x)
        stored = S("out_stored")
        with nc.Block() as block:
            @block.sync
            def _(sp):
                sp.dma_start(out.rearrange("(b p) f -> p b f", p=P), K.x[:]).then_inc(stored, 16)
                sp.wait_ge(stored, 16)


@phase
def key_values(nc, K, S, qkv, ks):
    with nc.Block() as block:
        @block.vector
        def _(v):
            v.tensor_copy(ks[:, :, 0:D], qkv[:, :, D:2 * D])

        @block.gpsimd
        def _(pool):
            pool.memset(ks[:, :, D:D + 1], 1.0)


def kernel(**inputs):
    import numpy as _np
    import concourse.bacc as _bacc
    from concourse import mybir as _mybir
    from concourse.bass_utils import run_bass_kernel_spmd as _run

    nc = _bacc.Bacc("TRN2", target_bir_lowering=False, num_devices=1)
    arrays, args = {}, {}

    def give(name, a):
        a = _np.ascontiguousarray(a)
        arrays["in_" + name] = a
        args[name] = nc.dram_tensor("in_" + name, a.shape, _mybir.dt.from_np(a.dtype), kind="ExternalInput").ap()

    i = {k: _np.asarray(v) for k, v in inputs.items()}
    give("src_t", i["src"].reshape(NCH, CH).T)
    give("dst_t", i["dst"].reshape(NCH, CH).T)
    give("typ_t", i["edge_type_3"].reshape(NCH, CH).T)
    give("dst_n", i["dst"].reshape(75, 11, CH))
    give("x_in", i["x"])
    give("w_in", _np.concatenate([i["L0_gnn_W"], i["L2_gnn_W"]]))
    cols = [i[k].reshape(-1, D) for k in (
        "L1_gnn_g_in", "L1_gnn_be_in", "L1_gnn_b1", "L1_gnn_g1", "L1_gnn_be1", "L1_gnn_b2", "L1_gnn_g2", "L1_gnn_be2",
        "L3_gnn_bo", "L3_gnn_b1", "L3_gnn_b2", "L3_gnn_g1", "L3_gnn_be1", "L3_gnn_g2", "L3_gnn_be2")]
    a0 = _np.stack([i["L0_gnn_a_src"], i["L0_gnn_a_dst"]], axis=1).reshape(6, D)
    a2 = _np.stack([i["L2_gnn_att_src"].reshape(R, D), i["L2_gnn_att_dst"].reshape(R, D)], axis=1).reshape(6, D)
    give("cols_in", _np.concatenate([a0, a2, i["L0_gnn_b"]] + cols).T)
    give("rows_in", _np.concatenate([i["L2_gnn_bias"].reshape(-1), i["L2_gnn_rel_w"], i["L3_gnn_bq"], i["L3_gnn_bk"],
                                     i["L3_gnn_bv"]]))
    for name, key in (("w1_in", "L1_gnn_w1"), ("w2_in", "L1_gnn_w2"), ("wq_in", "L3_gnn_wq"), ("wk_in", "L3_gnn_wk"),
                      ("wv_in", "L3_gnn_wv"), ("wo_in", "L3_gnn_wo"), ("fw1_in", "L3_gnn_w1"), ("fw2_in", "L3_gnn_w2")):
        give(name, i[key])
    out = nc.dram_tensor("out_x", (N, D), _mybir.dt.float32, kind="ExternalOutput").ap()
    build(nc, args, out)
    r = _run(nc, [arrays], core_ids=[0])
    return r.results[0]["out_x"]
```

```python
from contextlib import ExitStack

import concourse.bass as bass
from concourse import mybir

F32 = mybir.dt.float32
F16 = mybir.dt.float16
BF16 = mybir.dt.bfloat16
I32 = mybir.dt.int32
U32 = mybir.dt.uint32
ALU = mybir.AluOpType
ACT = mybir.ActivationFunctionType
AX = mybir.AxisListType

N = 3125
P = 125
NB = N // P
D = 128
PAD = 128
E = 103125
CH = P
NCH = E // CH
R = 3
DG = 5
NG = N // DG
GW = R * NB * DG
GE = GW + 1
SUB = 25
NSUB = E // SUB
ROW = CH // SUB
WIN = 2
NROWS = NSUB - ROW + 1
EPS = 1e-5
ROUND = 12582912.0


class Chain:

    def __init__(self, eng, sem, base=0):
        self.eng, self.sem, self.n, self.base = eng, sem, 0, base

    def __call__(self, ins):
        self.n += 1
        ins.then_inc(self.sem, 1)
        self.eng.wait_ge(self.sem, self.base + self.n)


def phase(body):
    def run(nc, K, *rest, **more):
        body(nc, K, nc.alloc_semaphore, *rest, **more)
    return run


def ready_first(eng, *values):
    for value in values:
        eng.compute_val(value)


@phase
def prepare_edges(nc, K, S):
    with ExitStack() as ctx:
        sb = lambda name, shape, dt: ctx.enter_context(nc.sbuf_tensor(name, shape, dt))
        ei = sb("ei", [P, 3, NCH], I32)
        ef = sb("ef", [P, 3, NCH], F32)
        q = sb("q", [P, NCH], F32)
        q5 = sb("q5", [P, NCH], F32)
        mm = sb("mm", [P, 2, NCH // SUB], F16)
        lohi = sb("lohi", [P, 2, NSUB], F16)
        cmp = sb("cmp", [P, NSUB], F16)
        gi = sb("gi", [P, DG], I32)
        gf = sb("gf", [P, DG], F32)
        gb = sb("gb", [P, DG], F32)
        wlo = sb("wlo", [P, DG], F32)
        whi = sb("whi", [P, DG], F32)
        need = sb("need", [P, DG], F32)
        rows = sb("rows_of", [P, DG, WIN], U32)
        win = sb("win", [P, DG, WIN, CH, 2], F32)
        big = sb("big", [P, 2], F32)
        alln = sb("alln", [P, 1], F32)
        flag = sb("flag", [1, 1], I32)
        ti = sb("ti", [P, NG], I32)
        ki = sb("ki", [P, GE], I32)
        pi = sb("pi", [P, PAD, 2], I32)
        (loaded, iotas, own, mmout, mmin, keys_ready, keys_out, table, flag_ready, flag_in, shared, need_ready,
         rows_ready, gathered, based, turned) = (S("prep_" + n) for n in
            ("loaded", "iotas", "own", "mmout", "mmin", "keysr", "keyso", "table", "flagr", "flagin", "shared", "need",
             "rowsr", "gath", "based", "turned"))
        with nc.Block() as block:
            @block.sync
            def _(sp):
                sp.dma_start(ei[:, 1], K.dst_in.rearrange("(p c) -> p c", p=P)).then_inc(loaded, 16)
                sp.dma_start(ei[:, 0], K.src_in.rearrange("(p c) -> p c", p=P)).then_inc(loaded, 16)
                sp.dma_start(ei[:, 2], K.typ_in.rearrange("(p c) -> p c", p=P)).then_inc(loaded, 16)
                sp.wait_ge(mmout, 2)
                sp.dma_start(K.sub_range[:].rearrange("a (p c) -> p a c", p=P), mm[:]).then_inc(mmin, 16)
                sp.wait_ge(mmin, 16)
                sp.dma_start(lohi[:].rearrange("p a c -> p (a c)"),
                             K.sub_range[:].rearrange("a c -> (a c)").partition_broadcast(P)).then_inc(mmin, 16)
                sp.wait_ge(keys_ready, 2)
                sp.dma_start(K.edge_keys[:].rearrange("(p c) -> p c", p=P),
                             K.keys[:].rearrange("p c k -> p (c k)")).then_inc(keys_out, 16)
                sp.wait_ge(keys_out, 16)
                for phase in range(ROW):
                    n = (NROWS - 1 - phase) // ROW + 1
                    sp.dma_start(K.windows[:].rearrange("(r s) e -> s r e", s=ROW)[phase, 0:n],
                                 K.edge_keys[2 * SUB * phase:2 * SUB * phase + 2 * CH * n]
                                 .rearrange("(r e) -> r e", e=2 * CH)).then_inc(table, 16)
                sp.wait_ge(flag_ready, 1)
                sp.dma_start(K.wide[0:1, :], flag[:]).then_inc(flag_in, 16)
                sp.wait_ge(flag_in, 16)

            @block.gpsimd
            def _(pool):
                pool.iota(gi[:], [[P, DG]], channel_multiplier=1).then_inc(iotas, 1)
                pool.iota(ti[:], [[GW, NG]], channel_multiplier=0).then_inc(iotas, 1)
                pool.iota(ki[:], [[1, GE]], channel_multiplier=0).then_inc(iotas, 1)
                pool.iota(pi[:], [[1, PAD], [0, 2]], channel_multiplier=0).then_inc(iotas, 1)
                pool.wait_ge(rows_ready, WIN)
                pool.wait_ge(table, 16 * ROW)
                for j in range(DG):
                    for w in range(WIN):
                        pool.indirect_dma_start(win[:, j, w].rearrange("p e k -> p (e k)"), None, K.windows[0:NROWS],
                                                bass.IndirectOffsetOnAxis(rows[:, j, w:w + 1], 0)).then_inc(gathered, 16)
                pool.wait_ge(need_ready, 1)
                pool.partition_all_reduce(alln[:], big[:, 0:1], P, bass.bass_isa.ReduceOp.max).then_inc(shared, 1)

            @block.vector
            def _(v):
                link = Chain(v, own)
                fs, fd, ft = ef[:, 0], ef[:, 1], ef[:, 2]
                v.wait_ge(loaded, 48)
                link(v.tensor_copy(ef[:], ei[:]))
                link(v.tensor_scalar(q5[:], fd, -2.0, 1.0 / DG, ALU.add, ALU.mult))
                link(v.tensor_scalar(q5[:], q5[:], ROUND, None, ALU.add))
                link(v.tensor_scalar(q5[:], q5[:], -ROUND, None, ALU.add))
                groups = q5[:].rearrange("p (c e) -> p c e", e=SUB)
                v.tensor_reduce(mm[:, 0], groups, AX.X, ALU.min).then_inc(mmout, 1)
                v.tensor_reduce(mm[:, 1], groups, AX.X, ALU.max).then_inc(mmout, 1)
                link(v.tensor_scalar(q[:], fs, -62.0, 1.0 / P, ALU.add, ALU.mult))
                link(v.tensor_scalar(q[:], q[:], ROUND, None, ALU.add))
                link(v.tensor_scalar(q[:], q[:], -ROUND, None, ALU.add))
                v.scalar_tensor_tensor(K.keys[:, :, 0], q[:], -float(P), fs, ALU.mult, ALU.add).then_inc(keys_ready, 1)
                link(v.scalar_tensor_tensor(fd, q5[:], float(GW - DG), fd, ALU.mult, ALU.add))
                link(v.scalar_tensor_tensor(fd, ft, float(NB * DG), fd, ALU.mult, ALU.add))
                v.scalar_tensor_tensor(K.keys[:, :, 1], q[:], float(DG), fd, ALU.mult, ALU.add).then_inc(keys_ready, 1)
                v.wait_ge(iotas, 4)
                link(v.tensor_copy(gf[:], gi[:]))
                link(v.tensor_scalar(gb[:], gf[:], float(GW), None, ALU.mult))
                link(v.tensor_copy(K.group_base[:], ti[:]))
                link(v.tensor_copy(K.iota_col[:], ki[:]))
                link(v.tensor_copy(K.iota_pair[:], pi[:]))
                v.wait_ge(mmin, 32)
                for j in range(DG):
                    link(v.tensor_scalar(cmp[:], lohi[:, 1], gf[:, j:j + 1], None, ALU.is_lt, ALU.add,
                                         accum_out=wlo[:, j:j + 1]))
                for w in range(WIN):
                    link(v.tensor_scalar(need[:], wlo[:], float(NSUB - WIN * ROW), float(w * ROW), ALU.min, ALU.add))
                    link(v.tensor_copy(rows[:, :, w], need[:]))
                    v.sem_inc(rows_ready, 1)
                for j in range(DG):
                    link(v.tensor_scalar(cmp[:], lohi[:, 0], gf[:, j:j + 1], None, ALU.is_le, ALU.add,
                                         accum_out=whi[:, j:j + 1]))
                link(v.tensor_tensor(need[:], whi[:], wlo[:], ALU.subtract))
                link(v.tensor_reduce(big[:, 0:1], need[:], AX.X, ALU.max))
                link(v.tensor_tensor(cmp[:, 0:NSUB - 1], lohi[:, 1, 0:NSUB - 1], lohi[:, 0, 1:NSUB], ALU.is_gt))
                link(v.tensor_reduce(big[:, 1:2], cmp[:, 0:NSUB - 1], AX.X, ALU.max))
                v.scalar_tensor_tensor(big[:, 0:1], big[:, 1:2], float(NSUB), big[:, 0:1], ALU.mult,
                                       ALU.add).then_inc(need_ready, 1)
                v.wait_ge(gathered, 16 * WIN * DG)
                cols = win[:].rearrange("p j w e k -> p j (w e) k")[:, :, :, 1]
                v.tensor_tensor(cols, cols, gb[:].unsqueeze(2).to_broadcast([P, DG, WIN * CH]),
                                ALU.subtract).then_inc(based, 1)
                v.wait_ge(shared, 1)
                v.tensor_scalar(flag[:], alln[0:1, :], float(WIN * ROW), None, ALU.is_gt).then_inc(flag_ready, 1)
                for j in range(DG):
                    v.wait_ge(turned, 2 * WIN * (j + 1))
                    got = K.ps[0:P, j, 0:2 * WIN * P].rearrange("p (w k g) -> p w k g", w=WIN, k=2)
                    for k, dst in enumerate((K.window_lo, K.window_col)):
                        v.tensor_copy(dst[:, P * j:P * j + P].rearrange("p g w -> p w g"), got[:, :, k])

            @block.tensor
            def _(pe):
                pe.wait_ge(based, 1)
                for j in range(DG):
                    for w in range(WIN):
                        for k in range(2):
                            n = 2 * w + k
                            pe.transpose(K.ps[0:P, j, n * P:(n + 1) * P], win[:, j, w, :, k],
                                         K.ident[0:P, 0:P]).then_inc(turned, 1)


@phase
def count_edges(nc, K, S):
    OHS = 5
    SLOTS = 25
    STEPS = NCH // SLOTS
    STAGES = 3
    with ExitStack() as ctx:
        sb = lambda name, shape, dt: ctx.enter_context(nc.sbuf_tensor(name, shape, dt))
        lo1 = sb("lo1", [P, P // DG, PAD, WIN], BF16)
        col1 = sb("col1", [P, SLOTS, GE], BF16)
        stage = sb("stage", [P, STAGES, R, NB, PAD], F16)
        total = sb("total", [P, 2, NB, PAD], F16)
        lo_wide = lo1[:].rearrange("p s l w -> p (s l w)")[:, 0:SLOTS * PAD].rearrange("p (s l) -> p s l", l=PAD)
        (hot, counted, taken, summed, stored, cleared, diag, wide_hot, wide_used) = (
            S("count_" + n) for n in ("hot", "counted", "taken", "summed", "stored", "cleared", "diag",
                                      "wide_hot", "wide_used"))
        with nc.Block() as block:
            @block.gpsimd
            def _(pool):
                pool.memset(stage[:], 0.0).then_inc(cleared, 1)
                with pool.Fori(0, NB) as i:
                    pool.wait_ge(taken, (i + 1) * (P // DG) + OHS)
                    pool.wait_ge(stored, 64 * i + 64 * (STAGES - 1))
                    st = stage[:, bass.ds(i % STAGES, 1)].rearrange("p a r h d -> p (a r) h d")
                    tot = total[:, bass.ds(i % 2, 1)].rearrange("p a h d -> p (a h) d")
                    link = Chain(pool, summed, 3 * i)
                    link(pool.tensor_tensor(tot, st[:, 0], st[:, 1], ALU.add))
                    link(pool.tensor_tensor(tot, tot, st[:, 2], ALU.add))
                    for r in range(R):
                        own_r = stage[:, bass.ds(i % STAGES, 1), r, bass.ds(i, 1), 0:P].rearrange("p a h d -> p (a h) d")
                        pool.tensor_tensor(own_r, own_r, K.ident16[0:P, 0:P].unsqueeze(1), ALU.add).then_inc(diag, 1)
                    pool.wait_ge(diag, 3 * i + 3)
                    own_t = total[:, bass.ds(i % 2, 1), bass.ds(i, 1), 0:P].rearrange("p a h d -> p (a h) d")
                    link(pool.tensor_tensor(own_t, own_t, K.ident16[0:P, 0:P].unsqueeze(1), ALU.add))
                    assert link.n == 3

            @block.vector
            def _(v):
                wide = v.value_load(K.wide[0:1, 0:1], min_val=0, max_val=1)
                with v.If(wide < 1):
                    with v.Fori(0, NB) as i:
                        for b in range(P // DG):
                            v.wait_ge(counted, i * (P // DG) + b + 1)
                            if b % OHS == 0:
                                v.tensor_tensor(
                                    lo1[:, b:b + OHS], K.iota_pair[:].unsqueeze(1).to_broadcast([P, OHS, PAD, WIN]),
                                    K.window_lo[:, bass.ds(i * (P // DG) + b, OHS)].unsqueeze(2)
                                    .to_broadcast([P, OHS, PAD, WIN]), ALU.is_equal)
                            for w in range(WIN):
                                ins = v.tensor_scalar(
                                    col1[:, b % OHS * WIN + w], K.iota_col[:],
                                    K.window_col[:, bass.ds(i * (P // DG) + b, 1), w], None, ALU.is_equal)
                            ins.then_inc(hot, 1)
                with v.Else():
                    with v.Fori(0, NG // OHS) as i:
                        for s in range(OHS):
                            with v.Fori(0, STEPS) as c:
                                v.wait_ge(wide_used, i * (OHS * STEPS) + s * STEPS + c + 1)
                                base = K.group_base[:, bass.ds(i * OHS + s, 1)]
                                for w in range(SLOTS):
                                    v.tensor_scalar(lo_wide[:, w], K.iota_col[:, 0:PAD],
                                                    K.keys[:, bass.ds(c * SLOTS + w, 1), 0], None, ALU.is_equal)
                                    ins = v.tensor_scalar(col1[:, w], K.iota_col[:], base,
                                                          K.keys[:, bass.ds(c * SLOTS + w, 1), 1],
                                                          ALU.add, ALU.is_equal)
                                ins.then_inc(wide_hot, 1)

            @block.tensor
            def _(pe):
                pe.sem_inc(counted, OHS)
                wide = pe.value_load(K.wide[0:1, 0:1], min_val=0, max_val=1)
                with pe.If(wide < 1):
                    with pe.Fori(0, NB) as i:
                        for b in range(P // DG):
                            s = b % OHS
                            pe.wait_ge(hot, i * (P // DG) + b + 1)
                            pe.wait_ge(taken, i * (P // DG) + b + 1)
                            for w in range(WIN):
                                ins = pe.matmul(K.ps[0:P, s, 0:GW], lo1[:, b, 0:P, w], col1[:, s * WIN + w, 0:GW],
                                                start=(w == 0), stop=(w == WIN - 1))
                            ins.then_inc(counted, 1)
                with pe.Else():
                    pe.sem_inc(wide_used, 1)
                    with pe.Fori(0, NG // OHS) as i:
                        for s in range(OHS):
                            pe.wait_ge(taken, i * OHS + s + 1)
                            pe.matmul(K.ps[:, s, :], K.zeros[:, 0:128], K.zeros[:], start=True, stop=True)
                            with pe.Fori(0, STEPS) as c:
                                pe.wait_ge(wide_hot, i * (OHS * STEPS) + s * STEPS + c + 1)
                                for w in range(SLOTS):
                                    ins = pe.matmul(K.ps[0:P, s, 0:GW], lo_wide[:, w, 0:P], col1[:, w, 0:GW], start=False, stop=False,
                                                    skip_group_check=True)
                                ins.then_inc(wide_used, 1)
                            pe.matmul(K.ps[:, s, 0:128], K.zeros[:, 0:128], K.zeros[:, 0:128], start=False, stop=False,
                                      skip_group_check=True).then_inc(counted, 1)

            @block.scalar
            def _(act):
                act.sem_inc(taken, OHS)
                act.wait_ge(cleared, 1)
                with act.Fori(0, NB) as i:
                    act.wait_ge(stored, 64 * i + 64)
                    for b in range(P // DG):
                        act.wait_ge(counted, i * (P // DG) + b + 1 + OHS)
                        dst = stage[:, bass.ds(i % STAGES, 1), :, :, DG * b:DG * (b + 1)]
                        act.activation(dst.rearrange("p a r h d -> p (a r h) d"),
                                       K.ps[0:P, b % OHS, 0:GW].rearrange("p (x d) -> p x d", d=DG),
                                       ACT.Copy).then_inc(taken, 1)

            @block.sync
            def _(sp):
                sp.sem_inc(stored, 64 * STAGES)
                with sp.Fori(0, NB) as i:
                    sp.wait_ge(summed, 3 * i + 3)
                    sp.wait_ge(stored, 64 * i + 64 * STAGES)
                    for r in range(R):
                        sp.dma_start(K.counts[r, :, bass.ds(i, 1)].rearrange("p a h d -> p (a h d)"),
                                     stage[:, bass.ds(i % STAGES, 1), r].rearrange("p a h d -> p (a h d)")).then_inc(stored, 16)
                    sp.dma_start(K.counts_all[:, bass.ds(i, 1)].rearrange("p a h d -> p (a h d)"),
                                 total[:, bass.ds(i % 2, 1)].rearrange("p a h d -> p (a h d)")).then_inc(stored, 16)
                sp.wait_ge(stored, 64 * NB + 64 * STAGES)


@phase
def load_constants(nc, K, S):
    loaded, cleared, made = S("const_loaded"), S("const_cleared"), S("const_made")
    with nc.Block() as block:
        @block.sync
        def _(sp):
            sp.dma_start(K.x[:], K.x_in.rearrange("(b p) f -> p b f", p=P)).then_inc(loaded, 16)
            sp.dma_start(K.cols[:], K.cols_in).then_inc(loaded, 16)
            sp.dma_start(K.wext[:, :, 0:D], K.w_in.rearrange("k f j -> f k j")).then_inc(loaded, 16)
            sp.wait_ge(loaded, 48)

        @block.gpsimd
        def _(pool):
            pool.memset(K.ident[:], 0.0).then_inc(cleared, 1)
            pool.memset(K.ident16[:], 0.0).then_inc(cleared, 1)
            pool.memset(K.zeros[:], 0.0).then_inc(made, 1)
            pool.wait_ge(cleared, 2)
            for m in (K.ident, K.ident16):
                pool.affine_select(out=m[:], in_=m[:], compare_op=ALU.not_equal, fill=1.0, base=0,
                                   pattern=[[-1, 128]], channel_multiplier=1).then_inc(made, 1)


@phase
def score_weights(nc, K, S):
    with ExitStack() as ctx:
        sb = lambda name, shape, dt: ctx.enter_context(nc.sbuf_tensor(name, shape, dt))
        wt = sb("wt", [D, 6, D], F32)
        a = sb("a", [D, 6, 8], F32)
        cleared, filled, turned, moved, scored = (S("sw_" + n) for n in
                                                  ("cleared", "filled", "turned", "moved", "scored"))
        with nc.Block() as block:
            @block.vector
            def _(v):
                v.memset(a[:], 0.0).then_inc(cleared, 1)
                v.wait_ge(cleared, 1)
                for l in range(3):
                    v.tensor_copy(a[:, l, 0:2], K.cols[:, COL["a"] + 2 * l:COL["a"] + 2 * l + 2]).then_inc(filled, 1)
                for r in range(R):
                    for h in range(4):
                        rows = slice(32 * h, 32 * h + 32)
                        for side in range(2):
                            c = COL["att"] + 2 * r + side
                            v.tensor_copy(a[rows, 3 + r, 4 * side + h:4 * side + h + 1],
                                          K.cols[rows, c:c + 1]).then_inc(filled, 1)
                for k in range(6):
                    v.wait_ge(turned, k + 1)
                    v.tensor_copy(wt[:, k], K.ps[:, k, 0:D]).then_inc(moved, 1)
                v.wait_ge(scored, 6)
                for k in range(6):
                    v.tensor_copy(K.wext[:, k, D:D + 8], K.ps[:, k, D:D + 8])

            @block.tensor
            def _(pe):
                for k in range(6):
                    pe.transpose(K.ps[:, k, 0:D], K.wext[:, k, 0:D], K.ident[:]).then_inc(turned, 1)
                pe.wait_ge(filled, 27)
                for k in range(6):
                    pe.wait_ge(moved, k + 1)
                    pe.matmul(K.ps[:, k, D:D + 8], wt[:, k], a[:, k], start=True, stop=True).then_inc(scored, 1)


@phase
def turn_to_columns(nc, K, S, tag, src, dst, bias=None, add=None):
    turned = S(tag + "_turned")
    with nc.Block() as block:
        @block.tensor
        def _(pe):
            for k in range(NB):
                pe.transpose(K.ps[:, k // 4, (k % 4) * P:(k % 4 + 1) * P], src[0:P, k, 0:D],
                             K.ident[0:P, 0:P]).then_inc(turned, 1)

        def move(eng, bank):
            eng.wait_ge(turned, min(4 * bank + 4, NB))
            w = min(4 * P, N - 4 * P * bank)
            out, got = dst[:, 4 * P * bank:4 * P * bank + w], K.ps[:, bank, 0:w]
            return out, got

        @block.vector
        def _(v):
            for bank in range(0, 7, 2):
                out, got = move(v, bank)
                v.tensor_scalar(out, got, 1.0 if bias is None else bias, None, ALU.mult if bias is None else ALU.add)

        @block.scalar
        def _(act):
            for bank in range(1, 7, 2):
                out, got = move(act, bank)
                act.activation(out, got, ACT.Identity, bias=0.0 if bias is None else bias)


@phase
def turn_to_rows(nc, K, S, tag, src, dst, residual=None):
    turned = S(tag + "_turned")
    with nc.Block() as block:
        @block.tensor
        def _(pe):
            for k in range(NB):
                pe.transpose(K.ps[0:P, k // 4, (k % 4) * D:(k % 4 + 1) * D], src[:, k * P:(k + 1) * P],
                             K.ident[:]).then_inc(turned, 1)

        @block.vector
        def _(v):
            for bank in range(7):
                v.wait_ge(turned, min(4 * bank + 4, NB))
                n = min(4, NB - 4 * bank)
                out = dst[0:P, 4 * bank:4 * bank + n, 0:D]
                got = K.ps[0:P, bank, 0:n * D].rearrange("p (b f) -> p b f", f=D)
                if residual is None:
                    v.tensor_copy(out, got)
                else:
                    v.tensor_tensor(out, got, residual[0:P, 4 * bank:4 * bank + n, 0:D], ALU.add)


@phase
def batch_norm(nc, K, S, tag, z, out, g=None, b=None, relu=False):
    with ExitStack() as ctx:
        sb = lambda name, shape, dt: ctx.enter_context(nc.sbuf_tensor(tag + name, shape, dt))
        st = sb("st", [D, 7, 6], F32)
        mv = sb("mv", [D, 2], F32)
        sc = sb("sc", [D, 2], F32)
        own, rstd = S(tag + "_own"), S(tag + "_rstd")
        with nc.Block() as block:
            @block.vector
            def _(v):
                link = Chain(v, own)
                for m in range(7):
                    ins = v.bn_stats(st[:, m], z[:, 500 * m:min(500 * m + 500, N)])
                link(ins)
                link(v.bn_aggr(mv[:], st[:].rearrange("p a b -> p (a b)")))
                link(v.tensor_scalar(mv[:, 1:2], mv[:, 1:2], EPS, None, ALU.add))
                v.wait_ge(rstd, 1)
                link(v.reciprocal(sc[:, 0:1], mv[:, 1:2]))
                if g is not None:
                    link(v.tensor_tensor(sc[:, 0:1], sc[:, 0:1], g, ALU.mult))
                link(v.scalar_tensor_tensor(sc[:, 1:2], mv[:, 0:1], -1.0, sc[:, 0:1], ALU.mult, ALU.mult))
                if b is not None:
                    link(v.tensor_tensor(sc[:, 1:2], sc[:, 1:2], b, ALU.add))
                half = 1700
                link(v.tensor_scalar(out[:, 0:half], z[:, 0:half], sc[:, 0:1], sc[:, 1:2], ALU.mult, ALU.add))
                if relu:
                    v.tensor_scalar(out[:, 0:half], out[:, 0:half], 0.0, None, ALU.max)

            @block.scalar
            def _(act):
                act.wait_ge(own, 3)
                act.activation(mv[:, 1:2], mv[:, 1:2], ACT.Sqrt).then_inc(rstd, 1)
                act.wait_ge(own, 5 + (g is not None) + (b is not None))
                act.activation(out[:, 1700:N], z[:, 1700:N], ACT.Relu if relu else ACT.Identity,
                               bias=sc[:, 1:2], scale=sc[:, 0:1])


@phase
def layer_norm(nc, K, S, tag, x):
    with ExitStack() as ctx:
        sb = lambda name, shape, dt: ctx.enter_context(nc.sbuf_tensor(tag + name, shape, dt))
        st = sb("st", [P, NB, 6], F32)
        mv = sb("mv", [P, NB, 2], F32)
        own, rstd = S(tag + "_own"), S(tag + "_rstd")
        with nc.Block() as block:
            @block.vector
            def _(v):
                link = Chain(v, own)
                for k in range(NB):
                    ins = v.bn_stats(st[:, k], x[:, k])
                link(ins)
                for k in range(NB):
                    ins = v.bn_aggr(mv[:, k], st[:, k])
                link(ins)
                link(v.tensor_scalar(mv[:, :, 1], mv[:, :, 1], EPS, None, ALU.add))
                v.wait_ge(rstd, 1)
                link(v.reciprocal(mv[:, :, 1], mv[:, :, 1]))
                for k in range(NB):
                    v.tensor_scalar(x[:, k], x[:, k], mv[:, k, 0:1], mv[:, k, 1:2], ALU.subtract, ALU.mult)

            @block.scalar
            def _(act):
                act.wait_ge(own, 3)
                act.activation(mv[:, :, 1], mv[:, :, 1], ACT.Sqrt).then_inc(rstd, 1)


@phase
def scores(nc, K, S, tag, k, H, F, T):
    FH = D // H
    with ExitStack() as ctx:
        sb = lambda name, shape, dt: ctx.enter_context(nc.sbuf_tensor(tag + name, shape, dt))
        hx = sb("hx", [P, NB, D + 8], F32)
        val = sb("val", [P, NB, H, 2, F], F32)
        adr = sb("adr", [H, NB, PAD], F32)
        gmax = sb("gmax", [P, 2, H + 1], F32)
        asg = sb("asg", [P, NB, H], F32)
        u = sb("u", [P, 4, NB, H], F32)
        t = sb("t", [P, NB, H], F32)
        tm = sb("tm", [P, NB, H, 2], F32)
        sv = sb("sv", [P, 2], F32)
        (proj, projv, adp, adt, adz, adst, own, mx, mxr, asr, ur, tr, part, rest, vals_ready) = (
            S(tag + "_" + n) for n in ("proj", "projv", "adp", "adt", "adz", "adst", "own", "mx", "mxr", "asr",
                                       "ur", "tr", "part", "rest", "vals"))
        W = D + 2 * H
        parts = T.mv[:, :, 0:4 * H * F].rearrange("p b (h c f) -> p b h c f", h=H, c=2)
        with nc.Block() as block:
            @block.tensor
            def _(pe):
                for m in range(7):
                    w = min(500, N - 500 * m)
                    pe.matmul(K.ps[0:H, m, 0:w], K.wext[:, k, D + H:D + 2 * H], K.zT[:, 500 * m:500 * m + w],
                              start=True, stop=True).then_inc(adp, 1)
                for b in range(NB):
                    if b < 7:
                        pe.wait_ge(adt, b + 1)
                    else:
                        pe.wait_ge(projv, b - 6)
                    pe.matmul(K.ps[0:P, b % 7, 0:W], K.zT[:, P * b:P * b + P], K.wext[:, k, 0:W],
                              start=True, stop=True).then_inc(proj, 1)

            @block.scalar
            def _(act):
                act.wait_ge(adz, 1)
                for m in range(7):
                    n = min(4, NB - 4 * m)
                    act.wait_ge(adp, m + 1)
                    act.activation(adr[:, 4 * m:4 * m + n, 0:P],
                                   K.ps[0:H, m, 0:n * P].rearrange("p (b c) -> p b c", c=P), ACT.Copy).then_inc(adt, 1)
                act.wait_ge(asr, 1)
                act.activation(u[:, 0], asg[:], ACT.Exp).then_inc(ur, 1)
                act.activation(u[:, 1], asg[:], ACT.Exp, scale=0.2).then_inc(ur, 1)
                act.wait_ge(tr, 2)
                act.activation(T.c[:], tm[:], ACT.Exp).then_inc(ur, 1)
                for p in range(2):
                    for q in range(5):
                        act.wait_ge(rest if p else vals_ready, q + 1)
                        act.activation(parts[:, 5 * q:5 * q + 5, :, p],
                                       val[:, 5 * q:5 * q + 5].rearrange("p b h a f -> p b h (a f)"),
                                       ACT.Copy).then_inc(part, 1)

            @block.gpsimd
            def _(pool):
                pool.memset(adr[:], 0.0).then_inc(adz, 1)
                pool.wait_ge(mx, 2)
                pool.partition_all_reduce(gmax[:, 1], gmax[:, 0], P, bass.bass_isa.ReduceOp.max).then_inc(mxr, 1)

            @block.sync
            def _(sp):
                sp.wait_ge(adt, 7)
                sp.dma_start(K.ad_rows[0:H], adr[:]).then_inc(adst, 16)
                sp.wait_ge(adst, 16)

            @block.vector
            def _(v):
                link = Chain(v, own)
                for b in range(NB):
                    v.wait_ge(proj, b + 1)
                    v.tensor_copy(hx[:, b, 0:W], K.ps[0:P, b % 7, 0:W]).then_inc(projv, 1)
                v.wait_ge(projv, NB)
                a_s, a_d = hx[:, :, D:D + H], hx[:, :, D + H:D + 2 * H]
                v.tensor_reduce(gmax[:, 0, 0:H], a_s.rearrange("p b h -> p h b"), AX.X, ALU.max).then_inc(mx, 1)
                v.tensor_reduce(gmax[:, 0, H:H + 1], hx[:, :, 0:D], AX.XY, ALU.max,
                                apply_absolute_value=True).then_inc(mx, 1)
                link(v.tensor_scalar(T.thr[:, 0], a_s, -1.0, None, ALU.mult))
                link(v.tensor_scalar(T.thr[:, 1], a_s, -STEEP, None, ALU.mult))
                v.wait_ge(mxr, 1)
                G = gmax[:, 1, 0:H].unsqueeze(1).to_broadcast([P, NB, H])
                v.tensor_tensor(asg[:], a_s, G, ALU.subtract).then_inc(asr, 1)
                link(v.tensor_tensor(t[:], a_d, G, ALU.add))
                v.tensor_scalar(tm[:, :, :, 1], t[:], 0.8, 0.0, ALU.mult, ALU.min).then_inc(tr, 1)
                v.tensor_scalar(tm[:, :, :, 0], t[:], -0.8, 0.0, ALU.mult, ALU.min).then_inc(tr, 1)
                link(v.tensor_scalar(T.top[:], gmax[:, 1, H:H + 1], TINY, None, ALU.max))
                link(v.reciprocal(sv[:, 0:1], T.top[:]))
                link(v.tensor_scalar(sv[:, 1:2], sv[:, 0:1], TOP, None, ALU.mult))
                v.wait_ge(ur, 2)
                link(v.tensor_scalar(u[:, 2:4], u[:, 0:2], sv[:, 1:2], None, ALU.mult))
                if F > FH + 1:
                    link(v.memset(val[:, :, :, 0, F - 1:F], 1.0))
                    link(v.memset(val[:, :, :, 1, F - 1:F], -1.0))
                link(v.tensor_scalar(val[:, :, :, 0, FH:FH + 1], u[:, 1].unsqueeze(3), TOP, None, ALU.mult))
                link(v.tensor_scalar(val[:, :, :, 1, FH:FH + 1], u[:, 0].unsqueeze(3), -TOP, None, ALU.mult))
                for q in range(5):
                    s = slice(5 * q, 5 * q + 5)
                    h4 = hx[:, s, 0:D].rearrange("p b (h f) -> p b h f", h=H)
                    ub = lambda i: u[:, i, s].unsqueeze(3).to_broadcast([P, 5, H, FH])
                    v.tensor_tensor(val[:, s, :, 0, 0:FH], h4, ub(3), ALU.mult).then_inc(own, 1)
                    v.scalar_tensor_tensor(val[:, s, :, 1, 0:FH], h4, -1.0, ub(2), ALU.mult,
                                           ALU.mult).then_inc(vals_ready, 1)
                for q in range(5):
                    s = slice(5 * q, 5 * q + 5)
                    v.wait_ge(part, q + 1)
                    vv = val[:, s].rearrange("p b h a f -> p b h (a f)")
                    v.tensor_tensor(vv, vv, parts[:, s, :, 0], ALU.subtract).then_inc(rest, 1)
                for c in range(2):
                    v.wait_ge(part, 5 * c + 5)
                    v.tensor_scalar(T.mv[:, :, (4 + c) * H * F:(5 + c) * H * F].rearrange("p b (h f) -> p b h f", h=H),
                                    parts[:, :, :, c].rearrange("p b h (a f) -> p b h a f", a=2)[:, :, :, 1],
                                    -1.0, None, ALU.mult)


@phase
def attention(nc, K, S, tag, counts, H, F, T, degree=False):
    HF = H * F
    by_act = lambda j: list(range(H - (2 + (j + 1) % 2), H)) if H > 1 else []
    masks = [sum(len(by_act(i)) for i in range(j)) for j in range(6)]
    with ExitStack() as ctx:
        sb = lambda name, shape, dt: ctx.enter_context(nc.sbuf_tensor(tag + name, shape, dt))
        ct = sb("ct", [P, 5, 5, 5, PAD], F16)
        ad = sb("ad", [P, 2, H, 5 * PAD], F32)
        sel = sb("sel", [P, 5, H, 5, PAD], F16)
        msk = sb("msk", [P, 5, 3 if H > 1 else 1, 5, PAD], F16)
        tmp = sb("tmp", [P, 2 * HF], F32)
        landed = [S(f"{tag}_landed{c}") for c in range(5)]
        turns = S(tag + "_turns")
        ad_landed, masked, used, drained, own, mready = (
            S(tag + "_" + n) for n in ("adl", "masked", "used", "drained", "own", "mready"))
        with nc.Block() as block:
            @block.sync
            def _(sp):
                sp.sem_inc(ad_landed, 16)
                with sp.Fori(0, 5) as g:
                    slot, first = sp.snap(g % 2), sp.snap(5 * g)
                    made, had = sp.snap(25 * g + 20), sp.snap(16 * g + 16)
                    ready_first(sp, slot, first, made, had)
                    sp.wait_ge(used, made)
                    sp.wait_ge(ad_landed, had)
                    sp.dma_start(ad[:, bass.ds(slot, 1)].rearrange("p a h d -> p (a h) d"),
                                 K.ad_rows[0:H, bass.ds(first, 5)].rearrange("h b d -> h (b d)").partition_broadcast(P)
                                 ).then_inc(ad_landed, 16)
                    for c in range(5):
                        sp.wait_ge(used, 25 * g + 5 * c + 5)
                        sp.dma_start(ct[:, c], counts[:, bass.ds(first, 5), 5 * c:5 * c + 5]).then_inc(landed[c], 16)

            @block.vector
            def _(v):
                v.sem_inc(drained, 5)
                with v.Fori(0, 5) as g:
                    for c in range(5):
                        v.wait_ge(ad_landed, 16 * g + 32)
                        v.wait_ge(landed[c], 16 * g + 16)
                        for j in range(5):
                            n = len(by_act(j))
                            v.wait_ge(used, 25 * g + 5 * c + j + 21)
                            for h in range(H - n):
                                ins = v.scalar_tensor_tensor(
                                    sel[:, j, h], ad[:, bass.ds(g % 2, 1), h].rearrange("p a (b d) -> p (a b) d", d=PAD),
                                    T.thr[:, 0, 5 * c + j, h:h + 1], ct[:, c, :, j], ALU.is_lt, ALU.mult)
                            if n:
                                v.wait_ge(mready, masks[5] * (5 * g + c) + masks[j + 1])
                                ins = v.tensor_tensor(sel[:, j, H - n:H], msk[:, j, 0:n],
                                                      ct[:, c, :, j].unsqueeze(1).to_broadcast([P, n, 5, PAD]), ALU.mult)
                            ins.then_inc(masked, 1)
                    v.wait_ge(used, 25 * g + 50)
                    for b in range(5):
                        t4 = tmp[:].rearrange("p (h a f) -> p h a f", h=H, a=2)
                        acc = K.ps[0:P, b, 0:2 * HF].rearrange("p (x f) -> p x f", f=F)
                        cb = T.c[:, bass.ds(5 * g + b, 1)].rearrange("p b h a -> p (b h a)").unsqueeze(2) \
                            .to_broadcast([P, 2 * H, F])
                        if degree:
                            v.tensor_copy(K.dinv[:, bass.ds(5 * g + b, 1)], acc[:, 0, F - 1:F])
                            v.tensor_copy(K.dinv2[:, bass.ds(5 * g + b, 1)], acc[:, 1, F - 1:F]).then_inc(own, 1)
                        v.tensor_tensor(tmp[:].rearrange("p (x f) -> p x f", f=F), acc, cb, ALU.mult).then_inc(drained, 1)
                        v.wait_ge(drained, 5 * g + b + 6)
                        v.tensor_tensor(T.num[:, bass.ds(5 * g + b, 1)].rearrange("p b h f -> p (b h) f"),
                                        t4[:, :, 0], t4[:, :, 1], ALU.add).then_inc(own, 1)
                        v.wait_ge(own, (1 + degree) * (5 * g + b + 1))

            @block.scalar
            def _(act):
                if H > 1:
                    with act.Fori(0, 5) as g:
                        for c in range(5):
                            act.wait_ge(ad_landed, 16 * g + 32)
                            for j in range(5):
                                act.wait_ge(used, 25 * g + 5 * c + j + 21)
                                act.sem_inc(turns, 1)
                                for n, h in enumerate(by_act(j)):
                                    act.activation(msk[:, j, n], ad[:, bass.ds(g % 2, 1), h]
                                                   .rearrange("p a (b d) -> p (a b) d", d=PAD),
                                                   ACT.Sigmoid, bias=T.thr[:, 1, 5 * c + j, h:h + 1],
                                                   scale=-STEEP).then_inc(mready, 1)

            @block.tensor
            def _(pe):
                pe.sem_inc(used, 25)
                with pe.Fori(0, 5) as g:
                    for b in range(5):
                        pe.wait_ge(drained, 5 * g + b + 1)
                        pe.matmul(K.ps[:, b, :], K.zeros[:, 0:128], K.zeros[:], start=True, stop=True)
                    for c in range(5):
                        pe.wait_ge(landed[c], 16 * g + 16)
                        for j in range(5):
                            pe.wait_ge(masked, 25 * g + 5 * c + j + 1)
                            vs = T.mv[:, 5 * c + j]
                            for b in range(5):
                                for h in range(H):
                                    for p in range(2):
                                        pe.matmul(K.ps[:, b, 2 * h * F:2 * (h + 1) * F], sel[:, j, h, b],
                                                  vs[:, (h * 2 + p) * 2 * F:(h * 2 + p + 1) * 2 * F],
                                                  start=False, stop=False, skip_group_check=True)
                                for p in range(2):
                                    ins = pe.matmul(K.ps[:, b, 0:2 * HF].rearrange("p (h a f) -> p h a f", h=H, a=2)[:, :, 1],
                                                    ct[:, c, b, j],
                                                    vs[:, (4 + p) * HF:(5 + p) * HF].rearrange("p (h f) -> p h f", h=H),
                                                    start=False, stop=False, skip_group_check=True)
                            ins.then_inc(used, 1)


@phase
def gat_normalise(nc, K, S, tag, num, top, z, degree):
    with ExitStack() as ctx:
        rden = ctx.enter_context(nc.sbuf_tensor(tag + "rden", [P, NB], F32))
        own, root = S(tag + "_own"), S(tag + "_root")
        with nc.Block() as block:
            @block.vector
            def _(v):
                link = Chain(v, own)
                if degree:
                    link(v.tensor_tensor(K.dinv[:], K.dinv[:], K.dinv2[:], ALU.add))
                    link(v.tensor_scalar(K.dinv[:], K.dinv[:], 1.0, None, ALU.max))
                link(v.reciprocal(rden[:], num[:, :, 0, D]))
                link(v.tensor_scalar(rden[:], rden[:], top[:], None, ALU.mult))
                v.tensor_tensor(z[0:P], num[:, :, 0, 0:D], rden[:].unsqueeze(2).to_broadcast([P, NB, D]), ALU.mult)
                if degree:
                    v.wait_ge(root, 1)
                    v.reciprocal(K.dinv[:], K.dinv[:])

            @block.scalar
            def _(act):
                if degree:
                    act.wait_ge(own, 2)
                    act.activation(K.dinv[:], K.dinv[:], ACT.Sqrt).then_inc(root, 1)


@phase
def relation_sum(nc, K, S, tag, num, top, r):
    with ExitStack() as ctx:
        sb = lambda name, shape, dt: ctx.enter_context(nc.sbuf_tensor(tag + name, shape, dt))
        rden = sb("rden", [P, NB, 4], F32)
        own = S(tag + "_own")
        with nc.Block() as block:
            @block.vector
            def _(v):
                link = Chain(v, own)
                wr = K.relw[0:P, 3 + r:4 + r]
                link(v.reciprocal(rden[:], num[:, :, :, 32]))
                link(v.tensor_scalar(rden[:], rden[:], wr, top[:], ALU.mult, ALU.mult))
                link(v.tensor_tensor(num[:, :, :, 0:32], num[:, :, :, 0:32],
                                     rden[:].unsqueeze(3).to_broadcast([P, NB, 4, 32]), ALU.mult))
                x4 = K.x[:].rearrange("p b (h f) -> p b h f", h=4)
                link(v.tensor_tensor(x4, x4, num[:, :, :, 0:32], ALU.add))
                v.scalar_tensor_tensor(K.x[:], K.rows[0:P, r * D:(r + 1) * D].unsqueeze(1).to_broadcast([P, NB, D]),
                                       wr, K.x[:], ALU.mult, ALU.add)


@phase
def relation_weights(nc, K, S):
    own, done = S("relw_own"), S("relw_exp")
    with ExitStack() as ctx:
        m = ctx.enter_context(nc.sbuf_tensor("relm", [128, 2], F32))
        with nc.Block() as block:
            @block.vector
            def _(v):
                link = Chain(v, own)
                link(v.tensor_copy(K.relw[:, 0:3], K.rows[:, ROW_RELW:ROW_RELW + 3]))
                link(v.tensor_reduce(m[:, 0:1], K.relw[:, 0:3], AX.X, ALU.max))
                link(v.tensor_scalar(K.relw[:, 0:3], K.relw[:, 0:3], m[:, 0:1], None, ALU.subtract))
                v.wait_ge(done, 1)
                link(v.tensor_reduce(m[:, 0:1], K.relw[:, 3:6], AX.X, ALU.add))
                link(v.reciprocal(m[:, 1:2], m[:, 0:1]))
                v.tensor_scalar(K.relw[:, 3:6], K.relw[:, 3:6], m[:, 1:2], None, ALU.mult)

            @block.scalar
            def _(act):
                act.wait_ge(own, 3)
                act.activation(K.relw[:, 3:6], K.relw[:, 0:3], ACT.Exp).then_inc(done, 1)


@phase
def split_parts(nc, K, S, tag, val, W, parts, scale=None):
    ready, part, rest = (S(tag + "_" + n) for n in ("ready", "part", "rest"))
    with nc.Block() as block:
        @block.vector
        def _(v):
            for q in range(5):
                s = slice(5 * q, 5 * q + 5)
                if scale is not None:
                    v.tensor_tensor(val[:, s], val[:, s], scale[:, s].unsqueeze(2).to_broadcast([P, 5, W]),
                                    ALU.mult).then_inc(ready, 1)
                else:
                    v.sem_inc(ready, 1)
            for p in range(2):
                for q in range(5):
                    s = slice(5 * q, 5 * q + 5)
                    v.wait_ge(part, 5 * p + q + 1)
                    if p == 0:
                        v.wait_ge(ready, q + 1)
                    else:
                        v.wait_ge(rest, q + 1)
                    v.tensor_tensor(val[:, s], val[:, s], parts[:, s, p], ALU.subtract).then_inc(rest, 1)

        @block.scalar
        def _(act):
            for p in range(3):
                for q in range(5):
                    act.wait_ge(ready if p == 0 else rest, q + 1 if p == 0 else 5 * (p - 1) + q + 1)
                    act.activation(parts[:, 5 * q:5 * q + 5, p], val[:, 5 * q:5 * q + 5], ACT.Copy).then_inc(part, 1)


@phase
def gather_in(nc, K, S, tag, parts, dst):
    with ExitStack() as ctx:
        ct = ctx.enter_context(nc.sbuf_tensor(tag + "ct", [P, 5, 5, 5, PAD], F16))
        landed = [S(f"{tag}_landed{c}") for c in range(5)]
        used, drained = S(tag + "_used"), S(tag + "_drained")
        with nc.Block() as block:
            @block.sync
            def _(sp):
                with sp.Fori(0, 5) as g:
                    for c in range(5):
                        sp.wait_ge(used, 5 * g + c + 1)
                        sp.dma_start(ct[:, c], K.counts_all[:, bass.ds(5 * g, 5), 5 * c:5 * c + 5]).then_inc(landed[c], 16)

            @block.tensor
            def _(pe):
                pe.sem_inc(used, 5)
                with pe.Fori(0, 5) as g:
                    pe.wait_ge(drained, 5 * g + 5)
                    for c in range(5):
                        pe.wait_ge(landed[c], 16 * g + 16)
                        for j in range(5):
                            hi = 5 * c + j
                            for b in range(5):
                                for p in range(3):
                                    ins = pe.matmul(K.ps[:, b, 0:D], ct[:, c, b, j], parts[:, hi, p],
                                                    start=(hi == 0 and p == 0), stop=(hi == NB - 1 and p == 2))
                        ins.then_inc(used, 1)

            @block.vector
            def _(v):
                v.sem_inc(drained, 5)
                with v.Fori(0, 5) as g:
                    v.wait_ge(used, 5 * g + 10)
                    for b in range(5):
                        v.tensor_scalar(dst[:, bass.ds(5 * g + b, 1)].rearrange("p a f -> p (a f)"), K.ps[0:P, b, 0:D],
                                        K.dinv[:, bass.ds(5 * g + b, 1)], None, ALU.mult).then_inc(drained, 1)


@phase
def gather_out(nc, K, S, tag, parts, W, dst):
    with ExitStack() as ctx:
        sb = lambda name, shape, dt: ctx.enter_context(nc.sbuf_tensor(tag + name, shape, dt))
        ct = sb("ct", [P, 5, 5, 5, PAD], F16)
        cT = sb("cT", [128, 5, 5, PAD], F16)
        landed = [S(f"{tag}_landed{c}") for c in range(5)]
        turned, moved_v, moved_a, used, drained, cleared = (S(tag + "_" + n) for n in
                                                ("turned", "movedv", "moveda", "used", "drained", "cleared"))
        T16 = K.ps[:].bitcast(F16)
        with nc.Block() as block:
            @block.sync
            def _(sp):
                with sp.Fori(0, 5) as c:
                    for g in range(5):
                        sp.wait_ge(turned, 25 * c + 5 * g + 5)
                        sp.dma_start(ct[:, g], K.counts_all[:, 5 * g:5 * g + 5, bass.ds(5 * c, 5)]).then_inc(landed[g], 16)

            def moved(eng, c, n):
                eng.wait_ge(moved_a if n % 2 else moved_v, (12 * c if n % 2 else 13 * c) + n // 2 + (13 if n % 2 else 14))

            @block.tensor
            def _(pe):
                pe.wait_ge(cleared, 1)
                pe.sem_inc(used, 5)
                pe.sem_inc(turned, 25)
                with pe.Fori(0, 5) as c:
                    for n in range(26):
                        if n < 25:
                            g, j = n // 5, n % 5
                            if j == 0:
                                pe.wait_ge(landed[g], 16 * c + 16)
                            if n >= 3:
                                moved(pe, c, n - 3)
                            else:
                                pe.wait_ge(moved_v, 13 * c + 13)
                                pe.wait_ge(moved_a, 12 * c + 12)
                            for b in range(5):
                                ins = pe.transpose(T16[:, 5 + n % 3, b * PAD:b * PAD + P], ct[:, g, b, j],
                                                   K.ident16[0:P, 0:P])
                            ins.then_inc(turned, 1)
                        if n >= 1:
                            m = n - 1
                            g, j = m // 5, m % 5
                            moved(pe, c, m)
                            if m == 0:
                                pe.wait_ge(drained, 5 * c + 5)
                            for b in range(5):
                                for p in range(3):
                                    ins = pe.matmul(K.ps[:, j, 0:W], cT[0:P, m % 5, b], parts[:, 5 * g + b, p],
                                                    start=(g == 0 and b == 0 and p == 0),
                                                    stop=(g == 4 and b == 4 and p == 2))
                            ins.then_inc(used, 1)

            def move(eng, c, n, copy, sem):
                eng.wait_ge(turned, 25 * c + n + 26)
                eng.wait_ge(used, 25 * c + n + 1)
                out = cT[:, n % 5, :, 0:P]
                got = T16[:, 5 + n % 3, 0:5 * PAD].rearrange("p (b s) -> p b s", s=PAD)[:, :, 0:P]
                copy(out, got).then_inc(sem, 1)

            @block.vector
            def _(v):
                v.memset(cT[:], 0.0).then_inc(cleared, 1)
                v.wait_ge(cleared, 1)
                v.sem_inc(moved_v, 13)
                v.sem_inc(drained, 5)
                with v.Fori(0, 5) as c:
                    for n in range(0, 25, 2):
                        move(v, c, n, v.tensor_copy, moved_v)
                    v.wait_ge(used, 25 * c + 30)
                    for j in range(5):
                        v.tensor_copy(dst[:, bass.ds(5 * c + j, 1)].rearrange("p a f -> p (a f)"),
                                      K.ps[0:P, j, 0:W]).then_inc(drained, 1)

            @block.scalar
            def _(act):
                act.wait_ge(cleared, 1)
                act.sem_inc(moved_a, 12)
                with act.Fori(0, 5) as c:
                    for n in range(1, 25, 2):
                        move(act, c, n, lambda o, i: act.activation(o, i, ACT.Copy), moved_a)


@phase
def linear_columns(nc, K, S, tag, outs):
    done, taken_a, taken_v = S(tag + "_done"), S(tag + "_takena"), S(tag + "_takenv")
    steps = [(o, m) for o in outs for m in range(7)]
    on_act = [o[3] is not None or (o[4] is None and m % 2 == 1) for o, m in steps]
    with nc.Block() as block:
        @block.tensor
        def _(pe):
            for n, ((dst, terms, bias, func, add), m) in enumerate(steps):
                if n >= 8:
                    a = on_act[n - 8]
                    pe.wait_ge(taken_a if a else taken_v, sum(x == a for x in on_act[:n - 7]))
                w = min(500, N - 500 * m)
                for i, (wt, src) in enumerate(terms):
                    ins = pe.matmul(K.ps[:, n % 8, 0:w], wt, src[:, 500 * m:500 * m + w], start=(i == 0),
                                    stop=(i == len(terms) - 1))
                ins.then_inc(done, 1)

        @block.scalar
        def _(act):
            for n, ((dst, terms, bias, func, add), m) in enumerate(steps):
                if on_act[n]:
                    w = min(500, N - 500 * m)
                    act.wait_ge(done, n + 1)
                    act.activation(dst[:, 500 * m:500 * m + w], K.ps[:, n % 8, 0:w], func or ACT.Identity,
                                   bias=bias).then_inc(taken_a, 1)

        @block.vector
        def _(v):
            for n, ((dst, terms, bias, func, add), m) in enumerate(steps):
                if not on_act[n]:
                    w = min(500, N - 500 * m)
                    s = slice(500 * m, 500 * m + w)
                    v.wait_ge(done, n + 1)
                    if add is None:
                        v.tensor_scalar(dst[:, s], K.ps[:, n % 8, 0:w], bias, None, ALU.add).then_inc(taken_v, 1)
                    else:
                        v.scalar_tensor_tensor(dst[:, s], K.ps[:, n % 8, 0:w], bias, add[:, s], ALU.add,
                                               ALU.add).then_inc(taken_v, 1)


@phase
def linear_rows(nc, K, S, tag, terms, W, dst, bias=None):
    done, taken = S(tag + "_done"), S(tag + "_taken")
    with nc.Block() as block:
        @block.tensor
        def _(pe):
            for b in range(NB):
                if b >= 8:
                    pe.wait_ge(taken, b - 7)
                for i, (src, wt) in enumerate(terms):
                    ins = pe.matmul(K.ps[0:P, b % 8, 0:W], src[:, P * b:P * b + P], wt, start=(i == 0),
                                    stop=(i == len(terms) - 1))
                ins.then_inc(done, 1)

        @block.vector
        def _(v):
            for b in range(NB):
                v.wait_ge(done, b + 1)
                if bias is None:
                    v.tensor_copy(dst[:, b, 0:W], K.ps[0:P, b % 8, 0:W]).then_inc(taken, 1)
                else:
                    v.tensor_tensor(dst[:, b, 0:W], K.ps[0:P, b % 8, 0:W], bias, ALU.add).then_inc(taken, 1)


@phase
def load(nc, K, S, tag, pairs):
    landed = S(tag + "_landed")
    with nc.Block() as block:
        @block.sync
        def _(sp):
            for dst, src in pairs:
                sp.dma_start(dst, src).then_inc(landed, 16)
            sp.wait_ge(landed, 16 * len(pairs))


@phase
def head_attention(nc, K, S, tag, qkv, ks, att):
    H, DH = 8, 16
    with ExitStack() as ctx:
        sb = lambda name, shape, dt: ctx.enter_context(nc.sbuf_tensor(tag + name, shape, dt))
        rc = sb("rc", [P, NB], F32)
        pr = sb("pr", [P, 4, H, H, DH], F32)
        s = sb("s", [P, NB, H, H], F32)
        m = sb("m", [P, NB, H], F32)
        own, mult, red, pown, edone = (S(tag + "_" + n) for n in ("own", "mult", "red", "pown", "exp"))
        q = qkv[:, :, 0:D].rearrange("p b (h d) -> p b h d", h=H)
        k = ks[:, :, 0:D].rearrange("p b (g d) -> p b g d", g=H)
        vT = qkv[:, :, 2 * D:3 * D].rearrange("p b (g d) -> p b d g", g=H)
        with nc.Block() as block:
            @block.vector
            def _(v):
                link = Chain(v, own)
                link(v.tensor_scalar(rc[:], ks[:, :, D], -1.0, 1.0, ALU.add, ALU.max))
                link(v.reciprocal(rc[:], rc[:]))
                link(v.tensor_tensor(ks[:, :, 0:D], ks[:, :, 0:D], qkv[:, :, D:2 * D], ALU.subtract))
                link(v.tensor_tensor(ks[:, :, 0:D], ks[:, :, 0:D], rc[:].unsqueeze(2).to_broadcast([P, NB, D]), ALU.mult))
                for b in range(NB):
                    if b >= 2:
                        v.wait_ge(red, b - 1)
                    v.tensor_tensor(pr[:, b % 2], q[:, b].unsqueeze(2).to_broadcast([P, H, H, DH]),
                                    k[:, b].unsqueeze(1).to_broadcast([P, H, H, DH]), ALU.mult).then_inc(mult, 1)
                    v.wait_ge(mult, b + 1)
                    v.tensor_reduce(s[:, b], pr[:, b % 2], AX.X, ALU.add).then_inc(red, 1)
                v.wait_ge(red, NB)
                link(v.tensor_reduce(m[:], s[:], AX.X, ALU.max))
                link(v.tensor_tensor(s[:], s[:], m[:].unsqueeze(3).to_broadcast([P, NB, H, H]), ALU.subtract))
                v.wait_ge(edone, 1)
                link(v.tensor_reduce(m[:], s[:], AX.X, ALU.add))
                link(v.reciprocal(m[:], m[:]))
                link(v.tensor_tensor(s[:], s[:], m[:].unsqueeze(3).to_broadcast([P, NB, H, H]), ALU.mult))
                for b in range(NB):
                    v.wait_ge(red, NB + max(b - 1, 0))
                    prb = pr[:, b % 2].rearrange("p h g d -> p (h g d)").rearrange("p (h d g) -> p h d g", h=H, d=DH)
                    v.tensor_tensor(prb, s[:, b].unsqueeze(2).to_broadcast([P, H, DH, H]),
                                    vT[:, b].unsqueeze(1).to_broadcast([P, H, DH, H]), ALU.mult).then_inc(mult, 1)
                    v.wait_ge(mult, NB + b + 1)
                    v.tensor_reduce(att[:, b].rearrange("p (h d) -> p h d", h=H), prb, AX.X, ALU.add).then_inc(red, 1)

            @block.scalar
            def _(act):
                act.wait_ge(own, 6)
                act.activation(s[:], s[:], ACT.Exp).then_inc(edone, 1)


STEEP = 1.0e8
TOP = 16384.0
TINY = 1e-30
COLS = [("a", 6), ("att", 6), ("b0", 3), ("g_in", 1), ("be_in", 1), ("b1", 2), ("g1", 2), ("be1", 2), ("b2", 1),
        ("g2", 1), ("be2", 1), ("bo", 1), ("fb1", 4), ("fb2", 1), ("fg1", 1), ("fbe1", 1), ("fg2", 1), ("fbe2", 1)]
COL, NCOL = {}, 0
for _name, _n in COLS:
    COL[_name] = NCOL
    NCOL += _n
ROW_RELW = 3 * D
ROW_QKV = 3 * D + 3
NROW = ROW_QKV + 3 * D


class Names:
    pass


def build(nc, args, out):
    K, T = Names(), Names()
    K.src_in, K.dst_in, K.typ_in = (args[n] for n in ("src", "dst", "typ"))
    K.x_in, K.w_in, K.cols_in, K.rows_in = (args[n] for n in ("x_in", "w_in", "cols_in", "rows_in"))
    K.w1_in, K.w2_in, K.wq_in, K.wk_in = (args[n] for n in ("w1_in", "w2_in", "wq_in", "wk_in"))
    K.wv_in, K.wo_in, K.fw1_in, K.fw2_in = (args[n] for n in ("wv_in", "wo_in", "fw1_in", "fw2_in"))
    with ExitStack() as ctx:
        sb = lambda name, shape, dt: ctx.enter_context(nc.sbuf_tensor(name, shape, dt))
        S = lambda name: ctx.enter_context(nc.semaphore(name))
        col = lambda name, i=0: K.cols[:, COL[name] + i:COL[name] + i + 1]
        K.ps = ctx.enter_context(nc.psum_tensor("ps", [128, 8, 512], F32))
        K.counts = nc.dram_tensor("counts", [R, P, NB, NB, PAD], F16)
        K.counts_all = nc.dram_tensor("counts_all", [P, NB, NB, PAD], F16)
        K.sub_range = nc.dram_tensor("sub_range", [2, NSUB], F16)
        K.edge_keys = nc.dram_tensor("edge_keys", [2 * E], F32)
        K.windows = nc.dram_tensor("windows", [NSUB, 2 * CH], F32)
        K.ad_rows = nc.dram_tensor("ad_rows", [4, NB, PAD], F32)
        K.x = sb("x", [P, NB, D], F32)
        K.zT = sb("zT", [D, N], F32)
        K.wext = sb("wext", [D, 6, D + 8], F32)
        K.cols = sb("cols", [D, NCOL], F32)
        K.rows = sb("rows", [128, NROW], F32)
        K.relw = sb("relw", [128, 6], F32)
        K.ident = sb("ident", [128, 128], F32)
        K.ident16 = sb("ident16", [128, 128], F16)
        K.zeros = sb("zeros", [P, 512], BF16)
        K.dinv = sb("dinv", [P, NB], F32)
        K.dinv2 = sb("dinv2", [P, NB], F32)
        with nc.cleanup_on_exit():
            load_constants(nc, K)
            load(nc, K, "rows", [(K.rows[:], K.rows_in.partition_broadcast(128))])
            score_weights(nc, K)
            relation_weights(nc, K)
            with ExitStack() as c2:
                sb2 = lambda name, shape, dt: c2.enter_context(nc.sbuf_tensor(name, shape, dt))
                K.keys = sb2("keys", [P, NCH, 2], F32)
                K.group_base = sb2("group_base", [P, NG], F32)
                K.iota_col = sb2("iota_col", [P, GE], F16)
                K.iota_pair = sb2("iota_pair", [P, PAD, WIN], F16)
                K.window_lo = sb2("window_lo", [P, NG, WIN], F16)
                K.window_col = sb2("window_col", [P, NG, WIN], F32)
                K.wide = sb2("wide", [1, 1], I32)
                prepare_edges(nc, K)
                count_edges(nc, K)

        def gat(tag, k, H, F, counts, finish, degree=False):
            with ExitStack() as c3:
                sb3 = lambda name, shape, dt: c3.enter_context(nc.sbuf_tensor(tag + name, shape, dt))
                T.mv = sb3("mv", [P, NB, 6 * H * F], F16)
                T.top = sb3("top", [P, 1], F32)
                T.thr = sb3("thr", [P, 2, NB, H], F32)
                T.c = sb3("c", [P, NB, H, 2], F32)
                scores(nc, K, tag + "s", k, H, F, T)
                T.num = sb3("num", [P, NB, H, F], F32)
                attention(nc, K, tag + "a", counts, H, F, T, degree)
                finish()

        turn_to_columns(nc, K, "t0", K.x, K.zT)
        for l in range(3):
            tag = f"g{l}"

            def finish():
                gat_normalise(nc, K, tag + "n", T.num, T.top, K.z, l == 0)
                turn_to_columns(nc, K, tag + "t", K.z, K.zT, bias=col("b0", l))
            with nc.cleanup_on_exit(), nc.sbuf_tensor(tag + "z", [P, NB, D], F32) as K.z:
                gat(tag, l, 1, D + 2, K.counts_all, finish, degree=(l == 0))
                batch_norm(nc, K, tag + "b", K.zT, K.zT, relu=True)
        with nc.cleanup_on_exit():
            turn_to_rows(nc, K, "r0", K.zT, K.x, residual=K.x)
            layer_norm(nc, K, "ln0", K.x)

        with nc.cleanup_on_exit(), ExitStack() as c2:
            sb2 = lambda name, shape, dt: c2.enter_context(nc.sbuf_tensor(name, shape, dt))
            z = sb2("z1", [P, NB, D], F32)
            parts = sb2("parts1", [P, NB, 3, D], BF16)
            wide = sb2("wide1", [D, 2, N], F32)
            w1 = sb2("w1", [D, 2, D], F32)
            w2 = sb2("w2", [D, 2, D], F32)
            load(nc, K, "w1", [(w1[:], K.w1_in.rearrange("f (j o) -> f j o", j=2)),
                                  (w2[:], K.w2_in.rearrange("(j f) o -> f j o", j=2))])
            turn_to_columns(nc, K, "t1", K.x, K.zT)
            batch_norm(nc, K, "b1", K.zT, K.zT, col("g_in"), col("be_in"))
            turn_to_rows(nc, K, "r1", K.zT, z)
            split_parts(nc, K, "p1", z, D, parts, scale=K.dinv)
            gather_in(nc, K, "c1", parts, z)
            turn_to_columns(nc, K, "t2", z, K.zT)
            linear_columns(nc, K, "l1", [(wide[:, j], [(w1[:, j], K.zT)], col("b1", j), None, None) for j in range(2)])
            for j in range(2):
                batch_norm(nc, K, f"b2{j}", wide[:, j], wide[:, j], col("g1", j), col("be1", j), relu=True)
            linear_rows(nc, K, "l2", [(wide[:, j], w2[:, j]) for j in range(2)], D, z)
            split_parts(nc, K, "p2", z, D, parts, scale=K.dinv)
            gather_in(nc, K, "c2", parts, z)
            turn_to_columns(nc, K, "t3", z, K.zT, bias=col("b2"))
            batch_norm(nc, K, "b3", K.zT, K.zT, col("g2"), col("be2"), relu=True)
            turn_to_rows(nc, K, "r2", K.zT, K.x, residual=K.x)
            layer_norm(nc, K, "ln1", K.x)

        turn_to_columns(nc, K, "t4", K.x, K.zT)
        for r in range(R):
            tag = f"r{r}"
            with nc.cleanup_on_exit():
                gat(tag, 3 + r, 4, 33, K.counts[r], lambda: relation_sum(nc, K, tag + "n", T.num, T.top, r))
        layer_norm(nc, K, "ln2", K.x)

        turn_to_columns(nc, K, "t5", K.x, K.zT)
        with ExitStack() as c2:
            sb2 = lambda name, shape, dt: c2.enter_context(nc.sbuf_tensor(name, shape, dt))
            att = sb2("att3", [P, NB, D], F32)
            with ExitStack() as c3:
                sb3 = lambda name, shape, dt: c3.enter_context(nc.sbuf_tensor(name, shape, dt))
                wqkv = sb3("wqkv", [D, 3 * D], F32)
                qkv = sb3("qkv", [P, NB, 3 * D], F32)
                ks = sb3("ks", [P, NB, D + 1], F32)
                load(nc, K, "wqkv", [(wqkv[:, i * D:(i + 1) * D], w) for i, w in enumerate((K.wq_in, K.wk_in, K.wv_in))])
                linear_rows(nc, K, "l3", [(K.zT, wqkv[:])], 3 * D, qkv, K.rows[0:P, ROW_QKV:NROW])
                with nc.sbuf_tensor("parts3", [P, NB, 3, D + 1], BF16) as parts:
                    key_values(nc, K, qkv, ks)
                    split_parts(nc, K, "p3", ks, D + 1, parts)
                    gather_out(nc, K, "c3", parts, D + 1, ks)
                head_attention(nc, K, "h3", qkv, ks, att)
            with ExitStack() as c3:
                sb3 = lambda name, shape, dt: c3.enter_context(nc.sbuf_tensor(name, shape, dt))
                wo = sb3("wo", [D, D], F32)
                fw1 = sb3("fw1", [D, 4, D], F32)
                fw2 = sb3("fw2", [D, 4, D], F32)
                aT = sb3("aT", [D, N], F32)
                hid = sb3("hid", [D, 4, N], F32)
                load(nc, K, "ffw", [(wo[:], K.wo_in), (fw1[:], K.fw1_in.rearrange("f (j o) -> f j o", j=4)),
                                       (fw2[:], K.fw2_in.rearrange("(j f) o -> f j o", j=4))])
                turn_to_columns(nc, K, "t6", att, aT)
                linear_columns(nc, K, "l4", [(K.zT, [(wo[:], aT)], col("bo"), None, K.zT)])
                batch_norm(nc, K, "b4", K.zT, K.zT, col("fg1"), col("fbe1"))
                linear_columns(nc, K, "l5", [(hid[:, j], [(fw1[:, j], K.zT)], col("fb1", j), ACT.Gelu, None)
                                                for j in range(4)])
                linear_columns(nc, K, "l6", [(K.zT, [(fw2[:, j], hid[:, j]) for j in range(4)], col("fb2"), None, K.zT)])
                batch_norm(nc, K, "b5", K.zT, K.zT, col("fg2"), col("fbe2"))
                turn_to_rows(nc, K, "r3", K.zT, K.x, residual=K.x)
                layer_norm(nc, K, "ln3", K.x)
        stored = S("out_stored")
        with nc.Block() as block:
            @block.sync
            def _(sp):
                sp.dma_start(out.rearrange("(b p) f -> p b f", p=P), K.x[:]).then_inc(stored, 16)
                sp.wait_ge(stored, 16)


@phase
def key_values(nc, K, S, qkv, ks):
    with nc.Block() as block:
        @block.vector
        def _(v):
            v.tensor_copy(ks[:, :, 0:D], qkv[:, :, D:2 * D])

        @block.gpsimd
        def _(pool):
            pool.memset(ks[:, :, D:D + 1], 1.0)


def kernel(**inputs):
    import numpy as _np
    import concourse.bacc as _bacc
    from concourse import mybir as _mybir
    from concourse.bass_utils import run_bass_kernel_spmd as _run

    nc = _bacc.Bacc("TRN2", target_bir_lowering=False, num_devices=1)
    arrays, args = {}, {}

    def give(name, a):
        a = _np.ascontiguousarray(a)
        arrays["in_" + name] = a
        args[name] = nc.dram_tensor("in_" + name, a.shape, _mybir.dt.from_np(a.dtype), kind="ExternalInput").ap()

    i = {k: _np.asarray(v) for k, v in inputs.items()}
    for name, key in (("src", "src"), ("dst", "dst"), ("typ", "edge_type_3")):
        give(name, i[key])
    give("x_in", i["x"])
    give("w_in", _np.concatenate([i["L0_gnn_W"], i["L2_gnn_W"]]))
    cols = [i[k].reshape(-1, D) for k in (
        "L1_gnn_g_in", "L1_gnn_be_in", "L1_gnn_b1", "L1_gnn_g1", "L1_gnn_be1", "L1_gnn_b2", "L1_gnn_g2", "L1_gnn_be2",
        "L3_gnn_bo", "L3_gnn_b1", "L3_gnn_b2", "L3_gnn_g1", "L3_gnn_be1", "L3_gnn_g2", "L3_gnn_be2")]
    a0 = _np.stack([i["L0_gnn_a_src"], i["L0_gnn_a_dst"]], axis=1).reshape(6, D)
    a2 = _np.stack([i["L2_gnn_att_src"].reshape(R, D), i["L2_gnn_att_dst"].reshape(R, D)], axis=1).reshape(6, D)
    give("cols_in", _np.concatenate([a0, a2, i["L0_gnn_b"]] + cols).T)
    give("rows_in", _np.concatenate([i["L2_gnn_bias"].reshape(-1), i["L2_gnn_rel_w"], i["L3_gnn_bq"], i["L3_gnn_bk"],
                                     i["L3_gnn_bv"]]))
    for name, key in (("w1_in", "L1_gnn_w1"), ("w2_in", "L1_gnn_w2"), ("wq_in", "L3_gnn_wq"), ("wk_in", "L3_gnn_wk"),
                      ("wv_in", "L3_gnn_wv"), ("wo_in", "L3_gnn_wo"), ("fw1_in", "L3_gnn_w1"), ("fw2_in", "L3_gnn_w2")):
        give(name, i[key])
    out = nc.dram_tensor("out_x", (N, D), _mybir.dt.float32, kind="ExternalOutput").ap()
    build(nc, args, out)
    r = _run(nc, [arrays], core_ids=[0])
    return r.results[0]["out_x"]
```

```python
from contextlib import ExitStack

import concourse.bass as bass
from concourse import mybir

F32 = mybir.dt.float32
F16 = mybir.dt.float16
BF16 = mybir.dt.bfloat16
I32 = mybir.dt.int32
U32 = mybir.dt.uint32
ALU = mybir.AluOpType
ACT = mybir.ActivationFunctionType
AX = mybir.AxisListType

N = 3125
P = 125
NB = N // P
D = 128
PAD = 128
E = 103125
CH = P
NCH = E // CH
R = 3
DG = 5
NG = N // DG
GW = R * NB * DG
GE = GW + 1
SUB = 25
NSUB = E // SUB
ROW = CH // SUB
WIN = 2
NROWS = NSUB - ROW + 1
EPS = 1e-5
ROUND = 12582912.0


class Chain:

    def __init__(self, eng, sem, base=0):
        self.eng, self.sem, self.n, self.base = eng, sem, 0, base

    def __call__(self, ins):
        self.n += 1
        ins.then_inc(self.sem, 1)
        self.eng.wait_ge(self.sem, self.base + self.n)


def phase(body):
    def run(nc, K, *rest, **more):
        body(nc, K, nc.alloc_semaphore, *rest, **more)
    return run


def ready_first(eng, *values):
    for value in values:
        eng.compute_val(value)


@phase
def prepare_edges(nc, K, S):
    with ExitStack() as ctx:
        sb = lambda name, shape, dt: ctx.enter_context(nc.sbuf_tensor(name, shape, dt))
        ei = sb("ei", [P, 3, NCH], I32)
        ef = sb("ef", [P, 3, NCH], F32)
        q = sb("q", [P, NCH], F32)
        q5 = sb("q5", [P, NCH], F32)
        mm = sb("mm", [P, 2, NCH // SUB], F16)
        lohi = sb("lohi", [P, 2, NSUB], F16)
        cmp = sb("cmp", [P, NSUB], F16)
        gi = sb("gi", [P, DG], I32)
        gf = sb("gf", [P, DG], F32)
        gb = sb("gb", [P, DG], F32)
        wlo = sb("wlo", [P, DG], F32)
        whi = sb("whi", [P, DG], F32)
        need = sb("need", [P, DG], F32)
        rows = sb("rows_of", [P, DG, WIN], U32)
        win = sb("win", [P, DG, WIN, CH, 2], F32)
        big = sb("big", [P, 2], F32)
        alln = sb("alln", [P, 1], F32)
        flag = sb("flag", [1, 1], I32)
        ti = sb("ti", [P, NG], I32)
        ki = sb("ki", [P, GE], I32)
        pi = sb("pi", [P, PAD, 2], I32)
        (loaded, iotas, own, mmout, mmin, keys_ready, keys_out, table, flag_ready, flag_in, shared, need_ready,
         rows_ready, gathered, based, turned) = (S("prep_" + n) for n in
            ("loaded", "iotas", "own", "mmout", "mmin", "keysr", "keyso", "table", "flagr", "flagin", "shared", "need",
             "rowsr", "gath", "based", "turned"))
        with nc.Block() as block:
            @block.sync
            def _(sp):
                sp.dma_start(ei[:, 1], K.dst_in.rearrange("(p c) -> p c", p=P)).then_inc(loaded, 16)
                sp.dma_start(ei[:, 0], K.src_in.rearrange("(p c) -> p c", p=P)).then_inc(loaded, 16)
                sp.dma_start(ei[:, 2], K.typ_in.rearrange("(p c) -> p c", p=P)).then_inc(loaded, 16)
                sp.wait_ge(mmout, 2)
                sp.dma_start(K.sub_range[:].rearrange("a (p c) -> p a c", p=P), mm[:]).then_inc(mmin, 16)
                sp.wait_ge(mmin, 16)
                sp.dma_start(lohi[:].rearrange("p a c -> p (a c)"),
                             K.sub_range[:].rearrange("a c -> (a c)").partition_broadcast(P)).then_inc(mmin, 16)
                sp.wait_ge(keys_ready, 2)
                sp.dma_start(K.edge_keys[:].rearrange("(p c) -> p c", p=P),
                             K.keys[:].rearrange("p c k -> p (c k)")).then_inc(keys_out, 16)
                sp.wait_ge(keys_out, 16)
                for phase in range(ROW):
                    n = (NROWS - 1 - phase) // ROW + 1
                    sp.dma_start(K.windows[:].rearrange("(r s) e -> s r e", s=ROW)[phase, 0:n],
                                 K.edge_keys[2 * SUB * phase:2 * SUB * phase + 2 * CH * n]
                                 .rearrange("(r e) -> r e", e=2 * CH)).then_inc(table, 16)
                sp.wait_ge(flag_ready, 1)
                sp.dma_start(K.wide[0:1, :], flag[:]).then_inc(flag_in, 16)
                sp.wait_ge(flag_in, 16)

            @block.gpsimd
            def _(pool):
                pool.iota(gi[:], [[P, DG]], channel_multiplier=1).then_inc(iotas, 1)
                pool.iota(ti[:], [[GW, NG]], channel_multiplier=0).then_inc(iotas, 1)
                pool.iota(ki[:], [[1, GE]], channel_multiplier=0).then_inc(iotas, 1)
                pool.iota(pi[:], [[1, PAD], [0, 2]], channel_multiplier=0).then_inc(iotas, 1)
                pool.wait_ge(rows_ready, WIN)
                pool.wait_ge(table, 16 * ROW)
                for j in range(DG):
                    for w in range(WIN):
                        pool.indirect_dma_start(win[:, j, w].rearrange("p e k -> p (e k)"), None, K.windows[0:NROWS],
                                                bass.IndirectOffsetOnAxis(rows[:, j, w:w + 1], 0)).then_inc(gathered, 16)
                pool.wait_ge(need_ready, 1)
                pool.partition_all_reduce(alln[:], big[:, 0:1], P, bass.bass_isa.ReduceOp.max).then_inc(shared, 1)

            @block.vector
            def _(v):
                link = Chain(v, own)
                fs, fd, ft = ef[:, 0], ef[:, 1], ef[:, 2]
                v.wait_ge(loaded, 48)
                link(v.tensor_copy(ef[:], ei[:]))
                link(v.tensor_scalar(q5[:], fd, -2.0, 1.0 / DG, ALU.add, ALU.mult))
                link(v.tensor_scalar(q5[:], q5[:], ROUND, None, ALU.add))
                link(v.tensor_scalar(q5[:], q5[:], -ROUND, None, ALU.add))
                groups = q5[:].rearrange("p (c e) -> p c e", e=SUB)
                v.tensor_reduce(mm[:, 0], groups, AX.X, ALU.min).then_inc(mmout, 1)
                v.tensor_reduce(mm[:, 1], groups, AX.X, ALU.max).then_inc(mmout, 1)
                link(v.tensor_scalar(q[:], fs, -62.0, 1.0 / P, ALU.add, ALU.mult))
                link(v.tensor_scalar(q[:], q[:], ROUND, None, ALU.add))
                link(v.tensor_scalar(q[:], q[:], -ROUND, None, ALU.add))
                v.scalar_tensor_tensor(K.keys[:, :, 0], q[:], -float(P), fs, ALU.mult, ALU.add).then_inc(keys_ready, 1)
                link(v.scalar_tensor_tensor(fd, q5[:], float(GW - DG), fd, ALU.mult, ALU.add))
                link(v.scalar_tensor_tensor(fd, ft, float(NB * DG), fd, ALU.mult, ALU.add))
                v.scalar_tensor_tensor(K.keys[:, :, 1], q[:], float(DG), fd, ALU.mult, ALU.add).then_inc(keys_ready, 1)
                v.wait_ge(iotas, 4)
                link(v.tensor_copy(gf[:], gi[:]))
                link(v.tensor_scalar(gb[:], gf[:], float(GW), None, ALU.mult))
                link(v.tensor_copy(K.group_base[:], ti[:]))
                link(v.tensor_copy(K.iota_col[:], ki[:]))
                link(v.tensor_copy(K.iota_pair[:], pi[:]))
                v.wait_ge(mmin, 32)
                for j in range(DG):
                    link(v.tensor_scalar(cmp[:], lohi[:, 1], gf[:, j:j + 1], None, ALU.is_lt, ALU.add,
                                         accum_out=wlo[:, j:j + 1]))
                for w in range(WIN):
                    link(v.tensor_scalar(need[:], wlo[:], float(NSUB - WIN * ROW), float(w * ROW), ALU.min, ALU.add))
                    link(v.tensor_copy(rows[:, :, w], need[:]))
                    v.sem_inc(rows_ready, 1)
                for j in range(DG):
                    link(v.tensor_scalar(cmp[:], lohi[:, 0], gf[:, j:j + 1], None, ALU.is_le, ALU.add,
                                         accum_out=whi[:, j:j + 1]))
                link(v.tensor_tensor(need[:], whi[:], wlo[:], ALU.subtract))
                link(v.tensor_reduce(big[:, 0:1], need[:], AX.X, ALU.max))
                link(v.tensor_tensor(cmp[:, 0:NSUB - 1], lohi[:, 1, 0:NSUB - 1], lohi[:, 0, 1:NSUB], ALU.is_gt))
                link(v.tensor_reduce(big[:, 1:2], cmp[:, 0:NSUB - 1], AX.X, ALU.max))
                v.scalar_tensor_tensor(big[:, 0:1], big[:, 1:2], float(NSUB), big[:, 0:1], ALU.mult,
                                       ALU.add).then_inc(need_ready, 1)
                v.wait_ge(gathered, 16 * WIN * DG)
                cols = win[:].rearrange("p j w e k -> p j (w e) k")[:, :, :, 1]
                v.tensor_tensor(cols, cols, gb[:].unsqueeze(2).to_broadcast([P, DG, WIN * CH]),
                                ALU.subtract).then_inc(based, 1)
                v.wait_ge(shared, 1)
                v.tensor_scalar(flag[:], alln[0:1, :], float(WIN * ROW), None, ALU.is_gt).then_inc(flag_ready, 1)
                for j in range(DG):
                    v.wait_ge(turned, 2 * WIN * (j + 1))
                    got = K.ps[0:P, j, 0:2 * WIN * P].rearrange("p (w k g) -> p w k g", w=WIN, k=2)
                    for k, dst in enumerate((K.window_lo, K.window_col)):
                        v.tensor_copy(dst[:, P * j:P * j + P].rearrange("p g w -> p w g"), got[:, :, k])

            @block.tensor
            def _(pe):
                pe.wait_ge(based, 1)
                for j in range(DG):
                    for w in range(WIN):
                        for k in range(2):
                            n = 2 * w + k
                            pe.transpose(K.ps[0:P, j, n * P:(n + 1) * P], win[:, j, w, :, k],
                                         K.ident[0:P, 0:P]).then_inc(turned, 1)


@phase
def count_edges(nc, K, S):
    OHS = 5
    SLOTS = 25
    STEPS = NCH // SLOTS
    STAGES = 3
    HALVES = ((0, 13), (13, NB))
    ADDED = (3, 8, 13, 18, 23)
    with ExitStack() as ctx:
        sb = lambda name, shape, dt: ctx.enter_context(nc.sbuf_tensor(name, shape, dt))
        lo1 = sb("lo1", [P, P // DG, PAD, WIN], BF16)
        col1 = sb("col1", [P, SLOTS, GE], BF16)
        stage = sb("stage", [P, STAGES, R, NB, PAD], F16)
        total = sb("total", [P, 2, NB, PAD], F16)
        lo_wide = lo1[:].rearrange("p s l w -> p (s l w)")[:, 0:SLOTS * PAD].rearrange("p (s l) -> p s l", l=PAD)
        (hot, counted, taken, summed, stored, cleared, diag, wide_hot, wide_used, moved) = (
            S("count_" + n) for n in ("hot", "counted", "taken", "summed", "stored", "cleared", "diag",
                                      "wide_hot", "wide_used", "moved"))
        with nc.Block() as block:
            @block.gpsimd
            def _(pool):
                pool.memset(stage[:], 0.0).then_inc(cleared, 1)
                pool.memset(total[:], 0.0).then_inc(cleared, 1)
                with pool.Fori(0, NB) as i:
                    pool.wait_ge(moved, 5 * i + 7)
                    for own in [stage[:, bass.ds(i % STAGES, 1), r, bass.ds(i, 1), 0:P] for r in range(R)] + \
                            [total[:, bass.ds(i % 2, 1), bass.ds(i, 1), 0:P]]:
                        own = own.rearrange("p a h d -> p (a h) d")
                        pool.tensor_tensor(own, own, K.ident16[0:P, 0:P].unsqueeze(1), ALU.add).then_inc(diag, 1)

            @block.vector
            def _(v):
                wide = v.value_load(K.wide[0:1, 0:1], min_val=0, max_val=1)
                with v.If(wide < 1):
                    with v.Fori(0, NB) as i:
                        for b in range(P // DG):
                            v.wait_ge(counted, i * (P // DG) + b + 1)
                            if b % OHS == 0:
                                v.tensor_tensor(
                                    lo1[:, b:b + OHS], K.iota_pair[:].unsqueeze(1).to_broadcast([P, OHS, PAD, WIN]),
                                    K.window_lo[:, bass.ds(i * (P // DG) + b, OHS)].unsqueeze(2)
                                    .to_broadcast([P, OHS, PAD, WIN]), ALU.is_equal)
                            for w in range(WIN):
                                ins = v.tensor_scalar(
                                    col1[:, b % OHS * WIN + w], K.iota_col[:],
                                    K.window_col[:, bass.ds(i * (P // DG) + b, 1), w], None, ALU.is_equal)
                            ins.then_inc(hot, 1)
                with v.Else():
                    with v.Fori(0, NG // OHS) as i:
                        for s in range(OHS):
                            with v.Fori(0, STEPS) as c:
                                v.wait_ge(wide_used, i * (OHS * STEPS) + s * STEPS + c + 1)
                                base = K.group_base[:, bass.ds(i * OHS + s, 1)]
                                for w in range(SLOTS):
                                    v.tensor_scalar(lo_wide[:, w], K.iota_col[:, 0:PAD],
                                                    K.keys[:, bass.ds(c * SLOTS + w, 1), 0], None, ALU.is_equal)
                                    ins = v.tensor_scalar(col1[:, w], K.iota_col[:], base,
                                                          K.keys[:, bass.ds(c * SLOTS + w, 1), 1],
                                                          ALU.add, ALU.is_equal)
                                ins.then_inc(wide_hot, 1)

            @block.tensor
            def _(pe):
                pe.sem_inc(counted, OHS)
                pe.sem_inc(moved, 1)
                pe.wait_ge(cleared, 2)

                def add_up(i, n, own=True):
                    slot, q = (i % STAGES, n - 1) if own else ((i + STAGES - 1) % STAGES, 4)
                    pe.wait_ge(taken, i * (P // DG) + 5 * n + OHS)
                    pe.wait_ge(moved, 5 * i + n + 1)
                    for half, (h0, h1) in enumerate(HALVES):
                        for r in range(R):
                            ins = pe.matmul(K.ps[0:P, OHS + half, 0:(h1 - h0) * NB], K.ident16[0:P, 0:P],
                                            stage[:, bass.ds(slot, 1), r, h0:h1, bass.ds(25 * q, 25)]
                                            .rearrange("p a h d -> p (a h) d"), start=(r == 0), stop=(r == R - 1))
                    ins.then_inc(summed, 1)

                wide = pe.value_load(K.wide[0:1, 0:1], min_val=0, max_val=1)
                with pe.If(wide < 1):
                    with pe.Fori(0, NB) as i:
                        for b in range(P // DG):
                            s = b % OHS
                            pe.wait_ge(hot, i * (P // DG) + b + 1)
                            pe.wait_ge(taken, i * (P // DG) + b + 1)
                            for w in range(WIN):
                                ins = pe.matmul(K.ps[0:P, s, 0:GW], lo1[:, b, 0:P, w], col1[:, s * WIN + w, 0:GW],
                                                start=(w == 0), stop=(w == WIN - 1))
                            ins.then_inc(counted, 1)
                            if b in ADDED:
                                add_up(i, ADDED.index(b), own=(b != ADDED[0]))
                with pe.Else():
                    pe.sem_inc(wide_used, 1)

                    def five_groups(i):
                        for s in range(OHS):
                            pe.wait_ge(taken, i * OHS + s + 1)
                            pe.matmul(K.ps[:, s, :], K.zeros[:, 0:128], K.zeros[:], start=True, stop=True)
                            with pe.Fori(0, STEPS) as c:
                                pe.wait_ge(wide_hot, i * (OHS * STEPS) + s * STEPS + c + 1)
                                for w in range(SLOTS):
                                    ins = pe.matmul(K.ps[0:P, s, 0:GW], lo_wide[:, w, 0:P], col1[:, w, 0:GW],
                                                    start=False, stop=False, skip_group_check=True)
                                ins.then_inc(wide_used, 1)
                            pe.matmul(K.ps[:, s, 0:128], K.zeros[:, 0:128], K.zeros[:, 0:128], start=False, stop=False,
                                      skip_group_check=True).then_inc(counted, 1)

                    with pe.Fori(0, NB) as i:
                        add_up(i, 0, own=False)
                        with pe.Fori(0, 4) as q:
                            five_groups(i * 5 + q)
                            add_up(i, q + 1)
                        five_groups(i * 5 + 4)
                add_up(NB, 0, own=False)

            @block.scalar
            def _(act):
                act.sem_inc(taken, OHS)
                act.wait_ge(cleared, 2)

                def move_total(i, n):
                    act.wait_ge(summed, 5 * i + n + 1)
                    if n == 1:
                        act.wait_ge(stored, 64 * i + 64 * (STAGES - 1))
                    slot, q = (i % 2, n - 1) if n else ((i + 1) % 2, 4)
                    for half, (h0, h1) in enumerate(HALVES):
                        ins = act.activation(total[:, bass.ds(slot, 1), h0:h1, 25 * q:25 * q + 25]
                                             .rearrange("p a h d -> p (a h) d"),
                                             K.ps[0:P, OHS + half, 0:(h1 - h0) * NB].rearrange("p (h d) -> p h d", d=NB),
                                             ACT.Copy)
                    ins.then_inc(moved, 1)

                with act.Fori(0, NB) as i:
                    act.wait_ge(stored, 64 * i + 64)
                    for b in range(P // DG):
                        act.wait_ge(counted, i * (P // DG) + b + 1 + OHS)
                        dst = stage[:, bass.ds(i % STAGES, 1), :, :, DG * b:DG * (b + 1)]
                        act.activation(dst.rearrange("p a r h d -> p (a r h) d"),
                                       K.ps[0:P, b % OHS, 0:GW].rearrange("p (x d) -> p x d", d=DG),
                                       ACT.Copy).then_inc(taken, 1)
                        if b - 1 in ADDED:
                            move_total(i, ADDED.index(b - 1))
                move_total(NB, 0)

            @block.sync
            def _(sp):
                sp.sem_inc(stored, 64 * STAGES)
                with sp.Fori(0, NB) as i:
                    sp.wait_ge(diag, 4 * i + 4)
                    sp.wait_ge(stored, 64 * i + 64 * STAGES)
                    for r in range(R):
                        sp.dma_start(K.counts[r, :, bass.ds(i, 1)].rearrange("p a h d -> p (a h d)"),
                                     stage[:, bass.ds(i % STAGES, 1), r].rearrange("p a h d -> p (a h d)")).then_inc(stored, 16)
                    sp.dma_start(K.counts_all[:, bass.ds(i, 1)].rearrange("p a h d -> p (a h d)"),
                                 total[:, bass.ds(i % 2, 1)].rearrange("p a h d -> p (a h d)")).then_inc(stored, 16)
                sp.wait_ge(stored, 64 * NB + 64 * STAGES)


@phase
def load_constants(nc, K, S):
    loaded, cleared, made = S("const_loaded"), S("const_cleared"), S("const_made")
    with nc.Block() as block:
        @block.sync
        def _(sp):
            sp.dma_start(K.x[:], K.x_in.rearrange("(b p) f -> p b f", p=P)).then_inc(loaded, 16)
            sp.dma_start(K.cols[:], K.cols_in).then_inc(loaded, 16)
            sp.dma_start(K.wext[:, :, 0:D], K.w_in.rearrange("k f j -> f k j")).then_inc(loaded, 16)
            sp.wait_ge(loaded, 48)

        @block.gpsimd
        def _(pool):
            pool.memset(K.ident[:], 0.0).then_inc(cleared, 1)
            pool.memset(K.ident16[:], 0.0).then_inc(cleared, 1)
            pool.memset(K.zeros[:], 0.0).then_inc(made, 1)
            pool.wait_ge(cleared, 2)
            for m in (K.ident, K.ident16):
                pool.affine_select(out=m[:], in_=m[:], compare_op=ALU.not_equal, fill=1.0, base=0,
                                   pattern=[[-1, 128]], channel_multiplier=1).then_inc(made, 1)


@phase
def score_weights(nc, K, S):
    with ExitStack() as ctx:
        sb = lambda name, shape, dt: ctx.enter_context(nc.sbuf_tensor(name, shape, dt))
        wt = sb("wt", [D, 6, D], F32)
        a = sb("a", [D, 6, 8], F32)
        cleared, filled, turned, moved, scored = (S("sw_" + n) for n in
                                                  ("cleared", "filled", "turned", "moved", "scored"))
        with nc.Block() as block:
            @block.vector
            def _(v):
                v.memset(a[:], 0.0).then_inc(cleared, 1)
                v.wait_ge(cleared, 1)
                for l in range(3):
                    v.tensor_copy(a[:, l, 0:2], K.cols[:, COL["a"] + 2 * l:COL["a"] + 2 * l + 2]).then_inc(filled, 1)
                for r in range(R):
                    for h in range(4):
                        rows = slice(32 * h, 32 * h + 32)
                        for side in range(2):
                            c = COL["att"] + 2 * r + side
                            v.tensor_copy(a[rows, 3 + r, 4 * side + h:4 * side + h + 1],
                                          K.cols[rows, c:c + 1]).then_inc(filled, 1)
                for k in range(6):
                    v.wait_ge(turned, k + 1)
                    v.tensor_copy(wt[:, k], K.ps[:, k, 0:D]).then_inc(moved, 1)
                v.wait_ge(scored, 6)
                for k in range(6):
                    v.tensor_copy(K.wext[:, k, D:D + 8], K.ps[:, k, D:D + 8])

            @block.tensor
            def _(pe):
                for k in range(6):
                    pe.transpose(K.ps[:, k, 0:D], K.wext[:, k, 0:D], K.ident[:]).then_inc(turned, 1)
                pe.wait_ge(filled, 27)
                for k in range(6):
                    pe.wait_ge(moved, k + 1)
                    pe.matmul(K.ps[:, k, D:D + 8], wt[:, k], a[:, k], start=True, stop=True).then_inc(scored, 1)


@phase
def turn_to_columns(nc, K, S, tag, src, dst):
    turned = S(tag + "_turned")
    with nc.Block() as block:
        @block.tensor
        def _(pe):
            for k in range(NB):
                pe.transpose(K.ps[:, k // 4, (k % 4) * P:(k % 4 + 1) * P], src[0:P, k, 0:D],
                             K.ident[0:P, 0:P]).then_inc(turned, 1)

        def move(eng, bank):
            eng.wait_ge(turned, min(4 * bank + 4, NB))
            w = min(4 * P, N - 4 * P * bank)
            out, got = dst[:, 4 * P * bank:4 * P * bank + w], K.ps[:, bank, 0:w]
            return out, got

        @block.vector
        def _(v):
            for bank in range(0, 7, 2):
                out, got = move(v, bank)
                v.tensor_copy(out, got)

        @block.scalar
        def _(act):
            for bank in range(1, 7, 2):
                out, got = move(act, bank)
                act.activation(out, got, ACT.Copy)


@phase
def turn_to_rows(nc, K, S, tag, src, dst, residual=None):
    turned = S(tag + "_turned")
    with nc.Block() as block:
        @block.tensor
        def _(pe):
            for k in range(NB):
                pe.transpose(K.ps[0:P, k // 4, (k % 4) * D:(k % 4 + 1) * D], src[:, k * P:(k + 1) * P],
                             K.ident[:]).then_inc(turned, 1)

        @block.vector
        def _(v):
            for bank in range(7):
                v.wait_ge(turned, min(4 * bank + 4, NB))
                n = min(4, NB - 4 * bank)
                out = dst[0:P, 4 * bank:4 * bank + n, 0:D]
                got = K.ps[0:P, bank, 0:n * D].rearrange("p (b f) -> p b f", f=D)
                if residual is None:
                    v.tensor_copy(out, got)
                else:
                    v.tensor_tensor(out, got, residual[0:P, 4 * bank:4 * bank + n, 0:D], ALU.add)


@phase
def batch_norm(nc, K, S, tag, z, out, g=None, b=None, relu=False, rows=None, bias=None):
    with ExitStack() as ctx:
        sb = lambda name, shape, dt: ctx.enter_context(nc.sbuf_tensor(tag + name, shape, dt))
        st = sb("st", [D, 7, 6], F32)
        mv = sb("mv", [D, 2], F32)
        sc = sb("sc", [D, 2], F32)
        own, rstd, turned, filled_v, filled_a = (S(tag + "_" + n) for n in
                                                 ("own", "rstd", "turned", "filledv", "filleda"))
        with nc.Block() as block:
            def bank(eng, m):
                eng.wait_ge(turned, min(4 * m + 4, NB))
                w = min(500, N - 500 * m)
                return z[:, 500 * m:500 * m + w], K.ps[:, m, 0:w]

            if rows is not None:
                @block.tensor
                def _(pe):
                    for k in range(NB):
                        pe.transpose(K.ps[:, k // 4, (k % 4) * P:(k % 4 + 1) * P], rows[0:P, k, 0:D],
                                     K.ident[0:P, 0:P]).then_inc(turned, 1)

            @block.vector
            def _(v):
                link = Chain(v, own)
                for m in range(7):
                    if rows is not None and m % 2 == 0:
                        dst, got = bank(v, m)
                        v.tensor_scalar(dst, got, 1.0 if bias is None else bias, None,
                                        ALU.mult if bias is None else ALU.add).then_inc(filled_v, 1)
                        v.wait_ge(filled_v, m // 2 + 1)
                    elif rows is not None:
                        v.wait_ge(filled_a, m // 2 + 1)
                    ins = v.bn_stats(st[:, m], z[:, 500 * m:min(500 * m + 500, N)])
                link(ins)
                link(v.bn_aggr(mv[:], st[:].rearrange("p a b -> p (a b)")))
                link(v.tensor_scalar(mv[:, 1:2], mv[:, 1:2], EPS, None, ALU.add))
                v.wait_ge(rstd, 1)
                link(v.reciprocal(sc[:, 0:1], mv[:, 1:2]))
                if g is not None:
                    link(v.tensor_tensor(sc[:, 0:1], sc[:, 0:1], g, ALU.mult))
                link(v.scalar_tensor_tensor(sc[:, 1:2], mv[:, 0:1], -1.0, sc[:, 0:1], ALU.mult, ALU.mult))
                if b is not None:
                    link(v.tensor_tensor(sc[:, 1:2], sc[:, 1:2], b, ALU.add))
                half = 1700
                link(v.tensor_scalar(out[:, 0:half], z[:, 0:half], sc[:, 0:1], sc[:, 1:2], ALU.mult, ALU.add))
                if relu:
                    v.tensor_scalar(out[:, 0:half], out[:, 0:half], 0.0, None, ALU.max)

            @block.scalar
            def _(act):
                if rows is not None:
                    for m in range(1, 7, 2):
                        dst, got = bank(act, m)
                        act.activation(dst, got, ACT.Identity, bias=0.0 if bias is None else bias).then_inc(filled_a, 1)
                act.wait_ge(own, 3)
                act.activation(mv[:, 1:2], mv[:, 1:2], ACT.Sqrt).then_inc(rstd, 1)
                act.wait_ge(own, 5 + (g is not None) + (b is not None))
                act.activation(out[:, 1700:N], z[:, 1700:N], ACT.Relu if relu else ACT.Identity,
                               bias=sc[:, 1:2], scale=sc[:, 0:1])


@phase
def layer_norm(nc, K, S, tag, x):
    BY_ACT = 11
    with ExitStack() as ctx:
        sb = lambda name, shape, dt: ctx.enter_context(nc.sbuf_tensor(tag + name, shape, dt))
        st = sb("st", [P, NB, 6], F32)
        mv = sb("mv", [P, NB, 2], F32)
        shift = sb("shift", [P, NB], F32)
        own, rstd = S(tag + "_own"), S(tag + "_rstd")
        with nc.Block() as block:
            @block.vector
            def _(v):
                link = Chain(v, own)
                for k in range(NB):
                    ins = v.bn_stats(st[:, k], x[:, k])
                link(ins)
                for k in range(NB):
                    ins = v.bn_aggr(mv[:, k], st[:, k])
                link(ins)
                link(v.tensor_scalar(mv[:, :, 1], mv[:, :, 1], EPS, None, ALU.add))
                v.wait_ge(rstd, 1)
                link(v.reciprocal(mv[:, :, 1], mv[:, :, 1]))
                v.scalar_tensor_tensor(shift[:], mv[:, :, 0], -1.0, mv[:, :, 1], ALU.mult, ALU.mult).then_inc(own, 1)
                for k in range(BY_ACT, NB):
                    v.tensor_scalar(x[:, k], x[:, k], mv[:, k, 0:1], mv[:, k, 1:2], ALU.subtract, ALU.mult)

            @block.scalar
            def _(act):
                act.wait_ge(own, 3)
                act.activation(mv[:, :, 1], mv[:, :, 1], ACT.Sqrt).then_inc(rstd, 1)
                act.wait_ge(own, 5)
                for k in range(BY_ACT):
                    act.activation(x[:, k], x[:, k], ACT.Identity, bias=shift[:, k:k + 1], scale=mv[:, k, 1:2])


@phase
def scores(nc, K, S, tag, k, counts, H, F, T):
    FH = D // H
    with ExitStack() as ctx:
        sb = lambda name, shape, dt: ctx.enter_context(nc.sbuf_tensor(tag + name, shape, dt))
        hx = sb("hx", [P, NB, D + 8], F32)
        val = sb("val", [P, NB, H, 2, F], F32)
        adr = sb("adr", [H, NB, PAD], F32)
        gmax = sb("gmax", [P, 2, H + 1], F32)
        piece = sb("piece", [P, 5], F32)
        asg = sb("asg", [P, NB, H], F32)
        u = sb("u", [P, 4, NB, H], F32)
        t = sb("t", [P, NB, H], F32)
        tm = sb("tm", [P, NB, H, 2], F32)
        sv = sb("sv", [P, 2], F32)
        (proj, projv, adp, adt, adz, adst, own, mx, mxr, asr, ur, tr, part, rest, vals_ready) = (
            S(tag + "_" + n) for n in ("proj", "projv", "adp", "adt", "adz", "adst", "own", "mx", "mxr", "asr",
                                       "ur", "tr", "part", "rest", "vals"))
        W = D + 2 * H
        sign = 1.0 if H == 1 else -1.0
        parts = T.mv[:, :, 0:4 * H * F].rearrange("p b (h c f) -> p b h c f", h=H, c=2)
        with nc.Block() as block:
            @block.tensor
            def _(pe):
                for b in range(NB):
                    if b >= 7:
                        pe.wait_ge(projv, b - 6)
                    pe.matmul(K.ps[0:P, b % 7, 0:W], K.zT[:, P * b:P * b + P], K.wext[:, k, 0:W],
                              start=True, stop=True).then_inc(proj, 1)
                for m in range(7):
                    w = min(500, N - 500 * m)
                    pe.wait_ge(projv, (NB - 1 - m) // 7 * 7 + m + 1)
                    pe.matmul(K.ps[0:H, m, 0:w], K.wext[:, k, D + H:D + 2 * H], K.zT[:, 500 * m:500 * m + w],
                              start=True, stop=True).then_inc(adp, 1)

            @block.scalar
            def _(act):
                for b in range(NB):
                    act.wait_ge(proj, b + 1)
                    act.activation(hx[:, b, 0:W], K.ps[0:P, b % 7, 0:W], ACT.Copy).then_inc(projv, 1)
                act.wait_ge(asr, 1)
                act.activation(u[:, 0], asg[:], ACT.Exp).then_inc(ur, 1)
                act.activation(u[:, 1], asg[:], ACT.Exp, scale=0.2).then_inc(ur, 1)
                act.wait_ge(adz, 1)
                for m in range(7):
                    n = min(4, NB - 4 * m)
                    act.wait_ge(adp, m + 1)
                    act.activation(adr[:, 4 * m:4 * m + n, 0:P],
                                   K.ps[0:H, m, 0:n * P].rearrange("p (b c) -> p b c", c=P), ACT.Copy).then_inc(adt, 1)
                act.wait_ge(tr, 2)
                act.activation(T.c[:], tm[:], ACT.Exp).then_inc(ur, 1)
                for p in range(2):
                    for q in range(5):
                        act.wait_ge(rest if p else vals_ready, q + 1)
                        act.activation(parts[:, 5 * q:5 * q + 5, :, p],
                                       val[:, 5 * q:5 * q + 5].rearrange("p b h a f -> p b h (a f)"),
                                       ACT.Copy).then_inc(part, 1)

            @block.gpsimd
            def _(pool):
                pool.memset(adr[:], 0.0).then_inc(adz, 1)
                pool.wait_ge(mx, 2)
                pool.partition_all_reduce(gmax[:, 1], gmax[:, 0], P, bass.bass_isa.ReduceOp.max).then_inc(mxr, 1)

            @block.sync
            def _(sp):
                for c in range(5):
                    sp.dma_start(T.ct[:, c], counts[:, 0:5, 5 * c:5 * c + 5]).then_inc(T.landed[c], 16)
                sp.wait_ge(adt, 7)
                sp.dma_start(K.ad_rows[0:H], adr[:]).then_inc(adst, 16)
                sp.wait_ge(adst, 16)
                sp.sem_inc(T.ad_landed, 16)
                sp.dma_start(T.ad[:, 0].rearrange("p h d -> p (h d)"),
                             K.ad_rows[0:H, 0:5].rearrange("h b d -> h (b d)").partition_broadcast(P)
                             ).then_inc(T.ad_landed, 16)

            @block.vector
            def _(v):
                link = Chain(v, own)
                for q in range(5):
                    v.wait_ge(projv, 5 * q + 5)
                    ins = v.tensor_reduce(piece[:, q:q + 1], hx[:, 5 * q:5 * q + 5, 0:D], AX.XY, ALU.max,
                                          apply_absolute_value=True)
                link(ins)
                a_s, a_d = hx[:, :, D:D + H], hx[:, :, D + H:D + 2 * H]
                v.tensor_reduce(gmax[:, 0, 0:H], a_s.rearrange("p b h -> p h b"), AX.X, ALU.max).then_inc(mx, 1)
                v.tensor_reduce(gmax[:, 0, H:H + 1], piece[:], AX.X, ALU.max).then_inc(mx, 1)
                link(v.tensor_scalar(T.thr[:, 0], a_s, -1.0, None, ALU.mult))
                link(v.tensor_scalar(T.thr[:, 1], a_s, -STEEP, None, ALU.mult))
                v.wait_ge(mxr, 1)
                G = gmax[:, 1, 0:H].unsqueeze(1).to_broadcast([P, NB, H])
                v.tensor_tensor(asg[:], a_s, G, ALU.subtract).then_inc(asr, 1)
                link(v.tensor_tensor(t[:], a_d, G, ALU.add))
                v.tensor_scalar(tm[:, :, :, 1], t[:], 0.8, 0.0, ALU.mult, ALU.min).then_inc(tr, 1)
                v.tensor_scalar(tm[:, :, :, 0], t[:], -0.8, 0.0, ALU.mult, ALU.min).then_inc(tr, 1)
                link(v.tensor_scalar(T.top[:], gmax[:, 1, H:H + 1], TINY, None, ALU.max))
                link(v.reciprocal(sv[:, 0:1], T.top[:]))
                link(v.tensor_scalar(sv[:, 1:2], sv[:, 0:1], TOP, None, ALU.mult))
                v.wait_ge(ur, 2)
                link(v.tensor_scalar(u[:, 2:4], u[:, 0:2], sv[:, 1:2], None, ALU.mult))
                if F > FH + 1:
                    link(v.memset(val[:, :, :, 0, F - 1:F], 1.0))
                    link(v.memset(val[:, :, :, 1, F - 1:F], sign))
                link(v.tensor_scalar(val[:, :, :, 0, FH:FH + 1], u[:, 1].unsqueeze(3), TOP, None, ALU.mult))
                link(v.tensor_scalar(val[:, :, :, 1, FH:FH + 1], u[:, 0].unsqueeze(3), sign * TOP, None, ALU.mult))
                for q in range(5):
                    s = slice(5 * q, 5 * q + 5)
                    h4 = hx[:, s, 0:D].rearrange("p b (h f) -> p b h f", h=H)
                    ub = lambda i: u[:, i, s].unsqueeze(3).to_broadcast([P, 5, H, FH])
                    v.tensor_tensor(val[:, s, :, 0, 0:FH], h4, ub(3), ALU.mult).then_inc(own, 1)
                    v.scalar_tensor_tensor(val[:, s, :, 1, 0:FH], h4, sign, ub(2), ALU.mult,
                                           ALU.mult).then_inc(vals_ready, 1)
                for q in range(5):
                    s = slice(5 * q, 5 * q + 5)
                    v.wait_ge(part, q + 1)
                    vv = val[:, s].rearrange("p b h a f -> p b h (a f)")
                    v.tensor_tensor(vv, vv, parts[:, s, :, 0], ALU.subtract).then_inc(rest, 1)
                for c in range(2 if H > 1 else 0):
                    v.wait_ge(part, 5 * c + 5)
                    v.tensor_scalar(T.mv[:, :, (4 + c) * H * F:(5 + c) * H * F].rearrange("p b (h f) -> p b h f", h=H),
                                    parts[:, :, :, c].rearrange("p b h (a f) -> p b h a f", a=2)[:, :, :, 1],
                                    -1.0, None, ALU.mult)


@phase
def attention_one(nc, K, S, tag, counts, F, T, degree=False):
    AHEAD = 3
    with ExitStack() as ctx:
        sb = lambda name, shape, dt: ctx.enter_context(nc.sbuf_tensor(tag + name, shape, dt))
        ct, ad, landed, ad_landed = T.ct, T.ad[:, :, 0], T.landed, T.ad_landed
        msk = sb("msk", [P, 5, 5, PAD], F16)
        sel = sb("sel", [P, 5, 2, 5, PAD], F16)
        tmp = sb("tmp", [P, 5, F], F32)
        (mready, turns, below, masked, used, full, half, drained) = (S(tag + "_" + n) for n in (
            "mready", "turns", "below", "masked", "used", "full", "half", "drained"))

        def ordered(eng, step, drain):
            for s in range(AHEAD):
                step(0, s)
            with eng.Fori(0, 4) as g:
                for s in range(AHEAD, NB):
                    step(g, s)
                for s in range(AHEAD):
                    step(g + 1, s)
                for b in range(5):
                    drain(g, b)
            for s in range(AHEAD, NB):
                step(4, s)
            for b in range(5):
                drain(4, b)

        def sums_complete(eng, g, b):
            if b < 4:
                eng.wait_ge(full, 4 * g + b + 1)
            else:
                eng.wait_ge(used, 25 * g + 50)

        with nc.Block() as block:
            @block.sync
            def _(sp):
                with sp.Fori(1, 5) as g:
                    slot, first = sp.snap(g % 2), sp.snap(5 * g)
                    made, had = sp.snap(25 * g + 1), sp.snap(16 * g + 16)
                    ready_first(sp, slot, first, made, had)
                    sp.wait_ge(used, made)
                    sp.wait_ge(ad_landed, had)
                    sp.dma_start(ad[:, bass.ds(slot, 1)].rearrange("p a d -> p (a d)"),
                                 K.ad_rows[0:1, bass.ds(first, 5)].rearrange("h b d -> (h b d)").partition_broadcast(P)
                                 ).then_inc(ad_landed, 16)
                    for c in range(5):
                        sp.wait_ge(used, 25 * g + 5 * c + 5)
                        sp.dma_start(ct[:, c], counts[:, bass.ds(first, 5), 5 * c:5 * c + 5]).then_inc(landed[c], 16)

            @block.scalar
            def _(act):
                def step(g, s):
                    act.wait_ge(ad_landed, 16 * g + 32)
                    act.wait_ge(below, 25 * g + s + 1)
                    act.sem_inc(turns, 1)
                    act.activation(msk[:, s % 5], ad[:, bass.ds(g % 2, 1)].rearrange("p a (b d) -> p (a b) d", d=PAD),
                                   ACT.Sigmoid, bias=T.thr[:, 1, s, 0:1], scale=-STEEP).then_inc(mready, 1)

                def drain(g, b):
                    sums_complete(act, g, b)
                    act.wait_ge(drained, 5 * g + b + 1)
                    act.sem_inc(turns, 1)
                    act.activation(tmp[:, b], K.ps[0:P, b, 0:F], ACT.Copy,
                                   scale=T.c[:, bass.ds(5 * g + b, 1), 0, 0]).then_inc(half, 1)

                ordered(act, step, drain)

            @block.vector
            def _(v):
                v.sem_inc(drained, 5)
                v.sem_inc(below, 5)

                def step(g, s):
                    v.wait_ge(used, 25 * g + s + 21)
                    v.wait_ge(landed[s // 5], 16 * g + 16)
                    v.wait_ge(mready, 25 * g + s + 1)
                    c = ct[:, s // 5, :, s % 5]
                    v.tensor_tensor(sel[:, s % 5, 0], msk[:, s % 5], c, ALU.mult).then_inc(below, 1)
                    v.wait_ge(below, 25 * g + s + 6)
                    v.tensor_tensor(sel[:, s % 5, 1], c, sel[:, s % 5, 0], ALU.subtract).then_inc(masked, 1)

                def drain(g, b):
                    sums_complete(v, g, b)
                    v.wait_ge(half, 5 * g + b + 1)
                    if degree:
                        v.tensor_copy(K.dinv[:, bass.ds(5 * g + b, 1)], K.ps[0:P, b, F - 1:F])
                        v.tensor_copy(K.dinv2[:, bass.ds(5 * g + b, 1)], K.ps[0:P, b, 2 * F - 1:2 * F])
                    v.scalar_tensor_tensor(T.num[:, bass.ds(5 * g + b, 1), 0].rearrange("p a f -> p (a f)"),
                                           K.ps[0:P, b, F:2 * F], T.c[:, bass.ds(5 * g + b, 1), 0, 1], tmp[:, b],
                                           ALU.mult, ALU.add).then_inc(drained, 1)

                ordered(v, step, drain)

            @block.tensor
            def _(pe):
                pe.sem_inc(used, 25)
                with pe.Fori(0, 5) as g:
                    for s in range(NB):
                        if s % 5 == 0:
                            pe.wait_ge(landed[s // 5], 16 * g + 16)
                        pe.wait_ge(masked, 25 * g + s + 1)
                        for b in range(5):
                            if s == 0:
                                pe.wait_ge(drained, 5 * g + b + 1)
                                pe.matmul(K.ps[:, b, 0:2 * F], K.zeros[:, 0:128], K.zeros[:, 0:2 * F], start=True,
                                          stop=True)
                            for a in range(2):
                                for p in range(2):
                                    ins = pe.matmul(K.ps[:, b, a * F:(a + 1) * F], sel[:, s % 5, a, b],
                                                    T.mv[:, s, (2 * p + a) * F:(2 * p + a + 1) * F],
                                                    start=False, stop=False, skip_group_check=True)
                            if s == NB - 1 and b < 4:
                                ins.then_inc(full, 1)
                        ins.then_inc(used, 1)


@phase
def attention_heads(nc, K, S, tag, counts, H, F, T):
    AHEAD = 3
    HF = H * F
    by_act = lambda s: list(range(2 if s % 8 == 7 else 1, H))
    masks = [sum(len(by_act(i)) for i in range(s)) for s in range(NB + 1)]
    with ExitStack() as ctx:
        sb = lambda name, shape, dt: ctx.enter_context(nc.sbuf_tensor(tag + name, shape, dt))
        ct, ad, landed, ad_landed = T.ct, T.ad, T.landed, T.ad_landed
        sel = sb("sel", [P, 5, H, 5, PAD], F16)
        msk = sb("msk", [P, 5, 3, 5, PAD], F16)
        tmp = sb("tmp", [P, 2, 2 * HF], F32)
        (masked, used, full, scaled, drained, mready, turns) = (
            S(tag + "_" + n) for n in ("masked", "used", "full", "scaled", "drained", "mready", "turns"))
        with nc.Block() as block:
            @block.sync
            def _(sp):
                with sp.Fori(1, 5) as g:
                    slot, first = sp.snap(g % 2), sp.snap(5 * g)
                    made, had = sp.snap(25 * g + 1), sp.snap(16 * g + 16)
                    ready_first(sp, slot, first, made, had)
                    sp.wait_ge(used, made)
                    sp.wait_ge(ad_landed, had)
                    sp.dma_start(ad[:, bass.ds(slot, 1)].rearrange("p a h d -> p (a h) d"),
                                 K.ad_rows[0:H, bass.ds(first, 5)].rearrange("h b d -> h (b d)").partition_broadcast(P)
                                 ).then_inc(ad_landed, 16)
                    for c in range(5):
                        sp.wait_ge(used, 25 * g + 5 * c + 5)
                        sp.dma_start(ct[:, c], counts[:, bass.ds(first, 5), 5 * c:5 * c + 5]).then_inc(landed[c], 16)

            @block.scalar
            def _(act):
                with act.Fori(0, 5) as g:
                    for s in range(NB):
                        act.wait_ge(ad_landed, 16 * g + 32)
                        act.wait_ge(masked, 25 * g + s + 1)
                        act.sem_inc(turns, 1)
                        for n, h in enumerate(by_act(s)):
                            act.activation(msk[:, s % 5, n], ad[:, bass.ds(g % 2, 1), h]
                                           .rearrange("p a (b d) -> p (a b) d", d=PAD),
                                           ACT.Sigmoid, bias=T.thr[:, 1, s, h:h + 1],
                                           scale=-STEEP).then_inc(mready, 1)

            @block.vector
            def _(v):
                v.sem_inc(drained, 5)
                v.sem_inc(masked, 5)

                def step(g, s):
                    n, c = len(by_act(s)), ct[:, s // 5, :, s % 5]
                    v.wait_ge(ad_landed, 16 * g + 32)
                    v.wait_ge(landed[s // 5], 16 * g + 16)
                    v.wait_ge(used, 25 * g + s + 21)
                    for h in range(H - n):
                        v.scalar_tensor_tensor(
                            sel[:, s % 5, h], ad[:, bass.ds(g % 2, 1), h].rearrange("p a (b d) -> p (a b) d", d=PAD),
                            T.thr[:, 0, s, h:h + 1], c, ALU.is_lt, ALU.mult)
                    v.wait_ge(mready, masks[NB] * g + masks[s + 1])
                    v.tensor_tensor(sel[:, s % 5, H - n:H], msk[:, s % 5, 0:n],
                                    c.unsqueeze(1).to_broadcast([P, n, 5, PAD]), ALU.mult).then_inc(masked, 1)

                def drain(g):
                    for b in range(6):
                        if b < 4:
                            v.wait_ge(full, 4 * g + b + 1)
                        elif b == 4:
                            v.wait_ge(used, 25 * g + 50)
                        if b < 5:
                            v.tensor_tensor(tmp[:, b % 2].rearrange("p (x f) -> p x f", f=F),
                                            K.ps[0:P, b, 0:2 * HF].rearrange("p (x f) -> p x f", f=F),
                                            T.c[:, bass.ds(5 * g + b, 1)].rearrange("p b h a -> p (b h a)").unsqueeze(2)
                                            .to_broadcast([P, 2 * H, F]), ALU.mult).then_inc(drained, 1)
                        if b > 0:
                            v.wait_ge(drained, 5 * g + b + 5)
                            t4 = tmp[:, (b - 1) % 2].rearrange("p (h a f) -> p h a f", h=H, a=2)
                            v.tensor_tensor(T.num[:, bass.ds(5 * g + b - 1, 1)].rearrange("p b h f -> p (b h) f"),
                                            t4[:, :, 0], t4[:, :, 1], ALU.add).then_inc(scaled, 1)
                            v.wait_ge(scaled, 5 * g + b)

                for s in range(AHEAD):
                    step(0, s)
                with v.Fori(0, 4) as g:
                    for s in range(AHEAD, NB):
                        step(g, s)
                    for s in range(AHEAD):
                        step(g + 1, s)
                    drain(g)
                for s in range(AHEAD, NB):
                    step(4, s)
                drain(4)

            @block.tensor
            def _(pe):
                pe.sem_inc(used, 25)
                with pe.Fori(0, 5) as g:
                    for s in range(NB):
                        if s % 5 == 0:
                            pe.wait_ge(landed[s // 5], 16 * g + 16)
                        pe.wait_ge(masked, 25 * g + s + 6)
                        vs = T.mv[:, s]
                        for b in range(5):
                            if s == 0:
                                pe.wait_ge(drained, 5 * g + b + 1)
                                pe.matmul(K.ps[:, b, 0:2 * HF], K.zeros[:, 0:128], K.zeros[:, 0:2 * HF], start=True,
                                          stop=True)
                            for h in range(H):
                                for p in range(2):
                                    pe.matmul(K.ps[:, b, 2 * h * F:2 * (h + 1) * F], sel[:, s % 5, h, b],
                                              vs[:, (h * 2 + p) * 2 * F:(h * 2 + p + 1) * 2 * F],
                                              start=False, stop=False, skip_group_check=True)
                            for p in range(2):
                                ins = pe.matmul(K.ps[:, b, 0:2 * HF].rearrange("p (h a f) -> p h a f", h=H, a=2)[:, :, 1],
                                                ct[:, s // 5, b, s % 5],
                                                vs[:, (4 + p) * HF:(5 + p) * HF].rearrange("p (h f) -> p h f", h=H),
                                                start=False, stop=False, skip_group_check=True)
                            if s == NB - 1 and b < 4:
                                ins.then_inc(full, 1)
                        ins.then_inc(used, 1)


@phase
def gat_normalise(nc, K, S, tag, num, top, z, degree):
    with ExitStack() as ctx:
        rden = ctx.enter_context(nc.sbuf_tensor(tag + "rden", [P, NB], F32))
        own, root = S(tag + "_own"), S(tag + "_root")
        with nc.Block() as block:
            @block.vector
            def _(v):
                link = Chain(v, own)
                if degree:
                    link(v.tensor_tensor(K.dinv[:], K.dinv[:], K.dinv2[:], ALU.add))
                    link(v.tensor_scalar(K.dinv[:], K.dinv[:], 1.0, None, ALU.max))
                link(v.reciprocal(rden[:], num[:, :, 0, D]))
                link(v.tensor_scalar(rden[:], rden[:], top[:], None, ALU.mult))
                v.tensor_tensor(z[0:P], num[:, :, 0, 0:D], rden[:].unsqueeze(2).to_broadcast([P, NB, D]), ALU.mult)
                if degree:
                    v.wait_ge(root, 1)
                    v.reciprocal(K.dinv[:], K.dinv[:])

            @block.scalar
            def _(act):
                if degree:
                    act.wait_ge(own, 2)
                    act.activation(K.dinv[:], K.dinv[:], ACT.Sqrt).then_inc(root, 1)


@phase
def relation_sum(nc, K, S, tag, num, top, r):
    with ExitStack() as ctx:
        sb = lambda name, shape, dt: ctx.enter_context(nc.sbuf_tensor(tag + name, shape, dt))
        rden = sb("rden", [P, NB, 4], F32)
        own = S(tag + "_own")
        with nc.Block() as block:
            @block.vector
            def _(v):
                link = Chain(v, own)
                wr = K.relw[0:P, 3 + r:4 + r]
                link(v.reciprocal(rden[:], num[:, :, :, 32]))
                link(v.tensor_scalar(rden[:], rden[:], wr, top[:], ALU.mult, ALU.mult))
                link(v.tensor_tensor(num[:, :, :, 0:32], num[:, :, :, 0:32],
                                     rden[:].unsqueeze(3).to_broadcast([P, NB, 4, 32]), ALU.mult))
                x4 = K.x[:].rearrange("p b (h f) -> p b h f", h=4)
                link(v.tensor_tensor(x4, x4, num[:, :, :, 0:32], ALU.add))
                if r == 0:
                    bias = K.rows[0:P, 0:D]
                    link(v.tensor_scalar(bias, bias, wr, None, ALU.mult))
                    for i in range(1, R):
                        link(v.scalar_tensor_tensor(bias, K.rows[0:P, i * D:(i + 1) * D], K.relw[0:P, 3 + i:4 + i], bias,
                                                    ALU.mult, ALU.add))
                    v.tensor_tensor(K.x[:], K.x[:], bias.unsqueeze(1).to_broadcast([P, NB, D]), ALU.add)


@phase
def relation_weights(nc, K, S):
    own, done = S("relw_own"), S("relw_exp")
    with ExitStack() as ctx:
        m = ctx.enter_context(nc.sbuf_tensor("relm", [128, 2], F32))
        with nc.Block() as block:
            @block.vector
            def _(v):
                link = Chain(v, own)
                link(v.tensor_copy(K.relw[:, 0:3], K.rows[:, ROW_RELW:ROW_RELW + 3]))
                link(v.tensor_reduce(m[:, 0:1], K.relw[:, 0:3], AX.X, ALU.max))
                link(v.tensor_scalar(K.relw[:, 0:3], K.relw[:, 0:3], m[:, 0:1], None, ALU.subtract))
                v.wait_ge(done, 1)
                link(v.tensor_reduce(m[:, 0:1], K.relw[:, 3:6], AX.X, ALU.add))
                link(v.reciprocal(m[:, 1:2], m[:, 0:1]))
                v.tensor_scalar(K.relw[:, 3:6], K.relw[:, 3:6], m[:, 1:2], None, ALU.mult)

            @block.scalar
            def _(act):
                act.wait_ge(own, 3)
                act.activation(K.relw[:, 3:6], K.relw[:, 0:3], ACT.Exp).then_inc(done, 1)


@phase
def split_parts(nc, K, S, tag, val, parts, span, first, scale=None):
    ready, part, rest, own, greatest, known, scaling = (S(tag + "_" + n) for n in (
        "ready", "part", "rest", "own", "greatest", "known", "scaling"))
    with ExitStack() as ctx:
        m = ctx.enter_context(nc.sbuf_tensor(tag + "m", [P, 2], F32))
        factor = ctx.enter_context(nc.sbuf_tensor(tag + "factor", [P, 1], F32))
        with nc.Block() as block:
            @block.sync
            def _(sp):
                for dst, src, landed in first:
                    sp.dma_start(dst, src).then_inc(landed, 16)

            @block.vector
            def _(v):
                link = Chain(v, own)
                if scale is not None:
                    link(v.tensor_tensor(val, val, scale[:].unsqueeze(2).to_broadcast([P, NB, D]), ALU.mult))
                v.tensor_reduce(m[:, 0:1], val, AX.XY, ALU.max, apply_absolute_value=True).then_inc(greatest, 1)
                v.wait_ge(known, 1)
                link(v.tensor_scalar(m[:, 1:2], m[:, 1:2], TINY, None, ALU.max))
                link(v.reciprocal(factor[:], m[:, 1:2]))
                v.tensor_scalar(factor[:], factor[:], TOP, None, ALU.mult).then_inc(scaling, 1)
                v.tensor_scalar(span, m[:, 1:2], 1.0 / TOP, None, ALU.mult)
                for q in range(5):
                    s = slice(5 * q, 5 * q + 5)
                    v.wait_ge(scaling, 1)
                    v.wait_ge(part, q + 1)
                    v.scalar_tensor_tensor(val[:, s], val[:, s], factor[:], parts[:, s, 0, 0:D], ALU.mult,
                                           ALU.subtract).then_inc(rest, 1)

            @block.gpsimd
            def _(pool):
                pool.wait_ge(greatest, 1)
                pool.partition_all_reduce(m[:, 1:2], m[:, 0:1], P, bass.bass_isa.ReduceOp.max).then_inc(known, 1)

            @block.scalar
            def _(act):
                act.wait_ge(scaling, 1)
                for q in range(5):
                    s = slice(5 * q, 5 * q + 5)
                    act.activation(parts[:, s, 0, 0:D], val[:, s], ACT.Copy, scale=factor[:]).then_inc(part, 1)
                for q in range(5):
                    s = slice(5 * q, 5 * q + 5)
                    act.wait_ge(rest, q + 1)
                    act.activation(parts[:, s, 1, 0:D], val[:, s], ACT.Copy)


@phase
def gather_in(nc, K, S, tag, ct, landed, parts, span, dst):
    used, full, drained = S(tag + "_used"), S(tag + "_full"), S(tag + "_drained")
    with nc.Block() as block:
        @block.sync
        def _(sp):
            with sp.Fori(1, 5) as g:
                for c in range(5):
                    sp.wait_ge(used, 5 * g + c + 1)
                    sp.dma_start(ct[:, c], K.counts_all[:, bass.ds(5 * g, 5), 5 * c:5 * c + 5]).then_inc(landed[c], 16)

        @block.tensor
        def _(pe):
            pe.sem_inc(used, 5)
            with pe.Fori(0, 5) as g:
                for s in range(NB):
                    if s % 5 == 0:
                        pe.wait_ge(landed[s // 5], 16 * g + 16)
                    for b in range(5):
                        if s == 0:
                            pe.wait_ge(drained, 5 * g + b + 1)
                        for p in range(2):
                            ins = pe.matmul(K.ps[:, b, 0:D], ct[:, s // 5, b, s % 5], parts[:, s, p],
                                            start=(s == 0 and p == 0), stop=(s == NB - 1 and p == 1))
                        if s == NB - 1 and b < 4:
                            ins.then_inc(full, 1)
                    if s % 5 == 4:
                        ins.then_inc(used, 1)

        @block.vector
        def _(v):
            v.sem_inc(drained, 5)
            with v.Fori(0, 5) as g:
                for b in range(5):
                    if b < 4:
                        v.wait_ge(full, 4 * g + b + 1)
                    else:
                        v.wait_ge(used, 5 * g + 10)
                    v.tensor_scalar(dst[:, bass.ds(5 * g + b, 1)].rearrange("p a f -> p (a f)"), K.ps[0:P, b, 0:D],
                                    K.dinv[:, bass.ds(5 * g + b, 1)], span, ALU.mult, ALU.mult).then_inc(drained, 1)


@phase
def attend_to_keys(nc, K, S, tag, ct, landed, parts, span, qkv, att):
    W = D + 1
    H, DH = 8, 16
    LAG = 2
    EXP_AT = 18
    LINKS = 6
    with ExitStack() as ctx:
        sb = lambda name, shape, dt: ctx.enter_context(nc.sbuf_tensor(tag + name, shape, dt))
        cT = sb("cT", [128, 5, 5, PAD], F16)
        cnt = sb("cnt", [P, 5], F32)
        kl = sb("kl", [P, 5, D], F32)
        pr = sb("pr", [P, 2, H * H * DH], F32)
        s = sb("s", [P, 5, H, H], F32)
        m = sb("m", [P, 5, H], F32)
        (turned, moved, used, drained, cleared, own, mult, red, centred, exped, turns) = (S(tag + "_" + n) for n in (
            "turned", "moved", "used", "drained", "cleared", "own", "mult", "red", "centred", "exped", "turns"))
        T16 = K.ps[:].bitcast(F16)
        with nc.Block() as block:
            @block.sync
            def _(sp):
                with sp.Fori(1, 5) as c:
                    for g in range(5):
                        sp.wait_ge(turned, 25 * c + 5 * g + 5)
                        sp.dma_start(ct[:, g], K.counts_all[:, 5 * g:5 * g + 5, bass.ds(5 * c, 5)]).then_inc(landed[g], 16)

            @block.tensor
            def _(pe):
                pe.wait_ge(cleared, 1)
                pe.sem_inc(used, 5)
                pe.sem_inc(turned, 25)
                with pe.Fori(0, 5) as c:
                    for n in range(25 + LAG):
                        if n < 25:
                            g, j = n // 5, n % 5
                            if j == 0:
                                pe.wait_ge(landed[g], 16 * c + 16)
                            pe.wait_ge(moved, 25 * c + (n - 3 if n >= 3 else -1) + 26)
                            for b in range(5):
                                ins = pe.transpose(T16[:, 5 + n % 3, b * PAD:b * PAD + P], ct[:, g, b, j],
                                                   K.ident16[0:P, 0:P])
                            ins.then_inc(turned, 1)
                        if n >= LAG:
                            t = n - LAG
                            g, j = t // 5, t % 5
                            pe.wait_ge(moved, 25 * c + t + 26)
                            if t < 5:
                                pe.wait_ge(drained, 5 * c + t + 1)
                            for b in range(5):
                                for p in range(2):
                                    ins = pe.matmul(K.ps[:, j, 0:W], cT[0:P, t % 5, b], parts[:, 5 * g + b, p],
                                                    start=(g == 0 and b == 0 and p == 0),
                                                    stop=(g == 4 and b == 4 and p == 1))
                            ins.then_inc(used, 1)

            @block.scalar
            def _(act):
                def move(c, n):
                    act.wait_ge(turned, 25 * c + n + 26)
                    act.wait_ge(used, 25 * c + n + 1)
                    act.activation(cT[:, n % 5, :, 0:P], T16[:, 5 + n % 3, 0:5 * PAD]
                                   .rearrange("p (b s) -> p b s", s=PAD)[:, :, 0:P], ACT.Copy).then_inc(moved, 1)

                def exponentials(c):
                    act.wait_ge(centred, c + 1)
                    act.activation(s[:], s[:], ACT.Exp).then_inc(exped, 1)

                act.wait_ge(cleared, 1)
                act.sem_inc(moved, 25)
                for n in range(25):
                    move(0, n)
                with act.Fori(0, 4) as c:
                    for n in range(EXP_AT):
                        move(c + 1, n)
                    exponentials(c)
                    for n in range(EXP_AT, 25):
                        move(c + 1, n)
                exponentials(4)

            @block.vector
            def _(v):
                v.memset(cT[:], 0.0).then_inc(cleared, 1)
                v.sem_inc(drained, 5)
                v.sem_inc(red, 2)
                with v.Fori(0, 5) as c:
                    link = Chain(v, own, LINKS * c)
                    heads = lambda first, b: qkv[:, bass.ds(5 * c + b, 1), first:first + D] \
                        .rearrange("p a (h d) -> p (a h) d", h=H)
                    v.wait_ge(used, 25 * c + 30)
                    for b in range(5):
                        v.tensor_scalar(cnt[:, b:b + 1], K.ps[0:P, b, D:W], -1.0, 1.0, ALU.add, ALU.max)
                        v.scalar_tensor_tensor(kl[:, b], K.ps[0:P, b, 0:D], span,
                                               qkv[:, bass.ds(5 * c + b, 1), D:2 * D].rearrange("p a f -> p (a f)"),
                                               ALU.mult, ALU.subtract).then_inc(drained, 1)
                    v.wait_ge(drained, 5 * c + 10)
                    link(v.reciprocal(cnt[:], cnt[:]))
                    link(v.tensor_tensor(kl[:], kl[:], cnt[:].unsqueeze(2).to_broadcast([P, 5, D]), ALU.mult))
                    for b in range(6):
                        if b < 5:
                            v.wait_ge(red, 10 * c + b + 1)
                            v.tensor_tensor(pr[:, b % 2].rearrange("p (h g d) -> p h g d", h=H, g=H),
                                            heads(0, b).unsqueeze(2).to_broadcast([P, H, H, DH]),
                                            kl[:, b].rearrange("p (g d) -> p g d", g=H).unsqueeze(1)
                                            .to_broadcast([P, H, H, DH]), ALU.mult).then_inc(mult, 1)
                        if b > 0:
                            v.wait_ge(mult, 10 * c + b)
                            v.tensor_reduce(s[:, b - 1], pr[:, (b - 1) % 2].rearrange("p (h g d) -> p h g d", h=H, g=H),
                                            AX.X, ALU.add).then_inc(red, 1)
                    v.wait_ge(red, 10 * c + 5 + 2)
                    link(v.tensor_reduce(m[:], s[:], AX.X, ALU.max))
                    v.tensor_tensor(s[:], s[:], m[:].unsqueeze(3).to_broadcast([P, 5, H, H]),
                                    ALU.subtract).then_inc(centred, 1)
                    v.wait_ge(exped, c + 1)
                    link(v.tensor_reduce(m[:], s[:], AX.X, ALU.add))
                    link(v.reciprocal(m[:], m[:]))
                    link(v.tensor_tensor(s[:], s[:], m[:].unsqueeze(3).to_broadcast([P, 5, H, H]), ALU.mult))
                    for b in range(6):
                        if b < 5:
                            v.wait_ge(red, 10 * c + b + 6)
                            v.tensor_tensor(pr[:, b % 2].rearrange("p (h d g) -> p h d g", h=H, d=DH),
                                            s[:, b].unsqueeze(2).to_broadcast([P, H, DH, H]),
                                            heads(2 * D, b).rearrange("p g d -> p d g").unsqueeze(1)
                                            .to_broadcast([P, H, DH, H]), ALU.mult).then_inc(mult, 1)
                        if b > 0:
                            v.wait_ge(mult, 10 * c + 5 + b)
                            v.tensor_reduce(att[:, bass.ds(5 * c + b - 1, 1)].rearrange("p a (h d) -> p (a h) d", h=H),
                                            pr[:, (b - 1) % 2].rearrange("p (h d g) -> p h d g", h=H, d=DH),
                                            AX.X, ALU.add).then_inc(red, 1)
                    assert link.n == LINKS


@phase
def linear_columns(nc, K, S, tag, outs):
    done, taken_a, taken_v = S(tag + "_done"), S(tag + "_takena"), S(tag + "_takenv")
    steps = [(o, m) for o in outs for m in range(7)]
    on_act = [o[3] is not None or (o[4] is None and m % 2 == 1) for o, m in steps]
    with nc.Block() as block:
        @block.tensor
        def _(pe):
            for n, ((dst, terms, bias, func, add), m) in enumerate(steps):
                if n >= 8:
                    a = on_act[n - 8]
                    pe.wait_ge(taken_a if a else taken_v, sum(x == a for x in on_act[:n - 7]))
                w = min(500, N - 500 * m)
                for i, (wt, src) in enumerate(terms):
                    ins = pe.matmul(K.ps[:, n % 8, 0:w], wt, src[:, 500 * m:500 * m + w], start=(i == 0),
                                    stop=(i == len(terms) - 1))
                ins.then_inc(done, 1)

        @block.scalar
        def _(act):
            for n, ((dst, terms, bias, func, add), m) in enumerate(steps):
                if on_act[n]:
                    w = min(500, N - 500 * m)
                    act.wait_ge(done, n + 1)
                    act.activation(dst[:, 500 * m:500 * m + w], K.ps[:, n % 8, 0:w], func or ACT.Identity,
                                   bias=bias).then_inc(taken_a, 1)

        @block.vector
        def _(v):
            for n, ((dst, terms, bias, func, add), m) in enumerate(steps):
                if not on_act[n]:
                    w = min(500, N - 500 * m)
                    s = slice(500 * m, 500 * m + w)
                    v.wait_ge(done, n + 1)
                    if add is None:
                        v.tensor_scalar(dst[:, s], K.ps[:, n % 8, 0:w], bias, None, ALU.add).then_inc(taken_v, 1)
                    else:
                        v.scalar_tensor_tensor(dst[:, s], K.ps[:, n % 8, 0:w], bias, add[:, s], ALU.add,
                                               ALU.add).then_inc(taken_v, 1)


@phase
def linear_rows(nc, K, S, tag, terms, W, dst, bias=None):
    done, taken = S(tag + "_done"), S(tag + "_taken")
    with nc.Block() as block:
        @block.tensor
        def _(pe):
            for b in range(NB):
                if b >= 8:
                    pe.wait_ge(taken, b - 7)
                for i, (src, wt) in enumerate(terms):
                    ins = pe.matmul(K.ps[0:P, b % 8, 0:W], src[:, P * b:P * b + P], wt, start=(i == 0),
                                    stop=(i == len(terms) - 1))
                ins.then_inc(done, 1)

        @block.vector
        def _(v):
            for b in range(NB):
                v.wait_ge(done, b + 1)
                if bias is None:
                    v.tensor_copy(dst[:, b, 0:W], K.ps[0:P, b % 8, 0:W]).then_inc(taken, 1)
                else:
                    v.tensor_tensor(dst[:, b, 0:W], K.ps[0:P, b % 8, 0:W], bias, ALU.add).then_inc(taken, 1)


@phase
def load(nc, K, S, tag, pairs):
    landed = S(tag + "_landed")
    with nc.Block() as block:
        @block.sync
        def _(sp):
            for dst, src in pairs:
                sp.dma_start(dst, src).then_inc(landed, 16)
            sp.wait_ge(landed, 16 * len(pairs))


STEEP = 1.0e8
TOP = 16384.0
TINY = 1e-30
COLS = [("a", 6), ("att", 6), ("b0", 3), ("g_in", 1), ("be_in", 1), ("b1", 2), ("g1", 2), ("be1", 2), ("b2", 1),
        ("g2", 1), ("be2", 1), ("bo", 1), ("fb1", 4), ("fb2", 1), ("fg1", 1), ("fbe1", 1), ("fg2", 1), ("fbe2", 1)]
COL, NCOL = {}, 0
for _name, _n in COLS:
    COL[_name] = NCOL
    NCOL += _n
ROW_RELW = 3 * D
ROW_QKV = 3 * D + 3
NROW = ROW_QKV + 3 * D


class Names:
    pass


def build(nc, args, out):
    K, T = Names(), Names()
    K.src_in, K.dst_in, K.typ_in = (args[n] for n in ("src", "dst", "typ"))
    K.x_in, K.w_in, K.cols_in, K.rows_in = (args[n] for n in ("x_in", "w_in", "cols_in", "rows_in"))
    K.w1_in, K.w2_in, K.wq_in, K.wk_in = (args[n] for n in ("w1_in", "w2_in", "wq_in", "wk_in"))
    K.wv_in, K.wo_in, K.fw1_in, K.fw2_in = (args[n] for n in ("wv_in", "wo_in", "fw1_in", "fw2_in"))
    with ExitStack() as ctx:
        sb = lambda name, shape, dt: ctx.enter_context(nc.sbuf_tensor(name, shape, dt))
        S = lambda name: ctx.enter_context(nc.semaphore(name))
        col = lambda name, i=0: K.cols[:, COL[name] + i:COL[name] + i + 1]
        K.ps = ctx.enter_context(nc.psum_tensor("ps", [128, 8, 512], F32))
        K.counts = nc.dram_tensor("counts", [R, P, NB, NB, PAD], F16)
        K.counts_all = nc.dram_tensor("counts_all", [P, NB, NB, PAD], F16)
        K.sub_range = nc.dram_tensor("sub_range", [2, NSUB], F16)
        K.edge_keys = nc.dram_tensor("edge_keys", [2 * E], F32)
        K.windows = nc.dram_tensor("windows", [NSUB, 2 * CH], F32)
        K.ad_rows = nc.dram_tensor("ad_rows", [4, NB, PAD], F32)
        K.x = sb("x", [P, NB, D], F32)
        K.zT = sb("zT", [D, N], F32)
        K.wext = sb("wext", [D, 6, D + 8], F32)
        K.cols = sb("cols", [D, NCOL], F32)
        K.rows = sb("rows", [128, NROW], F32)
        K.relw = sb("relw", [128, 6], F32)
        K.ident = sb("ident", [128, 128], F32)
        K.ident16 = sb("ident16", [128, 128], F16)
        K.zeros = sb("zeros", [P, 512], BF16)
        K.dinv = sb("dinv", [P, NB], F32)
        K.dinv2 = sb("dinv2", [P, NB], F32)
        with nc.cleanup_on_exit():
            load_constants(nc, K)
            load(nc, K, "rows", [(K.rows[:], K.rows_in.partition_broadcast(128))])
            score_weights(nc, K)
            relation_weights(nc, K)
            with ExitStack() as c2:
                sb2 = lambda name, shape, dt: c2.enter_context(nc.sbuf_tensor(name, shape, dt))
                K.keys = sb2("keys", [P, NCH, 2], F32)
                K.group_base = sb2("group_base", [P, NG], F32)
                K.iota_col = sb2("iota_col", [P, GE], F16)
                K.iota_pair = sb2("iota_pair", [P, PAD, WIN], F16)
                K.window_lo = sb2("window_lo", [P, NG, WIN], F16)
                K.window_col = sb2("window_col", [P, NG, WIN], F32)
                K.wide = sb2("wide", [1, 1], I32)
                prepare_edges(nc, K)
                count_edges(nc, K)

        def gat(tag, k, H, F, counts, finish, degree=False):
            with ExitStack() as c3:
                sb3 = lambda name, shape, dt: c3.enter_context(nc.sbuf_tensor(tag + name, shape, dt))
                T.mv = sb3("mv", [P, NB, (4 if H == 1 else 6) * H * F], F16)
                T.top = sb3("top", [P, 1], F32)
                T.thr = sb3("thr", [P, 2, NB, H], F32)
                T.c = sb3("c", [P, NB, H, 2], F32)
                T.ct = sb3("ct", [P, 5, 5, 5, PAD], F16)
                T.ad = sb3("ad", [P, 2, H, 5 * PAD], F32)
                T.landed = [nc.alloc_semaphore(f"{tag}_landed{c}") for c in range(5)]
                T.ad_landed = nc.alloc_semaphore(tag + "_ad_landed")
                scores(nc, K, tag + "s", k, counts, H, F, T)
                T.num = sb3("num", [P, NB, H, F], F32)
                if H == 1:
                    attention_one(nc, K, tag + "a", counts, F, T, degree)
                else:
                    attention_heads(nc, K, tag + "a", counts, H, F, T)
                finish()

        turn_to_columns(nc, K, "t0", K.x, K.zT)
        for l in range(3):
            tag = f"g{l}"

            def finish():
                gat_normalise(nc, K, tag + "n", T.num, T.top, K.z, l == 0)
            with nc.cleanup_on_exit(), nc.sbuf_tensor(tag + "z", [P, NB, D], F32) as K.z:
                gat(tag, l, 1, D + 2, K.counts_all, finish, degree=(l == 0))
                batch_norm(nc, K, tag + "b", K.zT, K.zT, relu=True, rows=K.z, bias=col("b0", l))
        with nc.cleanup_on_exit():
            turn_to_rows(nc, K, "r0", K.zT, K.x, residual=K.x)
            layer_norm(nc, K, "ln0", K.x)

        def counts_by_destination(tag, ct):
            landed = [nc.alloc_semaphore(f"{tag}_landed{c}") for c in range(5)]
            return landed, [(ct[:, c], K.counts_all[:, 0:5, 5 * c:5 * c + 5], landed[c]) for c in range(5)]

        with nc.cleanup_on_exit(), ExitStack() as c2:
            sb2 = lambda name, shape, dt: c2.enter_context(nc.sbuf_tensor(name, shape, dt))
            z = sb2("z1", [P, NB, D], F32)
            parts = sb2("parts1", [P, NB, 2, D], F16)
            span = sb2("span1", [P, 1], F32)
            ct = sb2("ct1", [P, 5, 5, 5, PAD], F16)
            wide = sb2("wide1", [D, 2, N], F32)
            w1 = sb2("w1", [D, 2, D], F32)
            w2 = sb2("w2", [D, 2, D], F32)
            load(nc, K, "w1", [(w1[:], K.w1_in.rearrange("f (j o) -> f j o", j=2)),
                                  (w2[:], K.w2_in.rearrange("(j f) o -> f j o", j=2))])
            batch_norm(nc, K, "b1", K.zT, K.zT, col("g_in"), col("be_in"), rows=K.x)
            turn_to_rows(nc, K, "r1", K.zT, z)
            landed, first = counts_by_destination("c1", ct)
            split_parts(nc, K, "p1", z[:], parts, span[:], first, scale=K.dinv)
            gather_in(nc, K, "c1", ct, landed, parts, span[:], z)
            turn_to_columns(nc, K, "t2", z, K.zT)
            linear_columns(nc, K, "l1", [(wide[:, j], [(w1[:, j], K.zT)], col("b1", j), None, None) for j in range(2)])
            for j in range(2):
                batch_norm(nc, K, f"b2{j}", wide[:, j], wide[:, j], col("g1", j), col("be1", j), relu=True)
            linear_rows(nc, K, "l2", [(wide[:, j], w2[:, j]) for j in range(2)], D, z)
            landed, first = counts_by_destination("c2", ct)
            split_parts(nc, K, "p2", z[:], parts, span[:], first, scale=K.dinv)
            gather_in(nc, K, "c2", ct, landed, parts, span[:], z)
            batch_norm(nc, K, "b3", K.zT, K.zT, col("g2"), col("be2"), relu=True, rows=z, bias=col("b2"))
            turn_to_rows(nc, K, "r2", K.zT, K.x, residual=K.x)
            layer_norm(nc, K, "ln1", K.x)

        turn_to_columns(nc, K, "t4", K.x, K.zT)
        for r in range(R):
            tag = f"r{r}"
            with nc.cleanup_on_exit():
                gat(tag, 3 + r, 4, 33, K.counts[r], lambda: relation_sum(nc, K, tag + "n", T.num, T.top, r))
        layer_norm(nc, K, "ln2", K.x)

        turn_to_columns(nc, K, "t5", K.x, K.zT)
        with ExitStack() as c2:
            sb2 = lambda name, shape, dt: c2.enter_context(nc.sbuf_tensor(name, shape, dt))
            att = sb2("att3", [P, NB, D], F32)
            with ExitStack() as c3:
                sb3 = lambda name, shape, dt: c3.enter_context(nc.sbuf_tensor(name, shape, dt))
                wqkv = sb3("wqkv", [D, 3 * D], F32)
                qkv = sb3("qkv", [P, NB, 3 * D], F32)
                ks = sb3("ks", [P, NB, D], F32)
                load(nc, K, "wqkv", [(wqkv[:, i * D:(i + 1) * D], w) for i, w in enumerate((K.wq_in, K.wk_in, K.wv_in))])
                linear_rows(nc, K, "l3", [(K.zT, wqkv[:])], 3 * D, qkv, K.rows[0:P, ROW_QKV:NROW])
                with nc.sbuf_tensor("parts3", [P, NB, 2, D + 1], F16) as parts, \
                        nc.sbuf_tensor("span3", [P, 1], F32) as span:
                    with nc.sbuf_tensor("ct3", [P, 5, 5, 5, PAD], F16) as ct:
                        landed = [nc.alloc_semaphore(f"c3_landed{g}") for g in range(5)]
                        first = [(ct[:, g], K.counts_all[:, 5 * g:5 * g + 5, 0:5], landed[g]) for g in range(5)]
                        key_values(nc, K, qkv, ks, parts)
                        split_parts(nc, K, "p3", ks[:], parts, span[:], first)
                        attend_to_keys(nc, K, "c3", ct, landed, parts, span[:], qkv, att)
            with ExitStack() as c3:
                sb3 = lambda name, shape, dt: c3.enter_context(nc.sbuf_tensor(name, shape, dt))
                wo = sb3("wo", [D, D], F32)
                fw1 = sb3("fw1", [D, 4, D], F32)
                fw2 = sb3("fw2", [D, 4, D], F32)
                aT = sb3("aT", [D, N], F32)
                hid = sb3("hid", [D, 4, N], F32)
                load(nc, K, "ffw", [(wo[:], K.wo_in), (fw1[:], K.fw1_in.rearrange("f (j o) -> f j o", j=4)),
                                       (fw2[:], K.fw2_in.rearrange("(j f) o -> f j o", j=4))])
                turn_to_columns(nc, K, "t6", att, aT)
                linear_columns(nc, K, "l4", [(K.zT, [(wo[:], aT)], col("bo"), None, K.zT)])
                batch_norm(nc, K, "b4", K.zT, K.zT, col("fg1"), col("fbe1"))
                linear_columns(nc, K, "l5", [(hid[:, j], [(fw1[:, j], K.zT)], col("fb1", j), ACT.Gelu, None)
                                                for j in range(4)])
                linear_columns(nc, K, "l6", [(K.zT, [(fw2[:, j], hid[:, j]) for j in range(4)], col("fb2"), None, K.zT)])
                batch_norm(nc, K, "b5", K.zT, K.zT, col("fg2"), col("fbe2"))
                turn_to_rows(nc, K, "r3", K.zT, K.x, residual=K.x)
                layer_norm(nc, K, "ln3", K.x)
        stored = S("out_stored")
        with nc.Block() as block:
            @block.sync
            def _(sp):
                sp.dma_start(out.rearrange("(b p) f -> p b f", p=P), K.x[:]).then_inc(stored, 16)
                sp.wait_ge(stored, 16)


@phase
def key_values(nc, K, S, qkv, ks, parts):
    with nc.Block() as block:
        @block.vector
        def _(v):
            v.tensor_copy(ks[:, :, 0:D], qkv[:, :, D:2 * D])

        @block.gpsimd
        def _(pool):
            pool.memset(parts[:, :, 0, D:D + 1], 1.0)
            pool.memset(parts[:, :, 1, D:D + 1], 0.0)


def kernel(**inputs):
    import numpy as _np
    import concourse.bacc as _bacc
    from concourse import mybir as _mybir
    from concourse.bass_utils import run_bass_kernel_spmd as _run

    nc = _bacc.Bacc("TRN2", target_bir_lowering=False, num_devices=1)
    arrays, args = {}, {}

    def give(name, a):
        a = _np.ascontiguousarray(a)
        arrays["in_" + name] = a
        args[name] = nc.dram_tensor("in_" + name, a.shape, _mybir.dt.from_np(a.dtype), kind="ExternalInput").ap()

    i = {k: _np.asarray(v) for k, v in inputs.items()}
    for name, key in (("src", "src"), ("dst", "dst"), ("typ", "edge_type_3")):
        give(name, i[key])
    give("x_in", i["x"])
    give("w_in", _np.concatenate([i["L0_gnn_W"], i["L2_gnn_W"]]))
    cols = [i[k].reshape(-1, D) for k in (
        "L1_gnn_g_in", "L1_gnn_be_in", "L1_gnn_b1", "L1_gnn_g1", "L1_gnn_be1", "L1_gnn_b2", "L1_gnn_g2", "L1_gnn_be2",
        "L3_gnn_bo", "L3_gnn_b1", "L3_gnn_b2", "L3_gnn_g1", "L3_gnn_be1", "L3_gnn_g2", "L3_gnn_be2")]
    a0 = _np.stack([i["L0_gnn_a_src"], i["L0_gnn_a_dst"]], axis=1).reshape(6, D)
    a2 = _np.stack([i["L2_gnn_att_src"].reshape(R, D), i["L2_gnn_att_dst"].reshape(R, D)], axis=1).reshape(6, D)
    give("cols_in", _np.concatenate([a0, a2, i["L0_gnn_b"]] + cols).T)
    give("rows_in", _np.concatenate([i["L2_gnn_bias"].reshape(-1), i["L2_gnn_rel_w"], i["L3_gnn_bq"], i["L3_gnn_bk"],
                                     i["L3_gnn_bv"]]))
    for name, key in (("w1_in", "L1_gnn_w1"), ("w2_in", "L1_gnn_w2"), ("wq_in", "L3_gnn_wq"), ("wk_in", "L3_gnn_wk"),
                      ("wv_in", "L3_gnn_wv"), ("wo_in", "L3_gnn_wo"), ("fw1_in", "L3_gnn_w1"), ("fw2_in", "L3_gnn_w2")):
        give(name, i[key])
    out = nc.dram_tensor("out_x", (N, D), _mybir.dt.float32, kind="ExternalOutput").ap()
    build(nc, args, out)
    r = _run(nc, [arrays], core_ids=[0])
    return r.results[0]["out_x"]
```
